# Optimizing a Trainium2 kernel written in Bass

```python
import numpy as np
import jax
import jax.numpy as jnp

def _softmax(x, axis=-1):
    return jax.nn.softmax(x, axis=axis)

def _gelu(x):
    return jax.nn.gelu(x, approximate=True)

def _silu(x):
    return jax.nn.silu(x)

def _sigmoid(x):
    return jax.nn.sigmoid(x)

def _layernorm(x, axis=-1, eps=1e-05):
    m = jnp.mean(x, axis=axis, keepdims=True)
    v = jnp.var(x, axis=axis, keepdims=True)
    return (x - m) / jnp.sqrt(v + eps)

def _scatter_add(tgt, idx, src, axis=0):
    return tgt.at[idx].add(src)

def _segment_sum(src, seg, n):
    return jax.ops.segment_sum(src, seg, n)
kernel_name = 'mk_gps_d1_gnn_r8_cfb6c8'

def setup_inputs(seed: int=0):
    np.random.seed(seed)
    _w = jnp.asarray

    def _rec_inputs():
        import jax
        import jax.numpy as jnp
        _gk = jax.random.key(seed)
        x = -0.0003713 + 1 * jax.random.normal(jax.random.fold_in(_gk, 1), (6250, 256), jnp.float32)
        _s = jax.random.randint(jax.random.fold_in(_gk, 2), (100000,), 0, 6250, jnp.int32)
        _d = jax.random.randint(jax.random.fold_in(_gk, 3), (100000,), 0, 6250, jnp.int32)
        _loop = jnp.arange(6250, dtype=jnp.int32)
        src = jnp.concatenate([_s, _d, _loop])
        dst = jnp.concatenate([_d, _s, _loop])
        _o = jnp.argsort(dst, stable=True)
        src = src[_o]
        dst = dst[_o]
        return (x, src, dst)
    x, src, dst = _rec_inputs()

    def _L0_gnn_setup():
        import jax, jax.numpy as jnp
        import numpy as np
        N = 6250
        E = 100000
        H = 8
        C = 32
        HS = H * C
        NEG_SLOPE = 0.2
        EPS = 1e-16
        key = jax.random.key(seed)
        ks = jax.random.split(key, 6)
        x = jax.random.normal(ks[0], (N, HS), dtype=jnp.float32)
        edge_index = jax.random.randint(ks[1], (2, E), 0, N, dtype=jnp.int64)
        W = jax.random.normal(ks[2], (HS, HS), dtype=jnp.float32) * (1.0 / np.sqrt(HS))
        att_src = jax.random.normal(ks[3], (H, C), dtype=jnp.float32) * (1.0 / np.sqrt(C))
        att_dst = jax.random.normal(ks[4], (H, C), dtype=jnp.float32) * (1.0 / np.sqrt(C))
        bias = jax.random.normal(ks[5], (HS,), dtype=jnp.float32) * 0.02
        return {'x': x, 'edge_index': edge_index, 'W': W, 'att_src': att_src, 'att_dst': att_dst, 'bias': bias}
    _L0_gnn_all = _L0_gnn_setup()
    _L0_gnn_in = {k: v for k, v in _L0_gnn_all.items() if k in ('W', 'att_src', 'att_dst', 'bias')}
    del _L0_gnn_all

    def _L0_mix_setup():
        import jax, jax.numpy as jnp
        import numpy as np
        N, F, C, H = (32, 512, 256, 8)
        D = C // H
        EPS_ATTN = 1e-06
        EPS_LN = 1e-05

        def layer_norm(x, g, b):
            mu = jnp.mean(x, axis=-1, keepdims=True)
            var = jnp.var(x, axis=-1, keepdims=True)
            return (x - mu) * jax.lax.rsqrt(var + EPS_LN) * g + b
        key = jax.random.key(seed)
        ks = jax.random.split(key, 8)
        s = 1.0 / np.sqrt(C)
        return {'x': jax.random.normal(ks[0], (N, F, C), jnp.float32), 'Wqkv': jax.random.uniform(ks[1], (3 * C, C), jnp.float32, -s, s), 'ln1_g': jnp.ones((C,), jnp.float32), 'ln1_b': jnp.zeros((C,), jnp.float32), 'W1': jax.random.uniform(ks[2], (C, C), jnp.float32, -s, s), 'b1': jax.random.uniform(ks[3], (C,), jnp.float32, -s, s), 'W2': jax.random.uniform(ks[4], (C, C), jnp.float32, -s, s), 'b2': jax.random.uniform(ks[5], (C,), jnp.float32, -s, s), 'ln2_g': jnp.ones((C,), jnp.float32), 'ln2_b': jnp.zeros((C,), jnp.float32)}
    _L0_mix_all = _L0_mix_setup()
    _L0_mix_in = {k: v for k, v in _L0_mix_all.items() if k in ('Wqkv', 'ln1_g', 'ln1_b', 'W1', 'b1', 'W2', 'b2', 'ln2_g', 'ln2_b')}
    del _L0_mix_all

    def _L0_ffn_setup():
        import jax, jax.numpy as jnp
        import numpy as np
        B, S, H, F, E, K = (8, 512, 256, 512, 16, 2)
        EPS = 1e-05
        key = jax.random.key(seed)
        ks = jax.random.split(key, 9)
        sc = 0.02
        return {'x': jax.random.normal(ks[0], (B, S, H), dtype=jnp.float32), 'gate_w': jax.random.normal(ks[1], (H, E), dtype=jnp.float32) * sc, 'gate_b': jnp.zeros((E,), dtype=jnp.float32), 'w1': jax.random.normal(ks[2], (E, H, F), dtype=jnp.float32) * sc, 'b1': jnp.zeros((E, F), dtype=jnp.float32), 'w2': jax.random.normal(ks[3], (E, F, H), dtype=jnp.float32) * sc, 'b2': jnp.zeros((E, H), dtype=jnp.float32), 'gamma': jnp.ones((H,), dtype=jnp.float32), 'beta': jnp.zeros((H,), dtype=jnp.float32)}
    _L0_ffn_all = _L0_ffn_setup()
    _L0_ffn_in = {k: v for k, v in _L0_ffn_all.items() if k in ('gate_w', 'gate_b', 'w1', 'b1', 'w2', 'b2', 'gamma', 'beta')}
    del _L0_ffn_all
    return {'x': x, 'src': src, 'dst': dst, 'L0_gnn_W': _L0_gnn_in['W'], 'L0_gnn_att_src': _L0_gnn_in['att_src'], 'L0_gnn_att_dst': _L0_gnn_in['att_dst'], 'L0_gnn_bias': _L0_gnn_in['bias'], 'L0_mix_Wqkv': _L0_mix_in['Wqkv'], 'L0_mix_ln1_g': _L0_mix_in['ln1_g'], 'L0_mix_ln1_b': _L0_mix_in['ln1_b'], 'L0_mix_W1': _L0_mix_in['W1'], 'L0_mix_b1': _L0_mix_in['b1'], 'L0_mix_W2': _L0_mix_in['W2'], 'L0_mix_b2': _L0_mix_in['b2'], 'L0_mix_ln2_g': _L0_mix_in['ln2_g'], 'L0_mix_ln2_b': _L0_mix_in['ln2_b'], 'L0_ffn_gate_w': _L0_ffn_in['gate_w'], 'L0_ffn_gate_b': _L0_ffn_in['gate_b'], 'L0_ffn_w1': _L0_ffn_in['w1'], 'L0_ffn_b1': _L0_ffn_in['b1'], 'L0_ffn_w2': _L0_ffn_in['w2'], 'L0_ffn_b2': _L0_ffn_in['b2'], 'L0_ffn_gamma': _L0_ffn_in['gamma'], 'L0_ffn_beta': _L0_ffn_in['beta']}

def reference(x, src, dst, L0_gnn_W, L0_gnn_att_src, L0_gnn_att_dst, L0_gnn_bias, L0_mix_Wqkv, L0_mix_ln1_g, L0_mix_ln1_b, L0_mix_W1, L0_mix_b1, L0_mix_W2, L0_mix_b2, L0_mix_ln2_g, L0_mix_ln2_b, L0_ffn_gate_w, L0_ffn_gate_b, L0_ffn_w1, L0_ffn_b1, L0_ffn_w2, L0_ffn_b2, L0_ffn_gamma, L0_ffn_beta):
    import jax
    import jax.numpy as jnp

    def _L0_gnn_ref(x, edge_index, W, att_src, att_dst, bias):
        import jax, jax.numpy as jnp
        import numpy as np
        N = 6250
        E = 100000
        H = 8
        C = 32
        HS = H * C
        NEG_SLOPE = 0.2
        EPS = 1e-16
        src, dst = (edge_index[0], edge_index[1])
        xw = (x @ W).reshape(N, H, C)
        a_src = jnp.einsum('nhc,hc->nh', xw, att_src)
        a_dst = jnp.einsum('nhc,hc->nh', xw, att_dst)
        e = a_src[src] + a_dst[dst]
        e = jax.nn.leaky_relu(e, NEG_SLOPE)
        m = jax.ops.segment_max(e, dst, num_segments=N)
        m = jnp.where(jnp.isfinite(m), m, 0.0)
        ex = jnp.exp(e - m[dst])
        denom = jax.ops.segment_sum(ex, dst, num_segments=N)
        alpha = ex / (denom[dst] + EPS)
        msg = xw[src] * alpha[:, :, None]
        out = jax.ops.segment_sum(msg, dst, num_segments=N)
        out = out.reshape(N, HS) + bias
        return jax.nn.relu(out)

    def _L0_mix_ref(x, Wqkv, ln1_g, ln1_b, W1, b1, W2, b2, ln2_g, ln2_b):
        import jax, jax.numpy as jnp
        import numpy as np
        N, F, C, H = (32, 512, 256, 8)
        D = C // H
        EPS_ATTN = 1e-06
        EPS_LN = 1e-05

        def layer_norm(x, g, b):
            mu = jnp.mean(x, axis=-1, keepdims=True)
            var = jnp.var(x, axis=-1, keepdims=True)
            return (x - mu) * jax.lax.rsqrt(var + EPS_LN) * g + b
        n, f, c = x.shape
        qkv = jnp.einsum('nfc,oc->nfo', x, Wqkv)
        q, k, v = jnp.split(qkv, 3, axis=-1)
        q = q.reshape(n, f, H, D)
        k = k.reshape(n, f, H, D)
        v = v.reshape(n, f, H, D)
        q = jax.nn.elu(q) + 1.0
        k = jax.nn.elu(k) + 1.0
        kv = jnp.einsum('nshd,nshm->nhmd', k, v)
        ksum = jnp.sum(k, axis=1)
        z = 1.0 / (jnp.einsum('nlhd,nhd->nlh', q, ksum) + EPS_ATTN)
        t = jnp.einsum('nlhd,nhmd,nlh->nlhm', q, kv, z)
        t = t.reshape(n, f, c)
        x1 = layer_norm(t + x, ln1_g, ln1_b)
        h = jax.nn.gelu(jnp.einsum('nfc,oc->nfo', x1, W1) + b1, approximate=False)
        y = jnp.einsum('nfc,oc->nfo', h, W2) + b2
        return layer_norm(y + x1, ln2_g, ln2_b)

    def _L0_ffn_ref(x, gate_w, gate_b, w1, b1, w2, b2, gamma, beta):
        import jax, jax.numpy as jnp
        import numpy as np
        B, S, H, F, E, K = (8, 512, 256, 512, 16, 2)
        EPS = 1e-05
        gate_logits = x @ gate_w + gate_b
        topk_vals, topk_idx = jax.lax.top_k(gate_logits, K)
        topk_w = jax.nn.softmax(topk_vals, axis=-1)
        h = jax.nn.relu(jnp.einsum('bsh,ehf->bsef', x, w1) + b1)
        expert_out = jnp.einsum('bsef,efh->bseh', h, w2) + b2
        sel = jnp.take_along_axis(expert_out, topk_idx[:, :, :, None], axis=2)
        moe = jnp.sum(topk_w[..., None] * sel, axis=2)
        y = x + moe
        mu = jnp.mean(y, axis=-1, keepdims=True)
        var = jnp.var(y, axis=-1, keepdims=True)
        return (y - mu) / jnp.sqrt(var + EPS) * gamma + beta
    edge_index = jnp.stack([src, dst])
    xn = _layernorm(x, axis=-1)
    x = x + _L0_gnn_ref(xn, edge_index, L0_gnn_W, L0_gnn_att_src, L0_gnn_att_dst, L0_gnn_bias) + _L0_mix_ref(xn[None], L0_mix_Wqkv, L0_mix_ln1_g, L0_mix_ln1_b, L0_mix_W1, L0_mix_b1, L0_mix_W2, L0_mix_b2, L0_mix_ln2_g, L0_mix_ln2_b)[0]
    x = x + _L0_ffn_ref(_layernorm(x, axis=-1)[None], L0_ffn_gate_w, L0_ffn_gate_b, L0_ffn_w1, L0_ffn_b1, L0_ffn_w2, L0_ffn_b2, L0_ffn_gamma, L0_ffn_beta)[0]
    return x

_drawn_inputs = setup_inputs


def setup_inputs(seed=0):
    import zlib

    import numpy as np

    out = dict(_drawn_inputs(seed))
    spreads = {'L0_mix_ln1_g': (1.0, 0.2),
     'L0_mix_ln1_b': (0.0, 0.1),
     'L0_mix_ln2_g': (1.0, 0.2),
     'L0_mix_ln2_b': (0.0, 0.1),
     'L0_ffn_gate_b': (0.0, 0.344),
     'L0_ffn_b1': (0.0, 0.8),
     'L0_ffn_b2': (0.0, 0.327),
     'L0_ffn_gamma': (1.0, 0.2),
     'L0_ffn_beta': (0.0, 0.1)}
    factors = {'L0_gnn_att_dst': 2.888,
     'L0_gnn_bias': 7.119,
     'L0_mix_Wqkv': 8.0,
     'L0_mix_b1': 8.0,
     'L0_mix_b2': 3.082,
     'L0_ffn_w1': 2.755}
    for name, (base, spread) in spreads.items():
        noise = np.random.default_rng([zlib.crc32(name.encode()), seed]).standard_normal(out[name].shape)
        drawn = base * np.exp(spread * noise) if base else spread * noise
        out[name] = jnp.asarray(drawn.astype(out[name].dtype))
    for name, factor in factors.items():
        out[name] = (out[name] * factor).astype(out[name].dtype)
    return out
```

```python
from contextlib import ExitStack

import concourse.bass as bass
from concourse import mybir

F32 = mybir.dt.float32
I32 = mybir.dt.int32
U32 = mybir.dt.uint32
ALU = mybir.AluOpType
ACT = mybir.ActivationFunctionType
AX = mybir.AxisListType

P = 128
N = 6250
D = 256
H = 8
C = D // H
CW = C + 1
ROW = H * CW
NT = -(-N // P)
NPAD = NT * P
E = 206250
J = 4
SE = J * P
STEPS = (E + NT * (SE - 1)) // SE
EPAD = E + SE
EC = -(-E // P)
PAD_DST = 1000000
X = 16
F = 512
XT = (2 * NPAD + X * (P - 1)) // P
NEG = -1.0e30
LN_EPS = 1e-5
RING = 8
CHUNK = 41
STEPS_PAD = -(-STEPS // CHUNK) * CHUNK


def walk(eng, count, lag, unroll, body, head=1):
    full = count // unroll - head
    for t in range(head * unroll):
        body(t, t % unroll, lambda l, t=t: 0 <= t - l < count)
    if full > 0:
        with eng.Fori(head, head + full) as u:
            for s in range(unroll):
                body(u * unroll + s, s, lambda l: True)
    for t in range((head + full) * unroll, count + lag):
        body(t, t % unroll, lambda l, t=t: 0 <= t - l < count)


def await_count(eng, sem, value, tick=None):
    if isinstance(value, int):
        if value > 0:
            eng.wait_ge(sem, value)
        return
    eng.wait_ge(sem, value)
    if tick is not None:
        eng.sem_inc(tick, 1)


def gps_kernel(nc, x, edges, gW, att_src, att_dst, gbias, wqkvT, ln1g, ln1b, w1T, b1, w2T, b2, ln2g, ln2b,
               gate_w, gate_b, ew1, eb1, ew2, eb2, gamma, beta, out):
    dram = lambda name, shape, dt=F32: nc.dram_tensor(name, shape, dt, kind="Internal").ap()
    table = dram("gather_table", (NPAD, ROW))
    xn_d = dram("xn_rows", (NPAD, D))
    x2_d = dram("x2_rows", (NPAD, D))
    slots_d = dram("slot_rows", (XT * P, D))
    eout_d = dram("expert_rows", (XT * P, D))

    with ExitStack() as whole:
        sb = lambda name, shape, dt=F32, ctx=whole: ctx.enter_context(nc.sbuf_tensor(name, shape, dt))
        sp_tick = whole.enter_context(nc.semaphore("sp_ticks"))
        dve_tick = whole.enter_context(nc.semaphore("dve_ticks"))
        ident = sb("ident", [P, P])
        mhalf = sb("mhalf", [P, 1])
        iota_n = sb("iota_n", [P, P])
        ones = sb("ones", [P, P])
        lower = sb("lower", [P, P])
        valid = sb("valid", [P, NT])
        adst = sb("adst", [P, NT, H])
        acc = sb("acc", [P, NT, ROW])
        kvb = sb("kvb", [P, 2, P + 4])
        top_v = sb("top_v", [P, NT, 2])
        top_i = sb("top_i", [P, NT, 2])
        slot = sb("slot", [P, NT, 2], I32)
        wtop = sb("wtop", [P, NT, 2])
        texp = sb("texp", [1, XT], I32)
        tile_f = sb("tile_f", [P, STEPS_PAD])
        reset = sb("reset", [P, STEPS_PAD])
        tile_i = sb("tile_i", [1, STEPS_PAD], I32)
        start_i = sb("start_i", [1, STEPS_PAD], I32)

        with ExitStack() as ctx:
            s = lambda name, shape, dt=F32: sb("t_" + name, shape, dt, ctx)
            dst_i = s("dst_i", [P, EC], I32)
            dst_f = s("dst_f", [P, EC])
            less = s("less", [P, EC])
            part = s("part", [P, NT + 1])
            below = s("below", [P, NT + 1])
            cnt = s("cnt", [P, NT])
            cnt_i = s("cnt_i", [P, NT], I32)
            cumt = s("cumt", [P, NT])
            fst = s("fst", [P, NT])
            dfst = s("dfst", [P, NT])
            stepno_i = s("stepno_i", [P, STEPS_PAD], I32)
            stepno = s("stepno", [P, STEPS_PAD])
            mask = s("mask", [P, CHUNK, NT])
            nodetile = s("nodetile", [P, STEPS_PAD])
            offs = s("offs", [P, STEPS_PAD])
            offs2 = s("offs2", [P, STEPS_PAD])
            iota_i = s("iota_i", [P, P], I32)
            ps = ctx.enter_context(nc.psum_tensor("t_ps", [P, 512], F32))
            loaded = ctx.enter_context(nc.semaphore("dst_loaded"))
            made = ctx.enter_context(nc.semaphore("constants_made"))
            summed = ctx.enter_context(nc.semaphore("counts_summed"))
            chain = ctx.enter_context(nc.semaphore("table_ops"))
            block = ctx.enter_context(nc.Block())

            @block.sync
            def _(sp):
                sp.dma_start(dst_i[:, :], edges[1, 0:P * EC].rearrange("(p n) -> p n", p=P)).then_inc(loaded, 16)

            @block.gpsimd
            def _(pool):
                pool.memset(ident[:, :], 0.0).then_inc(made, 1)
                pool.memset(lower[:, :], 1.0).then_inc(made, 1)
                pool.memset(valid[:, :], 1.0).then_inc(made, 1)
                pool.memset(ones[:, :], 1.0).then_inc(made, 1)
                pool.memset(mhalf[:, :], -0.5).then_inc(made, 1)
                pool.iota(iota_i[:, :], [[1, P]], base=0, channel_multiplier=0).then_inc(made, 1)
                pool.iota(stepno_i[:, :], [[1, STEPS_PAD]], base=0, channel_multiplier=0).then_inc(made, 1)
                pool.wait_ge(made, 7)
                pool.affine_select(out=ident[:, :], in_=ident[:, :], compare_op=ALU.not_equal, fill=1.0,
                                   base=0, pattern=[[-1, P]], channel_multiplier=1).then_inc(made, 1)
                pool.affine_select(out=lower[:, :], in_=lower[:, :], compare_op=ALU.is_gt, fill=0.0,
                                   base=0, pattern=[[1, P]], channel_multiplier=-1).then_inc(made, 1)
                pool.affine_select(out=valid[:, :], in_=valid[:, :], compare_op=ALU.is_gt, fill=0.0,
                                   base=N, pattern=[[-P, NT]], channel_multiplier=-1).then_inc(made, 1)

            @block.vector
            def _(dve):
                done = [0]

                def link(ins):
                    done[0] += 1
                    ins.then_inc(chain, 1)
                    dve.wait_ge(chain, done[0])

                link(dve.memset(acc[:, :, :], 0.0))
                link(dve.memset(part[:, :], 0.0))
                dve.wait_ge(made, 10)
                link(dve.tensor_copy(iota_n[:, :], iota_i[:, :]))
                link(dve.tensor_copy(stepno[:, :], stepno_i[:, :]))
                dve.wait_ge(loaded, 16)
                link(dve.tensor_copy(dst_f[:, :], dst_i[:, :]))
                for i in range(1, NT + 1):
                    link(dve.tensor_scalar(less[:, :], dst_f[:, :], float(min(P * i, N)) - 0.5, None, ALU.is_lt,
                                           ALU.add, accum_out=part[:, i:i + 1]))
                dve.wait_ge(summed, 1)
                link(dve.tensor_copy(below[:, :], ps[:, 0:NT + 1]))
                link(dve.tensor_tensor(cnt[:, :], below[:, 1:NT + 1], below[:, 0:NT], ALU.subtract))
                link(dve.tensor_scalar(cnt_i[:, :], cnt[:, :], float(SE - 1), None, ALU.add))
                link(dve.tensor_scalar(cnt_i[:, :], cnt_i[:, :], SE.bit_length() - 1, None,
                                       ALU.logical_shift_right))
                link(dve.tensor_copy(cnt[:, :], cnt_i[:, :]))
                link(dve.tensor_tensor_scan(cumt[:, :], cnt[:, :], ones[:, 0:NT], 0.0, ALU.add, ALU.mult))
                link(dve.tensor_tensor(fst[:, :], cumt[:, :], cnt[:, :], ALU.subtract))
                link(dve.scalar_tensor_tensor(fst[:, :], fst[:, :], -float(SE), below[:, 0:NT], ALU.mult, ALU.add))
                link(dve.tensor_tensor(dfst[:, 0:NT - 1], fst[:, 1:NT], fst[:, 0:NT - 1], ALU.subtract))
                for q in range(STEPS_PAD // CHUNK):
                    at = slice(q * CHUNK, (q + 1) * CHUNK)
                    m = mask[:, :, 0:NT - 1]
                    link(dve.tensor_tensor(m, stepno[:, at].unsqueeze(2).to_broadcast([P, CHUNK, NT - 1]),
                                           cumt[:, 0:NT - 1].unsqueeze(1).to_broadcast([P, CHUNK, NT - 1]),
                                           ALU.is_ge))
                    link(dve.tensor_reduce(nodetile[:, at], m, AX.X, ALU.add))
                    link(dve.tensor_tensor(m, m, dfst[:, 0:NT - 1].unsqueeze(1).to_broadcast([P, CHUNK, NT - 1]),
                                           ALU.mult))
                    link(dve.tensor_reduce(offs[:, at], m, AX.X, ALU.add))
                link(dve.tensor_scalar(tile_f[:, :], nodetile[:, :], float(P), None, ALU.mult))
                link(dve.tensor_copy(tile_i[:, :], nodetile[0:1, :]))
                link(dve.memset(reset[:, :], NEG))
                link(dve.tensor_tensor(offs2[:, 1:STEPS_PAD], nodetile[:, 1:STEPS_PAD], nodetile[:, 0:STEPS_PAD - 1],
                                       ALU.not_equal))
                link(dve.tensor_scalar(reset[:, 1:STEPS_PAD], offs2[:, 1:STEPS_PAD], NEG, None, ALU.mult))
                link(dve.tensor_scalar(offs[:, :], offs[:, :], fst[:, 0:1], None, ALU.add))
                link(dve.scalar_tensor_tensor(offs[:, :], stepno[:, :], float(SE), offs[:, :], ALU.mult, ALU.add))
                link(dve.tensor_scalar(start_i[:, :], offs[0:1, :], float(E), None, ALU.min))

            @block.tensor
            def _(pe):
                pe.wait_ge(made, 10)
                pe.wait_ge(chain, 5 + NT)
                pe.matmul(ps[:, 0:NT + 1], ones[:, :], part[:, :], start=True, stop=True).then_inc(summed, 1)

        with ExitStack() as ctx:
            s = lambda name, shape, dt=F32: sb("n_" + name, shape, dt, ctx)
            gw_sb = s("gw", [P, 2, D])
            wg = s("wg", [P, 2, ROW + H])
            prod = s("prod", [P, 2, D])
            attb = s("attb", [P, 2, D])
            wkv = s("wkv", [P, 2, 2 * D])
            xt = s("xt", [P, 2, D])
            xn = s("xn", [P, 2, D])
            xnT = s("xnT", [P, 2, 2, P])
            st = s("st", [P, 2, 6])
            mv = s("mv", [P, 2, 2])
            ve = s("ve", [P, 2, 1])
            rstd = s("rstd", [P, 2, 1])
            rows = s("rows", [P, 2, ROW])
            ek = s("ek", [P, 2, D])
            rk = s("rk", [P, 2, D])
            kf = s("kf", [P, 2, D])
            vv = s("vv", [P, 2, 2, P + 1])
            zero = s("zero", [P, P + 1])
            pT = ctx.enter_context(nc.psum_tensor("n_pT", [P, 2, 512], F32))
            pG = ctx.enter_context(nc.psum_tensor("n_pG", [P, 512], F32))
            pK = ctx.enter_context(nc.psum_tensor("n_pK", [P, 2, 512], F32))
            pKV = ctx.enter_context(nc.psum_tensor("n_pKV", [P, 2, 512], F32))
            sem = lambda n: ctx.enter_context(nc.semaphore("n_" + n))
            w_in = sem("weights_in")
            x_in = [sem(f"x_in{k}") for k in range(2)]
            xn_out = [sem(f"xn_out{k}") for k in range(2)]
            row_out = [sem(f"row_out{k}") for k in range(2)]
            prep, norm, tr, trc = sem("weights_ready"), sem("norm"), sem("transposed"), sem("transposed_copied")
            proj, kproj = sem("projected"), sem("kv_projected")
            evac, kact, kdone, kvsum = sem("rows_ready"), sem("k_activated"), sem("k_ready"), sem("kv_summed")
            seeded, fin = sem("seeded"), sem("kv_copied")
            tick = sem("pe_ticks")
            rooted = sem("rooted")
            block = ctx.enter_context(nc.Block())

            @block.gpsimd
            def _(pool):
                def body(t, k, on):
                    if on(0):
                        await_count(pool, norm, 4 * t + 3)
                        pool.tensor_tensor(rstd[:, k, :], ve[:, k, :], mhalf[:, :], ALU.pow).then_inc(rooted, 1)
                walk(pool, NT, 0, 2, body, head=2)

            @block.sync
            def _(sp):
                sp.dma_start(gw_sb[:, :, :], gW.rearrange("(k p) n -> p k n", p=P)).then_inc(w_in, 16)
                sp.dma_start(attb[:, 0, :], att_src.rearrange("h c -> (h c)").partition_broadcast(P)).then_inc(w_in, 16)
                sp.dma_start(attb[:, 1, :], att_dst.rearrange("h c -> (h c)").partition_broadcast(P)).then_inc(w_in, 16)
                sp.dma_start(wkv[:, :, :], wqkvT[:, D:3 * D].rearrange("(k p) n -> p k n", p=P)).then_inc(w_in, 16)

                def body(t, k, on):
                    if on(0):
                        await_count(sp, norm, 4 * (t - 2) + 4, sp_tick)
                        sp.dma_start(xt[:, k, :], x[bass.ds(t * P, P), :]).then_inc(x_in[k], 16)
                    if on(1):
                        k = (k - 1) % 2
                        await_count(sp, norm, 4 * (t - 1) + 4, sp_tick)
                        sp.dma_start(xn_d[bass.ds((t - 1) * P, P), :], xn[:, k, :]).then_inc(xn_out[k], 16)
                        await_count(sp, evac, 4 * (t - 1) + 1, sp_tick)
                        sp.dma_start(table[bass.ds((t - 1) * P, P), :], rows[:, k, :]).then_inc(row_out[k], 16)
                walk(sp, NT, 1, 2, body, head=2)
                for k in range(2):
                    sp.wait_ge(xn_out[k], 16 * ((NT + 1 - k) // 2))
                    sp.wait_ge(row_out[k], 16 * ((NT + 1 - k) // 2))

            @block.vector
            def _(dve):
                dve.memset(zero[:, :], 0.0).then_inc(prep, 1)
                dve.wait_ge(w_in, 64)
                for k in range(2):
                    dve.tensor_copy(wg[:, k, 0:ROW].rearrange("p (h c) -> p h c", h=H)[:, :, 0:C],
                                    gw_sb[:, k, :].rearrange("p (h c) -> p h c", h=H)).then_inc(prep, 1)
                n = 3
                for a in range(2):
                    for k in range(2):
                        dve.tensor_tensor(prod[:, k, :], gw_sb[:, k, :], attb[:, a, :], ALU.mult).then_inc(prep, 1)
                        n += 1
                        dve.wait_ge(prep, n)
                        o = (wg[:, k, 0:ROW].rearrange("p (h c) -> p h c", h=H)[:, :, C] if a == 0
                             else wg[:, k, ROW:ROW + H])
                        dve.tensor_reduce(o, prod[:, k, :].rearrange("p (h c) -> p h c", h=H), AX.X,
                                          ALU.add).then_inc(prep, 1)
                        n += 1
                        dve.wait_ge(prep, n)

                def body(t, k, on):
                    if on(0):
                        await_count(dve, x_in[k], 8 * (t - k) + 16)
                        dve.bn_stats(st[:, k, :], xt[:, k, :]).then_inc(norm, 1)
                        await_count(dve, norm, 4 * t + 1, dve_tick)
                        dve.bn_aggr(mv[:, k, :], st[:, k, :]).then_inc(norm, 1)
                        await_count(dve, norm, 4 * t + 2)
                        dve.tensor_scalar(ve[:, k, :], mv[:, k, 1:2], LN_EPS, None, ALU.add).then_inc(norm, 1)
                        await_count(dve, rooted, t + 1)
                        await_count(dve, xn_out[k], 8 * (t - k - 2) + 16)
                        await_count(dve, tr, t - 1)
                        dve.tensor_scalar(xn[:, k, :], xt[:, k, :], mv[:, k, 0:1], rstd[:, k, :],
                                          ALU.subtract, ALU.mult).then_inc(norm, 1)
                    if on(1):
                        t, k = t - 1, (k - 1) % 2
                        await_count(dve, kact, 3 * t + 2)
                        await_count(dve, kvsum, t - 1)
                        dve.scalar_tensor_tensor(kf[:, k, :], ek[:, k, :], 1.0, rk[:, k, :], ALU.min,
                                                 ALU.add).then_inc(kdone, 1)
                walk(dve, NT, 1, 2, body, head=2)
                dve.memset(kvb[:, :, :], 0.0).then_inc(fin, 1)
                dve.wait_ge(fin, 1)
                dve.wait_ge(kvsum, NT + 2)
                for c in range(2):
                    for h in range(4):
                        q = slice(C * h, C * h + C)
                        dve.tensor_copy(kvb[q, c, q], pKV[q, c, q]).then_inc(fin, 1)
                        dve.tensor_copy(kvb[q, c, P + h:P + h + 1], pKV[q, c, P:P + 1]).then_inc(fin, 1)

            @block.tensor
            def _(pe):
                pe.wait_ge(prep, 11)
                for c in range(2):
                    pe.matmul(pKV[:, c, 0:P + 1], zero[:, 0:P], zero[:, :], start=True, stop=False,
                              skip_group_check=True)

                def body(t, k, on):
                    if on(0):
                        await_count(pe, norm, 4 * t + 4, tick)
                        await_count(pe, trc, t - 1, tick)
                        for c in range(2):
                            last = pe.transpose(pT[:, k, P * c:P * c + P], xn[:, k, P * c:P * c + P], ident[:, :])
                        last.then_inc(tr, 1)
                        await_count(pe, trc, t + 1, tick)
                        await_count(pe, evac, 4 * (t - 1) + 2, tick)
                        for c in range(2):
                            last = pe.matmul(pG[:, 0:ROW + H], xnT[:, k, c, :], wg[:, c, :], start=(c == 0),
                                             stop=(c == 1))
                        last.then_inc(proj, 1)
                        await_count(pe, kact, 3 * (t - 2) + 3, tick)
                        for c in range(2):
                            last = pe.matmul(pK[:, k, :], xnT[:, k, c, :], wkv[:, c, :], start=(c == 0),
                                             stop=(c == 1))
                        last.then_inc(kproj, 1)
                    if on(1):
                        t, k = t - 1, (k - 1) % 2
                        await_count(pe, kdone, t + 1, tick)
                        await_count(pe, evac, 4 * t + 4, tick)
                        for c in range(2):
                            last = pe.matmul(pKV[:, c, 0:P + 1], kf[:, k, P * c:P * c + P], vv[:, k, c, :],
                                             start=False, stop=False, skip_group_check=True)
                        last.then_inc(kvsum, 1)
                walk(pe, NT, 1, 2, body, head=2)
                for c in range(2):
                    pe.matmul(pKV[:, c, 0:P + 1], zero[:, 0:P], zero[:, :], start=False, stop=True,
                              skip_group_check=True).then_inc(kvsum, 1)

            @block.scalar
            def _(act):
                def body(t, k, on):
                    if not on(0):
                        return
                    await_count(act, tr, t + 1)
                    await_count(act, kproj, t - 1)
                    act.activation(xnT[:, k, :, :].rearrange("p c n -> p (c n)"), pT[:, k, 0:2 * P],
                                   ACT.Copy).then_inc(trc, 1)
                    await_count(act, proj, t + 1)
                    await_count(act, row_out[k], 8 * (t - k - 2) + 16)
                    act.activation(rows[:, k, :], pG[:, 0:ROW], ACT.Copy).then_inc(evac, 1)
                    act.activation(adst[:, bass.ds(t, 1), :], pG[:, ROW:ROW + H].unsqueeze(1), ACT.Copy).then_inc(evac, 1)
                    await_count(act, kproj, t + 1)
                    await_count(act, kdone, t - 1)
                    act.activation(ek[:, k, :], pK[:, k, 0:D], ACT.Exp).then_inc(kact, 1)
                    act.activation(rk[:, k, :], pK[:, k, 0:D], ACT.Relu).then_inc(kact, 1)
                    await_count(act, kvsum, t - 1)
                    act.activation(vv[:, k, :, 0:P], pK[:, k, D:2 * D].rearrange("p (c n) -> p c n", c=2),
                                   ACT.Copy).then_inc(kact, 1)
                    act.activation(vv[:, k, 0, P:P + 1], valid[:, bass.ds(t, 1)], ACT.Copy).then_inc(evac, 1)
                    act.activation(vv[:, k, 1, P:P + 1], valid[:, bass.ds(t, 1)], ACT.Copy).then_inc(evac, 1)
                walk(act, NT, 0, 2, body, head=2)
                act.wait_ge(evac, 4 * NT)

        with ExitStack() as ctx:
            s = lambda name, shape, dt=F32: sb("e_" + name, shape, dt, ctx)
            pair = s("pair", [P, RING, 2, J], I32)
            gat = [s(f"gat{k}", [P, J, ROW]) for k in range(RING)]
            dloc = s("dloc", [P, RING, J])
            hot = s("hot", [P, RING, J, P])
            hotT = s("hotT", [P, RING, J, P])
            dsc = s("dsc", [P, RING, J, H])
            drow = s("drow", [J * H, RING, P])
            diff = s("diff", [J * H, RING, P + 1])
            smax = s("smax", [J * H, RING, P])
            lmax = s("lmax", [J * H, RING, P])
            zb = s("zb", [P, RING, J, H + 1])
            big = s("big", [P, 1])
            pen = s("pen", [P, RING, J])
            mc4 = s("mc4", [P, RING, J, H])
            mc = s("mc", [P, RING, H])
            uc = s("uc", [P, RING, H])
            lc = s("lc", [P, RING, H])
            dd = s("dd", [P, RING, 2 * H])
            dr = s("dr", [P, RING, H])
            rr = s("rr", [P, RING, H])
            ze = s("ze", [P, RING, J, H])
            le = s("le", [P, RING, J, H])
            se = s("se", [P, RING, J, H])
            sc = s("sc", [P, RING, J, H])
            AR = 4
            accb = s("accb", [P, AR, ROW])
            pX = ctx.enter_context(nc.psum_tensor("e_pX", [P, 2, 512], F32))
            pH = ctx.enter_context(nc.psum_tensor("e_pH", [P, 512], F32))
            pL = ctx.enter_context(nc.psum_tensor("e_pL", [P, 512], F32))
            pM = ctx.enter_context(nc.psum_tensor("e_pM", [P, 512], F32))
            pD = ctx.enter_context(nc.psum_tensor("e_pD", [P, 512], F32))
            pA = ctx.enter_context(nc.psum_tensor("e_pA", [P, 2, 512], F32))
            sem = lambda n: ctx.enter_context(nc.semaphore("e_" + n))
            pair_in = [sem(f"pair_in{k}") for k in range(RING)]
            rows_in = [sem(f"rows_in{k}") for k in range(RING)]
            init, absent, scored, stored = sem("init"), sem("absent"), sem("node_scores"), sem("sums_stored")
            atick = sem("act_ticks")
            local, scan, upd, shift, msg, accum = (sem("one_hot"), sem("segment_max"), sem("max_updated"),
                                                   sem("shifted"), sem("messages"), sem("accumulated"))
            dscaled, rowcopy, lastcopy, factor, expd = (sem("dst_scaled"), sem("rows_copied"), sem("last_copied"),
                                                        sem("rescale_factor"), sem("exponentials"))
            turned, lastT, tomax, expand, agg = (sem("turned"), sem("last_turned"), sem("chunk_max"),
                                                 sem("expanded"), sem("aggregated"))
            ptick, etick, dtick = sem("pool_ticks"), sem("pe_ticks"), sem("dve_ticks")
            block = ctx.enter_context(nc.Block())
            UPD = 6

            @block.sync
            def _(sp):
                def body(t, k, on):
                    start = sp.value_load(start_i[0:1, bass.ds(t, 1)], min_val=0, max_val=E)
                    await_count(sp, local, 2 * (t - RING) + 1, sp_tick)
                    await_count(sp, rows_in[k], 8 * (t - k - RING) + 64, sp_tick)
                    sp.dma_start(pair[:, k, :, :],
                                 edges[:, bass.ds(start, SE)].rearrange("a (p j) -> p a j", p=P)).then_inc(pair_in[k], 16)
                walk(sp, STEPS, 0, RING, body)

            @block.gpsimd
            def _(pool):
                def body(t, k, on):
                    await_count(pool, pair_in[k], 2 * (t - k) + 16, ptick)
                    await_count(pool, agg, t - RING + 1, ptick)
                    for j in range(J):
                        pool.indirect_dma_start(gat[k][:, j, :], None, table,
                                                bass.IndirectOffsetOnAxis(pair[:, k, 0, j:j + 1], 0)
                                                ).then_inc(rows_in[k], 16)
                walk(pool, STEPS, 0, RING, body)
                for k in range(RING):
                    pool.wait_ge(rows_in[k], 64 * ((STEPS + RING - 1 - k) // RING))

            def heads(k):
                return gat[k][:, :, :].rearrange("p j (h c) -> p j h c", h=H)

            @block.vector
            def _(dve):
                dve.memset(diff[:, :, :], -1.0e25).then_inc(init, 1)
                dve.memset(zb[:, :, :, :], 1.0).then_inc(init, 1)
                dve.memset(dd[:, :, :], NEG).then_inc(init, 1)
                dve.memset(accb[:, :, :], 0.0).then_inc(init, 1)
                dve.memset(big[:, :], -NEG).then_inc(init, 1)
                dve.wait_ge(init, 5)

                pm = pM[:, 0:J * (H + 1)].rearrange("p (j h) -> p j h", j=J)
                pd = pD[:, 0:J * 2 * H].rearrange("p (j h) -> p j h", j=J)
                per_head = lambda ap: ap.rearrange("p (h c) -> p h c", h=H)

                def body(t, k, on):
                    t1, k1 = t - 1, (k - 1) % RING
                    t3, k3 = t - 3, (k - 3) % RING
                    t4, k4 = t - 4, (k - 4) % RING
                    t7, k7 = t - 7, (k - 7) % RING
                    if on(4):
                        await_count(dve, expand, t4 + 1)
                        dve.tensor_tensor(ze[:, k4, :, :], heads(k4)[:, :, :, C], pd[:, :, 0:H],
                                          ALU.add).then_inc(shift, 1)
                    if on(0):
                        await_count(dve, pair_in[k], 2 * (t - k) + 16)
                        await_count(dve, agg, t - RING + 1)
                        dve.tensor_scalar(dloc[:, k, :], pair[:, k, 1, :], tile_f[:, bass.ds(t, 1)], None,
                                          ALU.subtract).then_inc(local, 1)
                    if on(4):
                        await_count(dve, shift, 3 * t4 + 1)
                        dve.scalar_tensor_tensor(le[:, k4, :, :], ze[:, k4, :, :], 0.2, ze[:, k4, :, :], ALU.mult,
                                                 ALU.max).then_inc(shift, 1)
                    if on(3):
                        await_count(dve, absent, t3 + 1)
                        dve.tensor_tensor(mc4[:, k3, :, :], pm[:, :, 0:H],
                                          pen[:, k3, :].unsqueeze(2).to_broadcast([P, J, H]),
                                          ALU.subtract).then_inc(upd, 1)
                    if on(4):
                        await_count(dve, shift, 3 * t4 + 2)
                        dve.tensor_tensor(se[:, k4, :, :], le[:, k4, :, :], pd[:, :, H:2 * H],
                                          ALU.subtract).then_inc(shift, 1)
                    if on(3):
                        await_count(dve, upd, UPD * t3 + 1)
                        dve.tensor_reduce(mc[:, k3, :], mc4[:, k3, :, :].rearrange("p j h -> p h j"), AX.X,
                                          ALU.max).then_inc(upd, 1)
                    if on(0):
                        await_count(dve, local, 2 * t + 1)
                        dve.tensor_tensor(hot[:, k, :, :], iota_n[:, :].unsqueeze(1).to_broadcast([P, J, P]),
                                          dloc[:, k, :].unsqueeze(2).to_broadcast([P, J, P]),
                                          ALU.is_equal).then_inc(local, 1)
                    if on(3):
                        await_count(dve, upd, UPD * t3 + 2)
                        await_count(dve, scored, t3 + 1)
                        dve.tensor_tensor(uc[:, k3, :], mc[:, k3, :], dd[:, k3, 0:H], ALU.add).then_inc(upd, 1)
                    if on(1):
                        await_count(dve, rowcopy, 2 * t1 + 1)
                        dve.tensor_tensor(diff[:, k1, 1:P], drow[:, k1, 0:P - 1], drow[:, k1, 1:P],
                                          ALU.subtract).then_inc(scan, 1)
                    if on(3):
                        await_count(dve, upd, UPD * t3 + 3)
                        dve.scalar_tensor_tensor(lc[:, k3, :], uc[:, k3, :], 0.2, uc[:, k3, :], ALU.mult,
                                                 ALU.max).then_inc(upd, 1)
                    if on(1):
                        await_count(dve, scan, 3 * t1 + 1)
                        dve.tensor_tensor_scan(smax[:, k1, :], diff[:, k1, 0:P], pX[0:J * H, k1 % 2, 0:P], 0.0,
                                               ALU.add, ALU.max).then_inc(scan, 1)
                    if on(3):
                        await_count(dve, upd, UPD * t3 + 4)
                        dve.scalar_tensor_tensor(dd[:, k3, H:2 * H], dd[:, (k3 - 1) % RING, H:2 * H],
                                                 reset[:, bass.ds(t3, 1)], lc[:, k3, :], ALU.add,
                                                 ALU.max).then_inc(upd, 1)
                    if on(7):
                        await_count(dve, accum, 2 * t7)
                        await_count(dve, factor, t7 + 1)
                        await_count(dve, stored, t7 - AR + 1)
                        a = accb[:, k7 % AR, :]
                        dve.tensor_tensor(per_head(a), per_head(accb[:, (k7 - 1) % AR, :]),
                                          rr[:, k7, :].unsqueeze(2).to_broadcast([P, H, CW]),
                                          ALU.mult).then_inc(accum, 1)
                    if on(3):
                        await_count(dve, upd, UPD * t3 + 5)
                        dve.scalar_tensor_tensor(dr[:, k3, :], dd[:, (k3 - 1) % RING, H:2 * H],
                                                 reset[:, bass.ds(t3, 1)], dd[:, k3, H:2 * H], ALU.add,
                                                 ALU.subtract).then_inc(upd, 1)
                    if on(1):
                        await_count(dve, scan, 3 * t1 + 2)
                        dve.scalar_tensor_tensor(lmax[:, k1, :], diff[:, k1, 1:P + 1], 0.0, smax[:, k1, :],
                                                 ALU.is_lt, ALU.mult).then_inc(scan, 1)
                    if on(4):
                        await_count(dve, expd, 2 * t4 + 2)
                        g = heads(k4)
                        dve.tensor_tensor(g[:, :, :, 0:C], g[:, :, :, 0:C],
                                          g[:, :, :, C:CW].to_broadcast([P, J, H, C]), ALU.mult).then_inc(msg, 1)
                    if on(7):
                        await_count(dve, accum, 2 * t7 + 1)
                        await_count(dve, agg, t7 + 1)
                        dve.tensor_tensor(a, a, pA[:, k7 % 2, 0:ROW], ALU.add).then_inc(accum, 1)
                walk(dve, STEPS, 7, RING, body, head=2)

            @block.scalar
            def _(act):
                def body(t, k, on):
                    t1, k1 = t - 1, (k - 1) % RING
                    t2, k2 = t - 2, (k - 2) % RING
                    t3, k3 = t - 3, (k - 3) % RING
                    t4, k4 = t - 4, (k - 4) % RING
                    if on(0):
                        await_count(act, local, 2 * t + 1)
                        act.activation(dsc[:, k, :, :], dloc[:, k, :].unsqueeze(2).to_broadcast([P, J, H]),
                                       ACT.Copy, scale=1.0e25).then_inc(dscaled, 1)
                    if on(4):
                        await_count(act, shift, 3 * t4 + 3)
                        act.activation(sc[:, k4, :, :], se[:, k4, :, :], ACT.Relu, scale=-1.0).then_inc(expd, 1)
                        await_count(act, expd, 2 * t4 + 1)
                        act.activation(heads(k4)[:, :, :, C], sc[:, k4, :, :], ACT.Exp, scale=-1.0).then_inc(expd, 1)
                    if on(3):
                        await_count(act, upd, UPD * t3 + 6)
                        act.activation(rr[:, k3, :], dr[:, k3, :], ACT.Exp).then_inc(factor, 1)
                    if on(0):
                        await_count(act, turned, 2 * t + 1)
                        act.activation(drow[:, k, :], pX[0:J * H, k % 2, P:2 * P], ACT.Copy).then_inc(rowcopy, 1)
                        await_count(act, turned, 2 * t + 2)
                        act.activation(hotT[:, k, :, :].rearrange("p j n -> p (j n)"), pH[:, :],
                                       ACT.Copy).then_inc(rowcopy, 1)
                    if on(1):
                        await_count(act, lastT, t1 + 1)
                        act.activation(zb[:, k1, :, 0:H], pL[:, 0:J * H].rearrange("p (j h) -> p j h", j=J),
                                       ACT.Copy).then_inc(lastcopy, 1)
                    if on(2):
                        await_count(act, tomax, t2 + 1)
                        act.activation(pen[:, k2, :], pM[:, 0:J * (H + 1)].rearrange("p (j h) -> p j h", j=J)[:, :, H],
                                       ACT.Relu, scale=NEG, bias=big[:, :]).then_inc(absent, 1)
                    if on(2):
                        i2 = act.value_load(tile_i[0:1, bass.ds(t2, 1)], min_val=0, max_val=NT - 1)
                        act.activation(dd[:, k2, 0:H], adst[:, bass.ds(i2, 1), :].rearrange("p a h -> p (a h)"),
                                       ACT.Copy).then_inc(scored, 1)
                    if on(8):
                        t8 = t - 8
                        i8 = act.value_load(tile_i[0:1, bass.ds(t8, 1)], min_val=0, max_val=NT - 1)
                        await_count(act, stored, t8, atick)
                        await_count(act, accum, 2 * t8 + 2, atick)
                        act.activation(acc[:, bass.ds(i8, 1), :].rearrange("p a n -> p (a n)"),
                                       accb[:, k % AR, :], ACT.Copy).then_inc(stored, 1)
                act.wait_ge(init, 5)
                walk(act, STEPS, 8, RING, body, head=2)
                act.wait_ge(stored, STEPS)

            @block.tensor
            def _(pe):
                def turn(t, k):
                    await_count(pe, pair_in[k], 2 * (t - k) + 16, etick)
                    await_count(pe, rows_in[k], 8 * (t - k) + 64, etick)
                    await_count(pe, dscaled, t + 1, etick)
                    await_count(pe, scan, 3 * (t - 2) + 2, etick)
                    pe.transpose(pX[0:J * H, k % 2, 0:P], heads(k)[:, :, :, C], ident[:, :])
                    pe.transpose(pX[0:J * H, k % 2, P:2 * P], dsc[:, k, :, :].rearrange("p j h -> p (j h)"),
                                 ident[:, :]).then_inc(turned, 1)
                    await_count(pe, local, 2 * t + 2, etick)
                    await_count(pe, rowcopy, 2 * (t - 1) + 2, etick)
                    for j in range(J):
                        last = pe.transpose(pH[:, P * j:P * j + P], hot[:, k, j, :], ident[:, :])
                    last.then_inc(turned, 1)

                def turn_last(t, k):
                    await_count(pe, scan, 3 * t + 3, etick)
                    await_count(pe, lastcopy, t, etick)
                    pe.transpose(pL[:, 0:J * H], lmax[:, k, :], ident[0:J * H, 0:J * H]).then_inc(lastT, 1)

                def chunk_max(t, k):
                    await_count(pe, lastcopy, t + 1, etick)
                    await_count(pe, upd, UPD * (t - 1) + 1, etick)
                    for j in range(J):
                        o = j * (H + 1)
                        last = pe.matmul(pM[:, o:o + H + 1], hot[:, k, j, :], zb[:, k, j, :], start=True,
                                         stop=True)
                    last.then_inc(tomax, 1)

                def expand_nodes(t, k):
                    await_count(pe, scored, t + 1, etick)
                    await_count(pe, upd, UPD * t + 5, etick)
                    await_count(pe, rowcopy, 2 * t + 2, etick)
                    await_count(pe, shift, 3 * (t - 1) + 3, etick)
                    for j in range(J):
                        o = j * 2 * H
                        last = pe.matmul(pD[:, o:o + 2 * H], hotT[:, k, j, :], dd[:, k, :], start=True,
                                         stop=True)
                    last.then_inc(expand, 1)

                def aggregate(t, k):
                    await_count(pe, msg, t + 1, etick)
                    await_count(pe, accum, 2 * (t - 2) + 2, etick)
                    for j in range(J):
                        last = pe.matmul(pA[:, k % 2, 0:ROW], hot[:, k, j, :], gat[k][:, j, :], start=(j == 0),
                                         stop=(j == J - 1))
                    last.then_inc(agg, 1)

                def body(t, k, on):
                    if on(6):
                        aggregate(t - 6, (k - 6) % RING)
                    if on(2):
                        chunk_max(t - 2, (k - 2) % RING)
                    if on(0):
                        turn(t, k)
                    if on(1):
                        turn_last(t - 1, (k - 1) % RING)
                    if on(3):
                        expand_nodes(t - 3, (k - 3) % RING)
                walk(pe, STEPS, 6, RING, body)

        with ExitStack() as ctx:
            s = lambda name, shape, dt=F32: sb("m_" + name, shape, dt, ctx)
            wq = s("wq", [P, 2, D])
            w1 = s("w1", [P, 2, D])
            w2 = s("w2", [P, 2, D])
            wgate = s("wgate", [P, 2, X])
            b1c = s("b1c", [P, 2])
            VEC = {n: s(n, [P, D]) for n in ("ln1g", "ln1b", "ln2g", "ln2b", "b2", "gbias")}
            gateb = s("gateb", [P, X])
            xt = s("xt", [P, 2, D])
            xn = s("xn", [P, 2, D])
            xnT = s("xnT", [P, 2, 2, P])
            eq = s("eq", [P, 2, 2, P])
            rq = s("rq", [P, 2, 2, P])
            qf = s("qf", [P, 2, 2, P])
            den = s("den", [P, 2, H])
            zi = s("zi", [P, 2, H])
            tt = s("tt", [P, 2, D])
            x1p = s("x1p", [P, 2, D])
            st = s("st", [P, 2, 6])
            mv = s("mv", [P, 2, 2])
            ve = s("ve", [P, 2, 1])
            rstd = s("rstd", [P, 2, 1])
            na = s("na", [P, 2, D])
            nb = s("nb", [P, 2, D])
            x1 = s("x1", [P, 2, D])
            x1T = s("x1T", [P, 2, 2, P])
            hT = s("hT", [P, 2, 2, P])
            ya = s("ya", [P, 2, D])
            yb = s("yb", [P, 2, D])
            gden = s("gden", [P, 2, H])
            gnn = s("gnn", [P, 2, D])
            x2 = s("x2", [P, 2, D])
            lg = s("lg", [P, 2, X])
            v8 = s("v8", [P, 2, 8])
            i8 = s("i8", [P, 2, 8], U32)
            zeros = s("zeros", [P, D])
            x3T = s("x3T", [P, 2, 2, P])
            ps = ctx.enter_context(nc.psum_tensor("m_ps", [P, 8, 512], F32))
            pX_, pQ, pT, p1, pH, pYY, p3, pL = (ps[:, b, :] for b in range(8))
            sem = lambda n: ctx.enter_context(nc.semaphore("m_" + n))
            w_in = sem("weights_in")
            x_in = [sem(f"x_in{k}") for k in range(2)]
            x2_out = [sem(f"x2_out{k}") for k in range(2)]
            zeroed, slots_zero = sem("zeroed"), sem("slots_zeroed")
            vec, pes, acts, tick = sem("vector_ops"), sem("products"), sem("activations"), sem("pe_ticks")
            block = ctx.enter_context(nc.Block())
            rooted = sem("rooted")
            NV, NP_, NA = 34, 8, 7

            @block.gpsimd
            def _(pool):
                def body(t, k, on):
                    for at in (9, 21, 27):
                        await_count(pool, vec, NV * t + at)
                        pool.tensor_tensor(rstd[:, k, :], ve[:, k, :], mhalf[:, :], ALU.pow).then_inc(rooted, 1)
                walk(pool, NT, 0, 2, body)

            @block.sync
            def _(sp):
                for dst, src in ((wq, wqkvT[:, 0:D]), (w1, w1T), (w2, w2T), (wgate, gate_w)):
                    sp.dma_start(dst[:, :, :], src.rearrange("(k p) n -> p k n", p=P)).then_inc(w_in, 16)
                with nc.allow_non_contiguous_dma(reason="a bias of 256 floats, once"):
                    sp.dma_start(b1c[:, :], b1.rearrange("(k p) -> p k", p=P)).then_inc(w_in, 16)
                for n, v in (("ln1g", ln1g), ("ln1b", ln1b), ("ln2g", ln2g), ("ln2b", ln2b), ("b2", b2),
                             ("gbias", gbias)):
                    sp.dma_start(VEC[n][:, :], v.partition_broadcast(P)).then_inc(w_in, 16)
                sp.dma_start(gateb[:, :], gate_b.partition_broadcast(P)).then_inc(w_in, 16)
                sp.wait_ge(zeroed, 1)
                sp.dma_start(slots_d.rearrange("(t p) n -> p t n", p=P),
                             zeros[:, :].unsqueeze(1).to_broadcast([P, XT, D])).then_inc(slots_zero, 16)

                def body(t, k, on):
                    if on(0):
                        await_count(sp, vec, NV * (t - 2) + NV, sp_tick)
                        sp.dma_start(xt[:, k, :], x[bass.ds(t * P, P), :]).then_inc(x_in[k], 16)
                        sp.dma_start(xn[:, k, :], xn_d[bass.ds(t * P, P), :]).then_inc(x_in[k], 16)
                    if on(1):
                        t, k = t - 1, (k - 1) % 2
                        await_count(sp, vec, NV * t + 24, sp_tick)
                        sp.dma_start(x2_d[bass.ds(t * P, P), :], x2[:, k, :]).then_inc(x2_out[k], 16)
                walk(sp, NT, 1, 2, body)
                for k in range(2):
                    sp.wait_ge(x2_out[k], 16 * ((NT + 1 - k) // 2))
                sp.wait_ge(slots_zero, 16)

            @block.vector
            def _(dve):
                dve.memset(zeros[:, :], 0.0).then_inc(zeroed, 1)
                dve.wait_ge(w_in, 16 * 12)

                def body(t, k, on):
                    if not on(0):
                        return
                    done, roots = [0], [0]

                    def link(ins):
                        done[0] += 1
                        ins.then_inc(vec, 1)
                        await_count(dve, vec, NV * t + done[0], dve_tick)

                    hd = lambda ap: ap.rearrange("p (h c) -> p h c", h=H)
                    await_count(dve, x_in[k], 16 * (t - k) + 32)
                    await_count(dve, acts, NA * t + 3)
                    link(dve.scalar_tensor_tensor(qf[:, k, :, :], eq[:, k, :, :], 1.0, rq[:, k, :, :], ALU.min, ALU.add))
                    await_count(dve, pes, NP_ * t + 3)
                    pt = pT[:, 0:2 * (P + 4)].rearrange("p (c n) -> p c n", c=2)
                    link(dve.tensor_scalar(den[:, k, :].rearrange("p (c h) -> p c h", c=2), pt[:, :, P:P + 4],
                                           1e-6, None, ALU.add))
                    link(dve.reciprocal(zi[:, k, :], den[:, k, :]))
                    for c in range(2):
                        link(dve.tensor_tensor(tt[:, k, P * c:P * c + P].rearrange("p (h c) -> p h c", h=4),
                                               pt[:, c, 0:P].rearrange("p (h c) -> p h c", h=4),
                                               zi[:, k, 4 * c:4 * c + 4].unsqueeze(2).to_broadcast([P, 4, C]),
                                               ALU.mult))
                    link(dve.tensor_tensor(x1p[:, k, :], tt[:, k, :], xn[:, k, :], ALU.add))

                    def stats(src):
                        link(dve.bn_stats(st[:, k, :], src))
                        link(dve.bn_aggr(mv[:, k, :], st[:, k, :]))
                        link(dve.tensor_scalar(ve[:, k, :], mv[:, k, 1:2], LN_EPS, None, ALU.add))
                        roots[0] += 1
                        await_count(dve, rooted, 3 * t + roots[0])

                    def affine(dst, src, g, b):
                        link(dve.scalar_tensor_tensor(na[:, k, :], src, mv[:, k, 0:1], g[:, :], ALU.subtract, ALU.mult))
                        link(dve.scalar_tensor_tensor(dst, na[:, k, :], rstd[:, k, :], b[:, :], ALU.mult, ALU.add))

                    stats(x1p[:, k, :])
                    affine(x1[:, k, :], x1p[:, k, :], VEC["ln1g"], VEC["ln1b"])
                    a = acc[:, bass.ds(t, 1), :].rearrange("p a n -> p (a n)")
                    ah = hd(a)
                    link(dve.tensor_scalar(gden[:, k, :], ah[:, :, C], 1e-16, None, ALU.add))
                    link(dve.reciprocal(zi[:, k, :], gden[:, k, :]))
                    link(dve.tensor_tensor(hd(gnn[:, k, :]), ah[:, :, 0:C],
                                           zi[:, k, :].unsqueeze(2).to_broadcast([P, H, C]), ALU.mult))
                    link(dve.tensor_tensor(gnn[:, k, :], gnn[:, k, :], VEC["gbias"][:, :], ALU.add))
                    link(dve.scalar_tensor_tensor(nb[:, k, :], gnn[:, k, :], 0.0, xt[:, k, :], ALU.max, ALU.add))
                    link(dve.tensor_tensor(ya[:, k, :], x1[:, k, :], VEC["b2"][:, :], ALU.add))
                    await_count(dve, pes, NP_ * t + 6)
                    link(dve.tensor_tensor(yb[:, k, :], pYY[:, 0:D], ya[:, k, :], ALU.add))
                    stats(yb[:, k, :])
                    affine(ya[:, k, :], yb[:, k, :], VEC["ln2g"], VEC["ln2b"])
                    await_count(dve, x2_out[k], 8 * (t - k - 2) + 16)
                    link(dve.tensor_tensor(x2[:, k, :], nb[:, k, :], ya[:, k, :], ALU.add))
                    stats(x2[:, k, :])
                    link(dve.tensor_scalar(a[:, 0:D], x2[:, k, :], mv[:, k, 0:1], rstd[:, k, :], ALU.subtract, ALU.mult))
                    link(dve.tensor_scalar(na[:, k, :], x2[:, k, :], mv[:, k, 0:1], rstd[:, k, :], ALU.subtract,
                                           ALU.mult))
                    await_count(dve, pes, NP_ * t + 8)
                    link(dve.tensor_tensor(lg[:, k, :], pL[:, 0:X], gateb[:, :], ALU.add))
                    link(dve.max(v8[:, k, :], lg[:, k, :]))
                    link(dve.max_index(i8[:, k, :], v8[:, k, :], lg[:, k, :]))
                    two = lambda tab: tab[:, bass.ds(t, 1), :].rearrange("p a n -> p (a n)")
                    link(dve.tensor_scalar(two(top_v), v8[:, k, 0:2], 1.0, None, ALU.mult))
                    link(dve.tensor_scalar(two(top_i), i8[:, k, 0:2], 1.0, None, ALU.mult))
                    assert done[0] == NV, done
                walk(dve, NT, 0, 2, body)

            @block.tensor
            def _(pe):
                pe.wait_ge(w_in, 16 * 12)

                def body(t, k, on):
                    if not on(0):
                        return
                    w = lambda sem, v: await_count(pe, sem, v, tick)
                    w(x_in[k], 16 * (t - k) + 32)
                    w(acts, NA * (t - 1) + NA)
                    for c in range(2):
                        last = pe.transpose(pX_[:, P * c:P * c + P], xn[:, k, P * c:P * c + P], ident[:, :])
                    last.then_inc(pes, 1)
                    w(acts, NA * t + 1)
                    for o in range(2):
                        for c in range(2):
                            last = pe.matmul(pQ[:, P * o:P * o + P], wq[:, c, P * o:P * o + P], xnT[:, k, c, :],
                                             start=(c == 0), stop=(c == 1))
                    last.then_inc(pes, 1)
                    w(vec, NV * t + 1)
                    for c in range(2):
                        last = pe.matmul(pT[:, (P + 4) * c:(P + 4) * (c + 1)], qf[:, k, c, :], kvb[:, c, :],
                                         start=True, stop=True)
                    last.then_inc(pes, 1)
                    w(vec, NV * t + 11)
                    for c in range(2):
                        last = pe.transpose(p1[:, P * c:P * c + P], x1[:, k, P * c:P * c + P], ident[:, :])
                    last.then_inc(pes, 1)
                    w(acts, NA * t + 4)
                    for o in range(2):
                        for c in range(2):
                            last = pe.matmul(pH[:, P * o:P * o + P], w1[:, c, P * o:P * o + P], x1T[:, k, c, :],
                                             start=(c == 0), stop=(c == 1))
                    last.then_inc(pes, 1)
                    w(acts, NA * t + 6)
                    for c in range(2):
                        last = pe.matmul(pYY[:, 0:D], hT[:, k, c, :], w2[:, c, :], start=(c == 0), stop=(c == 1))
                    last.then_inc(pes, 1)
                    w(vec, NV * t + 29)
                    for c in range(2):
                        last = pe.transpose(p3[:, P * c:P * c + P], na[:, k, P * c:P * c + P], ident[:, :])
                    last.then_inc(pes, 1)
                    w(acts, NA * t + 7)
                    for c in range(2):
                        last = pe.matmul(pL[:, 0:X], x3T[:, k, c, :], wgate[:, c, :], start=(c == 0), stop=(c == 1))
                    last.then_inc(pes, 1)
                walk(pe, NT, 0, 2, body)

            @block.scalar
            def _(act):
                act.wait_ge(w_in, 16 * 12)

                def body(t, k, on):
                    if not on(0):
                        return
                    both = lambda ap: ap[:, k, :, :].rearrange("p c n -> p (c n)")
                    await_count(act, pes, NP_ * t + 1)
                    act.activation(both(xnT), pX_[:, 0:D], ACT.Copy).then_inc(acts, 1)
                    await_count(act, pes, NP_ * t + 2)
                    act.activation(both(eq), pQ[:, 0:D], ACT.Exp).then_inc(acts, 1)
                    act.activation(both(rq), pQ[:, 0:D], ACT.Relu).then_inc(acts, 1)
                    await_count(act, pes, NP_ * t + 4)
                    act.activation(both(x1T), p1[:, 0:D], ACT.Copy).then_inc(acts, 1)
                    await_count(act, pes, NP_ * t + 5)
                    for c in range(2):
                        act.activation(hT[:, k, c, :], pH[:, P * c:P * c + P], ACT.Gelu, bias=b1c[:, c:c + 1]).then_inc(acts, 1)
                    await_count(act, pes, NP_ * t + 7)
                    act.activation(both(x3T), p3[:, 0:D], ACT.Copy).then_inc(acts, 1)
                walk(act, NT, 0, 2, body)
                act.wait_ge(acts, NA * NT)

        with ExitStack() as ctx:
            s = lambda name, shape, dt=F32: sb("r_" + name, shape, dt, ctx)
            oh = s("oh", [P, 2, NT, X])
            both = s("both", [P, NT, X])
            tot = s("tot", [P, NT, X])
            cum = s("cum", [P, NT, X])
            sl = s("sl", [P, NT, X])
            pick = s("pick", [P, NT, X])
            cnt = s("cnt", [P, X])
            cnt_i = s("cnt_i", [P, X], I32)
            cumx = s("cumx", [P, X])
            base = s("base", [P, X])
            slot_f = s("slot_f", [P, 2, NT])
            dv = s("dv", [P, NT])
            ev = s("ev", [P, NT])
            ev1 = s("ev1", [P, NT])
            past = s("past", [1, XT, X])
            te = s("te", [1, XT])
            R = 4
            stage = [s(f"stage{k}", [P, D]) for k in range(R)]
            sidx = [s(f"sidx{k}", [P, 2], I32) for k in range(R)]
            pr = ctx.enter_context(nc.psum_tensor("r_pr", [P, 4, 512], F32))
            sem = lambda n: ctx.enter_context(nc.semaphore("r_" + n))
            chain, hots, sums, diffs, exps = sem("ops"), sem("one_hots"), sem("prefix_sums"), sem("diffs"), sem("exps")
            rows_staged, idx_staged = sem("rows_staged"), sem("idx_staged")
            tick, dtick, atick = sem("pool_ticks"), sem("dve_ticks"), sem("act_ticks")
            scattered = [sem(f"scattered{k}") for k in range(R)]
            block = ctx.enter_context(nc.Block())
            HALF = 25 * X

            @block.vector
            def _(dve):
                done = [0]

                def link(ins):
                    done[0] += 1
                    ins.then_inc(chain, 1)
                    dve.wait_ge(chain, done[0])

                for k in range(2):
                    link(dve.tensor_tensor(oh[:, k, :, :], iota_n[:, 0:X].unsqueeze(1).to_broadcast([P, NT, X]),
                                           top_i[:, :, k:k + 1].to_broadcast([P, NT, X]), ALU.is_equal))
                dve.tensor_tensor(both[:, :, :], oh[:, 0, :, :], oh[:, 1, :, :], ALU.add).then_inc(hots, 1)
                dve.tensor_tensor(dv[:, :], top_v[:, :, 1], top_v[:, :, 0], ALU.subtract).then_inc(diffs, 1)
                dve.wait_ge(exps, 1)
                link(dve.tensor_scalar(ev1[:, :], ev[:, :], 1.0, None, ALU.add))
                link(dve.reciprocal(dv[:, :], ev1[:, :]))
                link(dve.tensor_copy(wtop[:, :, 0], dv[:, :]))
                link(dve.tensor_tensor(wtop[:, :, 1], dv[:, :], ev[:, :], ALU.mult))
                dve.wait_ge(sums, 1)
                fl = lambda ap: ap[:, :, :].rearrange("p t x -> p (t x)")
                link(dve.tensor_copy(fl(tot)[:, 0:HALF], pr[:, 2, 0:HALF]))
                link(dve.tensor_copy(fl(tot)[:, HALF:NT * X], pr[:, 3, 0:NT * X - HALF]))
                for e in range(X):
                    link(dve.tensor_tensor_scan(cum[:, :, e], tot[:, :, e], ones[:, 0:NT], 0.0, ALU.add, ALU.mult))
                link(dve.tensor_scalar(cnt_i[:, :], cum[:, NT - 1, :], float(P - 1), None, ALU.add))
                link(dve.tensor_scalar(cnt_i[:, :], cnt_i[:, :], P.bit_length() - 1, None, ALU.logical_shift_right))
                link(dve.tensor_copy(cnt[:, :], cnt_i[:, :]))
                link(dve.tensor_tensor_scan(cumx[:, :], cnt[:, :], ones[:, 0:X], 0.0, ALU.add, ALU.mult))
                link(dve.tensor_tensor(base[:, :], cumx[:, :], cnt[:, :], ALU.subtract))
                link(dve.tensor_tensor(sl[:, :, :], cum[:, :, :], tot[:, :, :], ALU.subtract))
                link(dve.tensor_tensor(fl(sl)[:, 0:HALF], fl(sl)[:, 0:HALF], pr[:, 0, 0:HALF], ALU.add))
                link(dve.tensor_tensor(fl(sl)[:, HALF:NT * X], fl(sl)[:, HALF:NT * X], pr[:, 1, 0:NT * X - HALF],
                                       ALU.add))
                link(dve.scalar_tensor_tensor(sl[:, :, :], base[:, :].unsqueeze(1).to_broadcast([P, NT, X]), float(P),
                                              sl[:, :, :], ALU.mult, ALU.add))
                for k in range(2):
                    link(dve.tensor_tensor(pick[:, :, :], sl[:, :, :], oh[:, k, :, :], ALU.mult))
                    link(dve.tensor_reduce(slot_f[:, k, :], pick[:, :, :], AX.X, ALU.add))
                    link(dve.tensor_copy(slot[:, :, k], slot_f[:, k, :]))
                link(dve.tensor_tensor(past[:, :, :], iota_n[0:1, 0:XT].unsqueeze(2).to_broadcast([1, XT, X]),
                                       cumx[0:1, :].unsqueeze(1).to_broadcast([1, XT, X]), ALU.is_ge))
                link(dve.tensor_reduce(te[:, :], past[:, :, :], AX.X, ALU.add))
                link(dve.tensor_scalar(texp[:, :], te[:, :], float(X - 1), None, ALU.min))

                def body(t, k, on):
                    await_count(dve, scattered[k], (t - k - R) * (32 // R) + 32, dtick)
                    dve.tensor_copy(sidx[k][:, :], slot[:, bass.ds(t, 1), :].rearrange("p a n -> p (a n)")
                                    ).then_inc(idx_staged, 1)
                walk(dve, NT, 0, R, body)

            @block.tensor
            def _(pe):
                pe.wait_ge(hots, 1)
                flat = both[:, :, :].rearrange("p t x -> p (t x)")
                for a, w in ((0, lower), (2, ones)):
                    pe.matmul(pr[:, a, 0:HALF], w[:, :], flat[:, 0:HALF], start=True, stop=True)
                    last = pe.matmul(pr[:, a + 1, 0:NT * X - HALF], w[:, :], flat[:, HALF:NT * X], start=True, stop=True)
                last.then_inc(sums, 1)

            @block.scalar
            def _(act):
                act.wait_ge(diffs, 1)
                act.activation(ev[:, :], dv[:, :], ACT.Exp).then_inc(exps, 1)

                def body(t, k, on):
                    await_count(act, scattered[k], (t - k - R) * (32 // R) + 32, atick)
                    act.activation(stage[k][:, :], acc[:, bass.ds(t, 1), 0:D].rearrange("p a n -> p (a n)"),
                                   ACT.Copy).then_inc(rows_staged, 1)
                walk(act, NT, 0, R, body)

            @block.gpsimd
            def _(pool):
                def body(t, k, on):
                    await_count(pool, rows_staged, t + 1, tick)
                    await_count(pool, idx_staged, t + 1, tick)
                    for c in range(2):
                        pool.indirect_dma_start(slots_d, bass.IndirectOffsetOnAxis(sidx[k][:, c:c + 1], 0),
                                                stage[k][:, :], None).then_inc(scattered[k], 16)
                walk(pool, NT, 0, R, body)
                for k in range(R):
                    pool.wait_ge(scattered[k], 32 * ((NT + R - 1 - k) // R))

        with ExitStack() as ctx:
            s = lambda name, shape, dt=F32: sb("x_" + name, shape, dt, ctx)
            R = 4
            w1e = s("w1e", [P, R, 2, F])
            w2e = s("w2e", [P, R, 4, D])
            b1a = s("b1a", [P, X * 4])
            b2a = s("b2a", [P, X, D])
            xs = s("xs", [P, R, D])
            xsT = s("xsT", [P, R, 2, P])
            hT = s("hT", [P, R, 4, P])
            ye = s("ye", [P, R, D])
            pT = ctx.enter_context(nc.psum_tensor("x_pT", [P, 2, 512], F32))
            pH = ctx.enter_context(nc.psum_tensor("x_pH", [P, 2, 512], F32))
            pY = ctx.enter_context(nc.psum_tensor("x_pY", [P, 2, 512], F32))
            sem = lambda n: ctx.enter_context(nc.semaphore("x_" + n))
            b_in = sem("biases_in")
            in_ = [sem(f"in{k}") for k in range(R)]
            out_ = [sem(f"out{k}") for k in range(R)]
            turned, tcopied, hid, relu, prod, summed = (sem("turned"), sem("turned_copied"), sem("hidden"),
                                                        sem("relu"), sem("product"), sem("bias_added"))
            tick, ptick, atick2 = sem("pe_ticks"), sem("pool_ticks"), sem("act_ticks")
            block = ctx.enter_context(nc.Block())
            UN = R

            @block.sync
            def _(sp):
                sp.dma_start(b1a[:, :], eb1).then_inc(b_in, 16)
                sp.dma_start(b2a[:, :, :].rearrange("p x n -> p (x n)"),
                             eb2.rearrange("x n -> (x n)").partition_broadcast(P)).then_inc(b_in, 16)

                def body(t, k, on):
                    e = sp.value_load(texp[0:1, bass.ds(t, 1)], min_val=0, max_val=X - 1)
                    await_count(sp, prod, t - R + 1, sp_tick)
                    sp.dma_start(xs[:, k, :], slots_d[bass.ds(t * P, P), :]).then_inc(in_[k], 16)
                    sp.dma_start(w1e[:, k, :, :], ew1[bass.ds(e, 1), :, :].rearrange("a (k p) f -> p (a k) f", p=P)
                                 ).then_inc(in_[k], 16)
                    sp.dma_start(w2e[:, k, :, :], ew2[bass.ds(e, 1), :, :].rearrange("a (k p) f -> p (a k) f", p=P)
                                 ).then_inc(in_[k], 16)
                walk(sp, XT, 0, UN, body)

            @block.tensor
            def _(pe):
                def body(t, k, on):
                    w = lambda sem, v: await_count(pe, sem, v, tick)
                    if on(0):
                        q, b = k % R, k % 2
                        w(in_[q], 12 * (t - q) + 48)
                        w(tcopied, t - 1)
                        for c in range(2):
                            last = pe.transpose(pT[:, b, P * c:P * c + P], xs[:, q, P * c:P * c + P], ident[:, :])
                        last.then_inc(turned, 1)
                    if on(1):
                        t1, q, b = t - 1, (k - 1) % R, (k - 1) % 2
                        w(tcopied, t1 + 1)
                        w(relu, 4 * (t1 - 2) + 4)
                        for o in range(4):
                            for c in range(2):
                                last = pe.matmul(pH[:, b, P * o:P * o + P], w1e[:, q, c, P * o:P * o + P],
                                                 xsT[:, q, c, :], start=(c == 0), stop=(c == 1))
                        last.then_inc(hid, 1)
                    if on(2):
                        t2, q, b = t - 2, (k - 2) % R, (k - 2) % 2
                        w(relu, 4 * t2 + 4)
                        w(summed, t2 - 1)
                        for c in range(4):
                            last = pe.matmul(pY[:, b, 0:D], hT[:, q, c, :], w2e[:, q, c, :], start=(c == 0),
                                             stop=(c == 3))
                        last.then_inc(prod, 1)
                walk(pe, XT, 2, UN, body)

            @block.scalar
            def _(act):
                act.wait_ge(b_in, 32)

                def body(t, k, on):
                    if on(0):
                        await_count(act, turned, t + 1)
                        await_count(act, hid, t - R + 1)
                        act.activation(xsT[:, k % R, :, :].rearrange("p c n -> p (c n)"), pT[:, k % 2, 0:D],
                                       ACT.Copy).then_inc(tcopied, 1)
                    if on(1):
                        t1, q, b = t - 1, (k - 1) % R, (k - 1) % 2
                        e = act.value_load(texp[0:1, bass.ds(t1, 1)], min_val=0, max_val=X - 1)
                        await_count(act, prod, t1 - R + 2, atick2)
                        await_count(act, hid, t1 + 1, atick2)
                        for o in range(4):
                            act.activation(hT[:, q, o, :], pH[:, b, P * o:P * o + P], ACT.Relu,
                                           bias=b1a[:, bass.ds(e * 4 + o, 1)]).then_inc(relu, 1)
                walk(act, XT, 1, UN, body)

            @block.vector
            def _(dve):
                dve.wait_ge(b_in, 32)

                def body(t, k, on):
                    if on(0):
                        e = dve.value_load(texp[0:1, bass.ds(t, 1)], min_val=0, max_val=X - 1)
                        await_count(dve, out_[k], 4 * (t - k))
                        await_count(dve, prod, t + 1)
                        dve.tensor_tensor(ye[:, k % R, :], pY[:, k % 2, 0:D],
                                          b2a[:, bass.ds(e, 1), :].rearrange("p a n -> p (a n)"), ALU.add
                                          ).then_inc(summed, 1)
                walk(dve, XT, 0, UN, body)

            @block.gpsimd
            def _(pool):
                def body(t, k, on):
                    await_count(pool, summed, t + 1, ptick)
                    pool.dma_start(eout_d[bass.ds(t * P, P), :], ye[:, k % R, :]).then_inc(out_[k % R], 16)
                walk(pool, XT, 0, UN, body)
                for k in range(R):
                    pool.wait_ge(out_[k], 16 * ((XT + R - 1 - k) // R))

        with ExitStack() as ctx:
            s = lambda name, shape, dt=F32: sb("c_" + name, shape, dt, ctx)
            R = 4
            gb = s("gb", [P, D])
            bb = s("bb", [P, D])
            sidx = [s(f"sidx{k}", [P, 2], I32) for k in range(R)]
            eo = [s(f"eo{k}", [P, 2, D]) for k in range(R)]
            x2 = s("x2", [P, R, D])
            y1 = s("y1", [P, R, D])
            y2 = s("y2", [P, R, D])
            st = s("st", [P, R, 6])
            mv = s("mv", [P, R, 2])
            ve = s("ve", [P, R, 1])
            rstd = s("rstd", [P, R, 1])
            o = s("o", [P, R, D])
            sem = lambda n: ctx.enter_context(nc.semaphore("c_" + n))
            w_in = sem("affine_in")
            eo_in = [sem(f"expert_rows_in{k}") for k in range(R)]
            x2_in = [sem(f"x2_in{k}") for k in range(R)]
            out_ = [sem(f"out{k}") for k in range(R)]
            staged, vec, ptick, atick = sem("index_staged"), sem("vector_ops"), sem("pool_ticks"), sem("act_ticks")
            block = ctx.enter_context(nc.Block())
            rooted = sem("rooted")
            NV = 8

            @block.sync
            def _(sp):
                sp.dma_start(gb[:, :], gamma.partition_broadcast(P)).then_inc(w_in, 16)
                sp.dma_start(bb[:, :], beta.partition_broadcast(P)).then_inc(w_in, 16)

                def body(t, k, on):
                    if on(0):
                        await_count(sp, vec, NV * (t - R) + NV, sp_tick)
                        sp.dma_start(x2[:, k, :], x2_d[bass.ds(t * P, P), :]).then_inc(x2_in[k], 16)
                    if on(2):
                        q = (k - 2) % R
                        await_count(sp, vec, NV * (t - 2) + NV, sp_tick)
                        sp.dma_start(out[bass.ds((t - 2) * P, P), :], o[:, q, :]).then_inc(out_[q], 16)
                walk(sp, NT, 2, R, body)
                for k in range(R):
                    sp.wait_ge(out_[k], 16 * ((NT + R - 1 - k) // R))

            @block.scalar
            def _(act):
                def body(t, k, on):
                    await_count(act, eo_in[k], 8 * (t - k), atick)
                    act.activation(sidx[k][:, :], slot[:, bass.ds(t, 1), :].rearrange("p a n -> p (a n)"),
                                   ACT.Copy).then_inc(staged, 1)
                walk(act, NT, 0, R, body)

            @block.gpsimd
            def _(pool):
                def body(t, k, on):
                    if on(0):
                        await_count(pool, staged, t + 1, ptick)
                        await_count(pool, vec, NV * (t - R) + NV, ptick)
                        for c in range(2):
                            pool.indirect_dma_start(eo[k][:, c, :], None, eout_d,
                                                    bass.IndirectOffsetOnAxis(sidx[k][:, c:c + 1], 0)
                                                    ).then_inc(eo_in[k], 16)
                    if on(2):
                        await_count(pool, vec, NV * (t - 2) + 5)
                        pool.tensor_tensor(rstd[:, (k - 2) % R, :], ve[:, (k - 2) % R, :], mhalf[:, :],
                                           ALU.pow).then_inc(rooted, 1)
                walk(pool, NT, 2, R, body)
                for k in range(R):
                    pool.wait_ge(eo_in[k], 32 * ((NT + R - 1 - k) // R))

            @block.vector
            def _(dve):
                dve.wait_ge(w_in, 32)

                def body(t, k, on):
                    done = [0]

                    def link(ins):
                        done[0] += 1
                        ins.then_inc(vec, 1)
                        await_count(dve, vec, NV * t + done[0], dve_tick)

                    wt = lambda c: wtop[:, bass.ds(t, 1), c:c + 1].rearrange("p a n -> p (a n)")
                    await_count(dve, eo_in[k], 8 * (t - k) + 32)
                    link(dve.scalar_tensor_tensor(y1[:, k, :], eo[k][:, 0, :], wt(0),
                                                  acc[:, bass.ds(t, 1), 0:D].rearrange("p a n -> p (a n)"),
                                                  ALU.mult, ALU.add))
                    link(dve.scalar_tensor_tensor(y2[:, k, :], eo[k][:, 1, :], wt(1), y1[:, k, :], ALU.mult, ALU.add))
                    link(dve.bn_stats(st[:, k, :], y2[:, k, :]))
                    link(dve.bn_aggr(mv[:, k, :], st[:, k, :]))
                    link(dve.tensor_scalar(ve[:, k, :], mv[:, k, 1:2], LN_EPS, None, ALU.add))
                    await_count(dve, rooted, t + 1)
                    link(dve.scalar_tensor_tensor(y1[:, k, :], y2[:, k, :], mv[:, k, 0:1], gb[:, :], ALU.subtract,
                                                  ALU.mult))
                    link(dve.scalar_tensor_tensor(y2[:, k, :], y1[:, k, :], rstd[:, k, :], bb[:, :], ALU.mult, ALU.add))
                    await_count(dve, x2_in[k], 4 * (t - k) + 16)
                    await_count(dve, out_[k], 4 * (t - k))
                    link(dve.tensor_tensor(o[:, k, :], y2[:, k, :], x2[:, k, :], ALU.add))
                walk(dve, NT, 0, R, body)


_OUTS = [((NPAD, D), 'float32')]


def kernel(**inputs):
    import numpy as _np
    import concourse.bacc as _bacc
    from concourse import mybir as _mybir
    from concourse.bass_utils import run_bass_kernel_spmd as _run

    g = {k: _np.asarray(v) for k, v in inputs.items()}
    c = _np.ascontiguousarray
    edges = _np.full((2, EPAD), 0, _np.int32)
    edges[1, E:] = PAD_DST
    edges[0, :E] = g['src']
    edges[1, :E] = g['dst']
    xp = _np.zeros((NPAD, D), _np.float32)
    xp[:N] = g['x']
    ins = {
        'x': xp, 'edges': edges, 'gW': g['L0_gnn_W'], 'att_src': g['L0_gnn_att_src'],
        'att_dst': g['L0_gnn_att_dst'], 'gbias': g['L0_gnn_bias'], 'wqkvT': c(g['L0_mix_Wqkv'].T),
        'ln1g': g['L0_mix_ln1_g'], 'ln1b': g['L0_mix_ln1_b'], 'w1T': c(g['L0_mix_W1'].T), 'b1': g['L0_mix_b1'],
        'w2T': c(g['L0_mix_W2'].T), 'b2': g['L0_mix_b2'], 'ln2g': g['L0_mix_ln2_g'], 'ln2b': g['L0_mix_ln2_b'],
        'gate_w': g['L0_ffn_gate_w'], 'gate_b': g['L0_ffn_gate_b'], 'ew1': g['L0_ffn_w1'],
        'eb1': c(g['L0_ffn_b1'].reshape(X, 4, P).transpose(2, 0, 1).reshape(P, X * 4)), 'ew2': g['L0_ffn_w2'],
        'eb2': g['L0_ffn_b2'], 'gamma': g['L0_ffn_gamma'], 'beta': g['L0_ffn_beta'],
    }
    nc = _bacc.Bacc("TRN2", target_bir_lowering=False, num_devices=1)
    arrays, args = {}, []
    for name, a in ins.items():
        a = c(a)
        arrays[f"in_{name}_dram"] = a
        args.append(nc.dram_tensor(f"in_{name}_dram", a.shape, _mybir.dt.from_np(a.dtype), kind="ExternalInput").ap())
    for i, (shape, dtype) in enumerate(_OUTS):
        dt = _mybir.dt.from_np(_np.dtype(dtype))
        args.append(nc.dram_tensor(f"out_{i}_dram", shape, dt, kind="ExternalOutput").ap())
    gps_kernel(nc, *args)
    r = _run(nc, [arrays], core_ids=[0])
    return r.results[0]["out_0_dram"][:N]
```

```python
from contextlib import ExitStack

import concourse.bass as bass
from concourse import mybir

F32 = mybir.dt.float32
I32 = mybir.dt.int32
U32 = mybir.dt.uint32
ALU = mybir.AluOpType
ACT = mybir.ActivationFunctionType
AX = mybir.AxisListType

P = 128
N = 6250
D = 256
H = 8
C = D // H
CW = C + 1
ROW = H * CW
NT = -(-N // P)
NPAD = NT * P
E = 206250
J = 4
SE = J * P
STEPS = (E + NT * (SE - 1)) // SE
EPAD = E + SE
EC = -(-E // P)
PAD_DST = 1000000
X = 16
F = 512
XT = (2 * NPAD + X * (P - 1)) // P
NEG = -1.0e30
LN_EPS = 1e-5
RING = 8
QS = -(-STEPS // P)
STEPS_PAD = QS * P
DIAGS = 17


def walk(eng, count, lag, unroll, body, head=1):
    full = count // unroll - head
    for t in range(head * unroll):
        body(t, t % unroll, lambda l, t=t: 0 <= t - l < count)
    if full > 0:
        with eng.Fori(head, head + full) as u:
            for s in range(unroll):
                body(u * unroll + s, s, lambda l: True)
    for t in range((head + full) * unroll, count + lag):
        body(t, t % unroll, lambda l, t=t: 0 <= t - l < count)


def await_count(eng, sem, value, tick=None):
    if isinstance(value, int):
        if value > 0:
            eng.wait_ge(sem, value)
        return
    eng.wait_ge(sem, value)
    if tick is not None:
        eng.sem_inc(tick, 1)


def gps_kernel(nc, x, edges, gW, att_src, att_dst, gbias, wqkvT, ln1g, ln1b, w1T, b1, w2T, b2, ln2g, ln2b,
               gate_w, gate_b, ew1, eb1, ew2, eb2, gamma, beta, out):
    dram = lambda name, shape, dt=F32: nc.dram_tensor(name, shape, dt, kind="Internal").ap()
    table = dram("gather_table", (NPAD, ROW))
    xn_d = dram("xn_rows", (NPAD, D))
    x2_d = dram("x2_rows", (NPAD, D))
    slots_d = dram("slot_rows", (XT * P, D))
    eout_d = dram("expert_rows", (XT * P, D))

    with ExitStack() as whole:
        sb = lambda name, shape, dt=F32, ctx=whole: ctx.enter_context(nc.sbuf_tensor(name, shape, dt))
        sp_tick = whole.enter_context(nc.semaphore("sp_ticks"))
        dve_tick = whole.enter_context(nc.semaphore("dve_ticks"))
        act_tick = whole.enter_context(nc.semaphore("act_ticks"))
        pe_tick = whole.enter_context(nc.semaphore("pe_ticks"))
        pool_tick = whole.enter_context(nc.semaphore("pool_ticks"))
        ident = sb("ident", [P, P])
        mhalf = sb("mhalf", [P, 1])
        iota_n = sb("iota_n", [P, P])
        ones = sb("ones", [P, P])
        stepcol = sb("stepcol", [P, QS])
        bound = sb("bound", [P, NT])
        lower = sb("lower", [P, P])
        valid = sb("valid", [P, NT])
        adst = sb("adst", [P, NT, H])
        acc = sb("acc", [P, NT, ROW])
        kvb = sb("kvb", [P, 2, P + 4])
        top_v = sb("top_v", [P, NT, 2])
        top_i = sb("top_i", [P, NT, 2])
        slot = sb("slot", [P, NT, 2], I32)
        wtop = sb("wtop", [P, NT, 2])
        texp = sb("texp", [1, XT], I32)
        tile_f = sb("tile_f", [P, STEPS_PAD])
        reset = sb("reset", [P, STEPS_PAD])
        tile_i = sb("tile_i", [1, STEPS_PAD], I32)
        start_i = sb("start_i", [1, STEPS_PAD], I32)

        with ExitStack() as ctx:
            iota_i = sb("t_iota_i", [P, P], I32, ctx)
            stepcol_i = sb("t_stepcol_i", [P, QS], I32, ctx)
            bound_i = sb("t_bound_i", [P, NT], I32, ctx)
            made = ctx.enter_context(nc.semaphore("constants_made"))
            cast = ctx.enter_context(nc.semaphore("constants_cast"))
            block = ctx.enter_context(nc.Block())

            @block.gpsimd
            def _(pool):
                pool.memset(ident[:, :], 0.0).then_inc(made, 1)
                pool.memset(lower[:, :], 1.0).then_inc(made, 1)
                pool.memset(valid[:, :], 1.0).then_inc(made, 1)
                pool.memset(ones[:, :], 1.0).then_inc(made, 1)
                pool.memset(mhalf[:, :], -0.5).then_inc(made, 1)
                pool.iota(iota_i[:, :], [[1, P]], base=0, channel_multiplier=0).then_inc(made, 1)
                pool.iota(stepcol_i[:, :], [[P, QS]], base=0, channel_multiplier=1).then_inc(made, 1)
                pool.iota(bound_i[:, :], [[P, NT]], base=P, channel_multiplier=0).then_inc(made, 1)
                pool.wait_ge(made, 8)
                pool.affine_select(out=ident[:, :], in_=ident[:, :], compare_op=ALU.not_equal, fill=1.0,
                                   base=0, pattern=[[-1, P]], channel_multiplier=1).then_inc(made, 1)
                pool.affine_select(out=lower[:, :], in_=lower[:, :], compare_op=ALU.is_gt, fill=0.0,
                                   base=0, pattern=[[1, P]], channel_multiplier=-1).then_inc(made, 1)
                pool.affine_select(out=valid[:, :], in_=valid[:, :], compare_op=ALU.is_gt, fill=0.0,
                                   base=N, pattern=[[-P, NT]], channel_multiplier=-1).then_inc(made, 1)

            @block.vector
            def _(dve):
                dve.wait_ge(made, 8)
                dve.tensor_copy(iota_n[:, :], iota_i[:, :]).then_inc(cast, 1)
                dve.tensor_copy(stepcol[:, :], stepcol_i[:, :]).then_inc(cast, 1)
                dve.tensor_copy(bound[:, :], bound_i[:, :]).then_inc(cast, 1)

        with ExitStack() as ctx:
            s = lambda name, shape, dt=F32: sb("n_" + name, shape, dt, ctx)
            R = 4
            gw_sb = s("gw", [P, 2, D])
            wg = s("wg", [P, 2, ROW + H])
            prod = s("prod", [P, 2, D])
            attb = s("attb", [P, 2, D])
            wkv = s("wkv", [P, 2, 2 * D])
            xt = s("xt", [P, R, D])
            xn = s("xn", [P, R, D])
            xnT = s("xnT", [P, R, 2, P])
            st = s("st", [P, R, 6])
            mv = s("mv", [P, R, 2])
            ve = s("ve", [P, R, 1])
            rstd = s("rstd", [P, R, 1])
            rows = s("rows", [P, R, ROW])
            ek = s("ek", [P, R, D])
            rk = s("rk", [P, R, D])
            kf = s("kf", [P, R, D])
            vv = s("vv", [P, R, 2, P + 1])
            zero = s("zero", [P, P + 1])
            dst_i = s("dst_i", [P, EC], I32)
            dst_f = s("dst_f", [P, EC])
            less = s("less", [P, EC])
            part = s("part", [P, NT + 1])
            below = s("below", [P, NT + 1])
            cnt = s("cnt", [P, NT])
            cnt_i = s("cnt_i", [P, NT], I32)
            cumt = s("cumt", [P, NT])
            fst = s("fst", [P, NT])
            dfst = s("dfst", [P, NT])
            mask = s("mask", [P, QS, NT])
            tile_c = s("tile_c", [P, QS])
            offs_c = s("offs_c", [P, QS])
            diag = s("diag", [P, 2, QS, P])
            changed = s("changed", [P, STEPS_PAD])
            pT = ctx.enter_context(nc.psum_tensor("n_pT", [P, 2, 512], F32))
            pG = ctx.enter_context(nc.psum_tensor("n_pG", [P, 2, 512], F32))
            pK = ctx.enter_context(nc.psum_tensor("n_pK", [P, 2, 512], F32))
            pKV = ctx.enter_context(nc.psum_tensor("n_pKV", [P, 2, 512], F32))
            sem = lambda n: ctx.enter_context(nc.semaphore("n_" + n))
            w_in, dst_in = sem("weights_in"), sem("dst_in")
            x_in = [sem(f"x_in{k}") for k in range(R)]
            xn_out = [sem(f"xn_out{k}") for k in range(R)]
            row_out = [sem(f"row_out{k}") for k in range(R)]
            prep, norm, tr, trc = sem("weights_ready"), sem("norm"), sem("transposed"), sem("transposed_copied")
            proj, kproj = sem("projected"), sem("kv_projected")
            evac, kact, kdone, kvsum = sem("rows_ready"), sem("k_activated"), sem("k_ready"), sem("kv_summed")
            fin, rooted = sem("kv_copied"), sem("rooted")
            counted, chain, summed = sem("counted"), sem("schedule_ops"), sem("schedule_sums")
            block = ctx.enter_context(nc.Block())

            @block.gpsimd
            def _(pool):
                pool.memset(acc[:, :, :], 0.0).then_inc(fin, 1)

                def body(t, k, on):
                    await_count(pool, norm, 4 * t + 3)
                    pool.tensor_tensor(rstd[:, k, :], ve[:, k, :], mhalf[:, :], ALU.pow).then_inc(rooted, 1)
                walk(pool, NT, 0, R, body, head=2)

            @block.sync
            def _(sp):
                sp.dma_start(gw_sb[:, :, :], gW.rearrange("(k p) n -> p k n", p=P)).then_inc(w_in, 16)
                sp.dma_start(attb[:, 0, :], att_src.rearrange("h c -> (h c)").partition_broadcast(P)).then_inc(w_in, 16)
                sp.dma_start(attb[:, 1, :], att_dst.rearrange("h c -> (h c)").partition_broadcast(P)).then_inc(w_in, 16)
                sp.dma_start(wkv[:, :, :], wqkvT[:, D:3 * D].rearrange("(k p) n -> p k n", p=P)).then_inc(w_in, 16)
                sp.dma_start(dst_i[:, :], edges[1, 0:P * EC].rearrange("(p n) -> p n", p=P)).then_inc(dst_in, 16)

                def body(t, k, on):
                    if on(0):
                        await_count(sp, norm, 4 * (t - R) + 4, sp_tick)
                        sp.dma_start(xt[:, k, :], x[bass.ds(t * P, P), :]).then_inc(x_in[k], 16)
                    if on(1):
                        t1, k1 = t - 1, (k - 1) % R
                        await_count(sp, norm, 4 * t1 + 4, sp_tick)
                        sp.dma_start(xn_d[bass.ds(t1 * P, P), :], xn[:, k1, :]).then_inc(xn_out[k1], 16)
                    if on(2):
                        t2, k2 = t - 2, (k - 2) % R
                        await_count(sp, evac, 3 * t2 + 1, sp_tick)
                        sp.dma_start(table[bass.ds(t2 * P, P), :], rows[:, k2, :]).then_inc(row_out[k2], 16)
                walk(sp, NT, 2, R, body, head=2)
                for k in range(R):
                    sp.wait_ge(xn_out[k], 16 * ((NT + R - 1 - k) // R))
                    sp.wait_ge(row_out[k], 16 * ((NT + R - 1 - k) // R))

            @block.vector
            def _(dve):
                dve.memset(zero[:, :], 0.0).then_inc(prep, 1)
                dve.memset(part[:, :], 0.0).then_inc(counted, 1)
                dve.wait_ge(w_in, 64)
                for k in range(2):
                    dve.tensor_copy(wg[:, k, 0:ROW].rearrange("p (h c) -> p h c", h=H)[:, :, 0:C],
                                    gw_sb[:, k, :].rearrange("p (h c) -> p h c", h=H)).then_inc(prep, 1)
                n = 3
                for a in range(2):
                    for k in range(2):
                        dve.tensor_tensor(prod[:, k, :], gw_sb[:, k, :], attb[:, a, :], ALU.mult).then_inc(prep, 1)
                        n += 1
                        dve.wait_ge(prep, n)
                        o = (wg[:, k, 0:ROW].rearrange("p (h c) -> p h c", h=H)[:, :, C] if a == 0
                             else wg[:, k, ROW:ROW + H])
                        dve.tensor_reduce(o, prod[:, k, :].rearrange("p (h c) -> p h c", h=H), AX.X,
                                          ALU.add).then_inc(prep, 1)
                        n += 1
                        dve.wait_ge(prep, n)
                dve.wait_ge(dst_in, 16)
                dve.tensor_copy(dst_f[:, :], dst_i[:, :]).then_inc(counted, 1)
                dve.wait_ge(counted, 2)

                def body(t, k, on):
                    t2, k2 = t - 2, (k - 2) % R
                    if on(0):
                        await_count(dve, x_in[k], 4 * (t - k) + 16, dve_tick)
                        dve.bn_stats(st[:, k, :], xt[:, k, :]).then_inc(norm, 1)
                        await_count(dve, norm, 4 * t + 1, dve_tick)
                        dve.bn_aggr(mv[:, k, :], st[:, k, :]).then_inc(norm, 1)
                        await_count(dve, norm, 4 * t + 2)
                        dve.tensor_scalar(ve[:, k, :], mv[:, k, 1:2], LN_EPS, None, ALU.add).then_inc(norm, 1)
                    if on(2):
                        await_count(dve, kact, 3 * t2 + 2)
                        dve.scalar_tensor_tensor(kf[:, k2, :], ek[:, k2, :], 1.0, rk[:, k2, :], ALU.min,
                                                 ALU.add).then_inc(kdone, 1)
                    if on(0):
                        await_count(dve, rooted, t + 1)
                        await_count(dve, xn_out[k], 4 * (t - k))
                        await_count(dve, tr, t - R + 1)
                        dve.tensor_scalar(xn[:, k, :], xt[:, k, :], mv[:, k, 0:1], rstd[:, k, :],
                                          ALU.subtract, ALU.mult).then_inc(norm, 1)
                        await_count(dve, counted, t + 2, dve_tick)
                        dve.tensor_scalar(less[:, :], dst_f[:, :], bound[:, bass.ds(t, 1)], None, ALU.is_lt,
                                          ALU.add, accum_out=part[:, bass.ds(t + 1, 1)]).then_inc(counted, 1)
                walk(dve, NT, 2, R, body, head=2)
                done = [0]

                def link(ins):
                    done[0] += 1
                    ins.then_inc(chain, 1)
                    dve.wait_ge(chain, done[0])

                dve.wait_ge(summed, 1)
                link(dve.tensor_copy(below[:, :], pT[:, 0, 0:NT + 1]))
                link(dve.tensor_tensor(cnt[:, :], below[:, 1:NT + 1], below[:, 0:NT], ALU.subtract))
                link(dve.tensor_scalar(cnt_i[:, :], cnt[:, :], float(SE - 1), None, ALU.add))
                link(dve.tensor_scalar(cnt_i[:, :], cnt_i[:, :], SE.bit_length() - 1, None,
                                       ALU.logical_shift_right))
                link(dve.tensor_copy(cnt[:, :], cnt_i[:, :]))
                link(dve.tensor_tensor_scan(cumt[:, :], cnt[:, :], ones[:, 0:NT], 0.0, ALU.add, ALU.mult))
                link(dve.tensor_tensor(fst[:, :], cumt[:, :], cnt[:, :], ALU.subtract))
                link(dve.scalar_tensor_tensor(fst[:, :], fst[:, :], -float(SE), below[:, 0:NT], ALU.mult, ALU.add))
                link(dve.tensor_tensor(dfst[:, 0:NT - 1], fst[:, 1:NT], fst[:, 0:NT - 1], ALU.subtract))
                m = mask[:, :, 0:NT - 1]
                link(dve.tensor_tensor(m, stepcol[:, :].unsqueeze(2).to_broadcast([P, QS, NT - 1]),
                                       cumt[:, 0:NT - 1].unsqueeze(1).to_broadcast([P, QS, NT - 1]), ALU.is_ge))
                link(dve.tensor_reduce(tile_c[:, :], m, AX.X, ALU.add))
                link(dve.tensor_tensor(m, m, dfst[:, 0:NT - 1].unsqueeze(1).to_broadcast([P, QS, NT - 1]), ALU.mult))
                link(dve.tensor_reduce(offs_c[:, :], m, AX.X, ALU.add))
                link(dve.tensor_scalar(offs_c[:, :], offs_c[:, :], fst[:, 0:1], None, ALU.add))
                link(dve.scalar_tensor_tensor(offs_c[:, :], stepcol[:, :], float(SE), offs_c[:, :], ALU.mult, ALU.add))
                for i, col in enumerate((tile_c, offs_c)):
                    link(dve.tensor_tensor(diag[:, i, :, :], ident[:, :].unsqueeze(1).to_broadcast([P, QS, P]),
                                           col[:, :].unsqueeze(2).to_broadcast([P, QS, P]), ALU.mult))
                assert done[0] == DIAGS
                dve.wait_ge(summed, 3)
                link(dve.tensor_scalar(tile_f[:, :], pG[:, 0, 0:STEPS_PAD], float(P), None, ALU.mult))
                link(dve.tensor_copy(tile_i[:, :], pG[0:1, 0, 0:STEPS_PAD]))
                link(dve.tensor_scalar(start_i[:, :], pG[0:1, 1, 0:STEPS_PAD], float(E), None, ALU.min))
                link(dve.memset(reset[:, :], NEG))
                link(dve.tensor_tensor(changed[:, 1:STEPS_PAD], tile_f[:, 1:STEPS_PAD], tile_f[:, 0:STEPS_PAD - 1],
                                       ALU.not_equal))
                link(dve.tensor_scalar(reset[:, 1:STEPS_PAD], changed[:, 1:STEPS_PAD], NEG, None, ALU.mult))
                dve.memset(kvb[:, :, :], 0.0).then_inc(fin, 1)
                dve.wait_ge(fin, 2)
                dve.wait_ge(kvsum, NT + 2)
                for c in range(2):
                    for h in range(4):
                        q = slice(C * h, C * h + C)
                        dve.tensor_copy(kvb[q, c, q], pKV[q, c, q]).then_inc(fin, 1)
                        dve.tensor_copy(kvb[q, c, P + h:P + h + 1], pKV[q, c, P:P + 1]).then_inc(fin, 1)

            @block.tensor
            def _(pe):
                pe.wait_ge(prep, 11)
                for c in range(2):
                    pe.matmul(pKV[:, c, 0:P + 1], zero[:, 0:P], zero[:, :], start=True, stop=False,
                              skip_group_check=True)

                def body(t, k, on):
                    w = lambda sem, v: await_count(pe, sem, v, pe_tick)
                    t1, k1 = t - 1, (k - 1) % R
                    t2, k2 = t - 2, (k - 2) % R
                    if on(0):
                        w(norm, 4 * t + 4)
                        w(trc, t - 1)
                        for c in range(2):
                            last = pe.transpose(pT[:, k % 2, P * c:P * c + P], xn[:, k, P * c:P * c + P],
                                                ident[:, :])
                        last.then_inc(tr, 1)
                    if on(1):
                        w(trc, t1 + 1)
                        w(evac, 3 * (t1 - 2) + 2)
                        for c in range(2):
                            last = pe.matmul(pG[:, k1 % 2, 0:ROW + H], xnT[:, k1, c, :], wg[:, c, :],
                                             start=(c == 0), stop=(c == 1))
                        last.then_inc(proj, 1)
                        w(kact, 3 * (t1 - 2) + 3)
                        for c in range(2):
                            last = pe.matmul(pK[:, k1 % 2, :], xnT[:, k1, c, :], wkv[:, c, :], start=(c == 0),
                                             stop=(c == 1))
                        last.then_inc(kproj, 1)
                    if on(2):
                        w(kdone, t2 + 1)
                        w(kact, 3 * t2 + 3)
                        w(evac, 3 * t2 + 3)
                        for c in range(2):
                            last = pe.matmul(pKV[:, c, 0:P + 1], kf[:, k2, P * c:P * c + P], vv[:, k2, c, :],
                                             start=False, stop=False, skip_group_check=True)
                        last.then_inc(kvsum, 1)
                walk(pe, NT, 2, R, body, head=2)
                for c in range(2):
                    pe.matmul(pKV[:, c, 0:P + 1], zero[:, 0:P], zero[:, :], start=False, stop=True,
                              skip_group_check=True).then_inc(kvsum, 1)
                pe.wait_ge(counted, NT + 2)
                pe.wait_ge(trc, NT)
                pe.matmul(pT[:, 0, 0:NT + 1], ones[:, :], part[:, :], start=True, stop=True).then_inc(summed, 1)
                pe.wait_ge(chain, DIAGS)
                pe.wait_ge(evac, 3 * NT)
                for i in range(2):
                    pe.matmul(pG[:, i, 0:STEPS_PAD], ones[:, :], diag[:, i, :, :].rearrange("p q n -> p (q n)"),
                              start=True, stop=True).then_inc(summed, 1)

            @block.scalar
            def _(act):
                def body(t, k, on):
                    t1, k1 = t - 1, (k - 1) % R
                    if on(0):
                        await_count(act, tr, t + 1)
                        await_count(act, kproj, t - R + 1)
                        act.activation(xnT[:, k, :, :].rearrange("p c n -> p (c n)"), pT[:, k % 2, 0:2 * P],
                                       ACT.Copy).then_inc(trc, 1)
                    if on(1):
                        await_count(act, proj, t1 + 1)
                        await_count(act, row_out[k1], 4 * (t1 - k1))
                        act.activation(rows[:, k1, :], pG[:, k1 % 2, 0:ROW], ACT.Copy).then_inc(evac, 1)
                        act.activation(adst[:, bass.ds(t1, 1), :], pG[:, k1 % 2, ROW:ROW + H].unsqueeze(1),
                                       ACT.Copy).then_inc(evac, 1)
                        await_count(act, kproj, t1 + 1)
                        await_count(act, kdone, t1 - R + 1)
                        act.activation(ek[:, k1, :], pK[:, k1 % 2, 0:D], ACT.Exp).then_inc(kact, 1)
                        act.activation(rk[:, k1, :], pK[:, k1 % 2, 0:D], ACT.Relu).then_inc(kact, 1)
                        await_count(act, kvsum, t1 - R + 1)
                        act.activation(vv[:, k1, :, 0:P], pK[:, k1 % 2, D:2 * D].rearrange("p (c n) -> p c n", c=2),
                                       ACT.Copy).then_inc(kact, 1)
                        act.activation(vv[:, k1, :, P], valid[:, bass.ds(t1, 1)].to_broadcast([P, 2]),
                                       ACT.Copy).then_inc(evac, 1)
                walk(act, NT, 1, R, body, head=2)
                act.wait_ge(evac, 3 * NT)

        with ExitStack() as ctx:
            s = lambda name, shape, dt=F32: sb("e_" + name, shape, dt, ctx)
            pair = s("pair", [P, RING, 2, J], I32)
            gat = [s(f"gat{k}", [P, J, ROW]) for k in range(RING)]
            dloc = s("dloc", [P, RING, J])
            hot = s("hot", [P, RING, J, P])
            hotT = s("hotT", [P, RING, J, P])
            dsc = s("dsc", [P, RING, J, H])
            drow = s("drow", [J * H, RING, P])
            diff = s("diff", [J * H, RING, P + 1])
            smax = s("smax", [J * H, RING, P])
            lmax = s("lmax", [J * H, RING, P])
            zb = s("zb", [P, RING, J, H + 1])
            big = s("big", [P, 1])
            pen = s("pen", [P, RING, J])
            mc4 = s("mc4", [P, RING, J, H])
            mc = s("mc", [P, RING, H])
            uc = s("uc", [P, RING, H])
            lc = s("lc", [P, RING, H])
            dd = s("dd", [P, RING, 2 * H])
            dr = s("dr", [P, RING, H])
            rr = s("rr", [P, RING, H])
            ze = s("ze", [P, RING, J, H])
            le = s("le", [P, RING, J, H])
            se = s("se", [P, RING, J, H])
            sc = s("sc", [P, RING, J, H])
            AR = 4
            accb = s("accb", [P, AR, ROW])
            pX = ctx.enter_context(nc.psum_tensor("e_pX", [P, 2, 512], F32))
            pH = ctx.enter_context(nc.psum_tensor("e_pH", [P, 512], F32))
            pL = ctx.enter_context(nc.psum_tensor("e_pL", [P, 512], F32))
            pM = ctx.enter_context(nc.psum_tensor("e_pM", [P, 512], F32))
            pD = ctx.enter_context(nc.psum_tensor("e_pD", [P, 512], F32))
            pA = ctx.enter_context(nc.psum_tensor("e_pA", [P, 2, 512], F32))
            sem = lambda n: ctx.enter_context(nc.semaphore("e_" + n))
            pair_in = [sem(f"pair_in{k}") for k in range(RING)]
            rows_in = [sem(f"rows_in{k}") for k in range(RING)]
            init, absent, scored, stored = sem("init"), sem("absent"), sem("node_scores"), sem("sums_stored")
            local, scan, upd, shift, msg, accum = (sem("one_hot"), sem("segment_max"), sem("max_updated"),
                                                   sem("shifted"), sem("messages"), sem("accumulated"))
            dscaled, rowcopy, lastcopy, factor, expd = (sem("dst_scaled"), sem("rows_copied"), sem("last_copied"),
                                                        sem("rescale_factor"), sem("exponentials"))
            turned, lastT, tomax, expand, agg = (sem("turned"), sem("last_turned"), sem("chunk_max"),
                                                 sem("expanded"), sem("aggregated"))
            block = ctx.enter_context(nc.Block())
            UPD = 6

            @block.sync
            def _(sp):
                def body(t, k, on):
                    start = sp.value_load(start_i[0:1, bass.ds(t, 1)], min_val=0, max_val=E)
                    await_count(sp, local, 2 * (t - RING) + 1, sp_tick)
                    await_count(sp, rows_in[k], 8 * (t - k - RING) + 64, sp_tick)
                    sp.dma_start(pair[:, k, :, :],
                                 edges[:, bass.ds(start, SE)].rearrange("a (p j) -> p a j", p=P)).then_inc(pair_in[k], 16)
                walk(sp, STEPS, 0, RING, body)

            @block.gpsimd
            def _(pool):
                def body(t, k, on):
                    await_count(pool, pair_in[k], 2 * (t - k) + 16, pool_tick)
                    await_count(pool, agg, t - RING + 1, pool_tick)
                    for j in range(J):
                        pool.indirect_dma_start(gat[k][:, j, :], None, table,
                                                bass.IndirectOffsetOnAxis(pair[:, k, 0, j:j + 1], 0)
                                                ).then_inc(rows_in[k], 16)
                walk(pool, STEPS, 0, RING, body)
                for k in range(RING):
                    pool.wait_ge(rows_in[k], 64 * ((STEPS + RING - 1 - k) // RING))

            def heads(k):
                return gat[k][:, :, :].rearrange("p j (h c) -> p j h c", h=H)

            @block.vector
            def _(dve):
                dve.memset(diff[:, :, :], -1.0e25).then_inc(init, 1)
                dve.memset(zb[:, :, :, :], 1.0).then_inc(init, 1)
                dve.memset(dd[:, :, :], NEG).then_inc(init, 1)
                dve.memset(accb[:, :, :], 0.0).then_inc(init, 1)
                dve.memset(big[:, :], -NEG).then_inc(init, 1)
                dve.wait_ge(init, 5)

                pm = pM[:, 0:J * (H + 1)].rearrange("p (j h) -> p j h", j=J)
                pd = pD[:, 0:J * 2 * H].rearrange("p (j h) -> p j h", j=J)
                per_head = lambda ap: ap.rearrange("p (h c) -> p h c", h=H)

                def body(t, k, on):
                    t1, k1 = t - 1, (k - 1) % RING
                    t3, k3 = t - 3, (k - 3) % RING
                    t4, k4 = t - 4, (k - 4) % RING
                    t7, k7 = t - 7, (k - 7) % RING
                    if on(4):
                        await_count(dve, expand, t4 + 1)
                        dve.tensor_tensor(ze[:, k4, :, :], heads(k4)[:, :, :, C], pd[:, :, 0:H],
                                          ALU.add).then_inc(shift, 1)
                    if on(0):
                        await_count(dve, pair_in[k], 2 * (t - k) + 16)
                        await_count(dve, agg, t - RING + 1)
                        dve.tensor_scalar(dloc[:, k, :], pair[:, k, 1, :], tile_f[:, bass.ds(t, 1)], None,
                                          ALU.subtract).then_inc(local, 1)
                    if on(4):
                        await_count(dve, shift, 3 * t4 + 1)
                        dve.scalar_tensor_tensor(le[:, k4, :, :], ze[:, k4, :, :], 0.2, ze[:, k4, :, :], ALU.mult,
                                                 ALU.max).then_inc(shift, 1)
                    if on(3):
                        await_count(dve, absent, t3 + 1)
                        dve.tensor_tensor(mc4[:, k3, :, :], pm[:, :, 0:H],
                                          pen[:, k3, :].unsqueeze(2).to_broadcast([P, J, H]),
                                          ALU.subtract).then_inc(upd, 1)
                    if on(4):
                        await_count(dve, shift, 3 * t4 + 2)
                        dve.tensor_tensor(se[:, k4, :, :], le[:, k4, :, :], pd[:, :, H:2 * H],
                                          ALU.subtract).then_inc(shift, 1)
                    if on(3):
                        await_count(dve, upd, UPD * t3 + 1)
                        dve.tensor_reduce(mc[:, k3, :], mc4[:, k3, :, :].rearrange("p j h -> p h j"), AX.X,
                                          ALU.max).then_inc(upd, 1)
                    if on(0):
                        await_count(dve, local, 2 * t + 1)
                        dve.tensor_tensor(hot[:, k, :, :], iota_n[:, :].unsqueeze(1).to_broadcast([P, J, P]),
                                          dloc[:, k, :].unsqueeze(2).to_broadcast([P, J, P]),
                                          ALU.is_equal).then_inc(local, 1)
                    if on(3):
                        await_count(dve, upd, UPD * t3 + 2)
                        await_count(dve, scored, t3 + 1)
                        dve.tensor_tensor(uc[:, k3, :], mc[:, k3, :], dd[:, k3, 0:H], ALU.add).then_inc(upd, 1)
                    if on(1):
                        await_count(dve, rowcopy, 2 * t1 + 1)
                        dve.tensor_tensor(diff[:, k1, 1:P], drow[:, k1, 0:P - 1], drow[:, k1, 1:P],
                                          ALU.subtract).then_inc(scan, 1)
                    if on(3):
                        await_count(dve, upd, UPD * t3 + 3)
                        dve.scalar_tensor_tensor(lc[:, k3, :], uc[:, k3, :], 0.2, uc[:, k3, :], ALU.mult,
                                                 ALU.max).then_inc(upd, 1)
                    if on(1):
                        await_count(dve, scan, 3 * t1 + 1)
                        dve.tensor_tensor_scan(smax[:, k1, :], diff[:, k1, 0:P], pX[0:J * H, k1 % 2, 0:P], 0.0,
                                               ALU.add, ALU.max).then_inc(scan, 1)
                    if on(3):
                        await_count(dve, upd, UPD * t3 + 4)
                        dve.scalar_tensor_tensor(dd[:, k3, H:2 * H], dd[:, (k3 - 1) % RING, H:2 * H],
                                                 reset[:, bass.ds(t3, 1)], lc[:, k3, :], ALU.add,
                                                 ALU.max).then_inc(upd, 1)
                    if on(7):
                        await_count(dve, accum, 2 * t7)
                        await_count(dve, factor, t7 + 1)
                        await_count(dve, stored, t7 - AR + 1)
                        a = accb[:, k7 % AR, :]
                        dve.tensor_tensor(per_head(a), per_head(accb[:, (k7 - 1) % AR, :]),
                                          rr[:, k7, :].unsqueeze(2).to_broadcast([P, H, CW]),
                                          ALU.mult).then_inc(accum, 1)
                    if on(3):
                        await_count(dve, upd, UPD * t3 + 5)
                        dve.scalar_tensor_tensor(dr[:, k3, :], dd[:, (k3 - 1) % RING, H:2 * H],
                                                 reset[:, bass.ds(t3, 1)], dd[:, k3, H:2 * H], ALU.add,
                                                 ALU.subtract).then_inc(upd, 1)
                    if on(1):
                        await_count(dve, scan, 3 * t1 + 2)
                        dve.scalar_tensor_tensor(lmax[:, k1, :], diff[:, k1, 1:P + 1], 0.0, smax[:, k1, :],
                                                 ALU.is_lt, ALU.mult).then_inc(scan, 1)
                    if on(4):
                        await_count(dve, expd, 2 * t4 + 2)
                        g = heads(k4)
                        dve.tensor_tensor(g[:, :, :, 0:C], g[:, :, :, 0:C],
                                          g[:, :, :, C:CW].to_broadcast([P, J, H, C]), ALU.mult).then_inc(msg, 1)
                    if on(7):
                        await_count(dve, accum, 2 * t7 + 1)
                        await_count(dve, agg, t7 + 1)
                        dve.tensor_tensor(a, a, pA[:, k7 % 2, 0:ROW], ALU.add).then_inc(accum, 1)
                walk(dve, STEPS, 7, RING, body, head=2)

            @block.scalar
            def _(act):
                def body(t, k, on):
                    t1, k1 = t - 1, (k - 1) % RING
                    t2, k2 = t - 2, (k - 2) % RING
                    t3, k3 = t - 3, (k - 3) % RING
                    t4, k4 = t - 4, (k - 4) % RING
                    if on(0):
                        await_count(act, local, 2 * t + 1)
                        act.activation(dsc[:, k, :, :], dloc[:, k, :].unsqueeze(2).to_broadcast([P, J, H]),
                                       ACT.Copy, scale=1.0e25).then_inc(dscaled, 1)
                    if on(4):
                        await_count(act, shift, 3 * t4 + 3)
                        act.activation(sc[:, k4, :, :], se[:, k4, :, :], ACT.Relu, scale=-1.0).then_inc(expd, 1)
                        await_count(act, expd, 2 * t4 + 1)
                        act.activation(heads(k4)[:, :, :, C], sc[:, k4, :, :], ACT.Exp, scale=-1.0).then_inc(expd, 1)
                    if on(3):
                        await_count(act, upd, UPD * t3 + 6)
                        act.activation(rr[:, k3, :], dr[:, k3, :], ACT.Exp).then_inc(factor, 1)
                    if on(0):
                        await_count(act, turned, 2 * t + 1)
                        act.activation(drow[:, k, :], pX[0:J * H, k % 2, P:2 * P], ACT.Copy).then_inc(rowcopy, 1)
                        await_count(act, turned, 2 * t + 2)
                        act.activation(hotT[:, k, :, :].rearrange("p j n -> p (j n)"), pH[:, :],
                                       ACT.Copy).then_inc(rowcopy, 1)
                    if on(2):
                        await_count(act, tomax, t2 + 1)
                        act.activation(pen[:, k2, :], pM[:, 0:J * (H + 1)].rearrange("p (j h) -> p j h", j=J)[:, :, H],
                                       ACT.Relu, scale=NEG, bias=big[:, :]).then_inc(absent, 1)
                    if on(1):
                        await_count(act, lastT, t1 + 1)
                        act.activation(zb[:, k1, :, 0:H], pL[:, 0:J * H].rearrange("p (j h) -> p j h", j=J),
                                       ACT.Copy).then_inc(lastcopy, 1)
                    if on(2):
                        i2 = act.value_load(tile_i[0:1, bass.ds(t2, 1)], min_val=0, max_val=NT - 1)
                        act.activation(dd[:, k2, 0:H], adst[:, bass.ds(i2, 1), :].rearrange("p a h -> p (a h)"),
                                       ACT.Copy).then_inc(scored, 1)
                    if on(8):
                        t8 = t - 8
                        i8 = act.value_load(tile_i[0:1, bass.ds(t8, 1)], min_val=0, max_val=NT - 1)
                        await_count(act, stored, t8, act_tick)
                        await_count(act, accum, 2 * t8 + 2, act_tick)
                        act.activation(acc[:, bass.ds(i8, 1), :].rearrange("p a n -> p (a n)"),
                                       accb[:, k % AR, :], ACT.Copy).then_inc(stored, 1)
                act.wait_ge(init, 5)
                walk(act, STEPS, 8, RING, body, head=2)
                act.wait_ge(stored, STEPS)

            @block.tensor
            def _(pe):
                def turn(t, k):
                    await_count(pe, pair_in[k], 2 * (t - k) + 16, pe_tick)
                    await_count(pe, rows_in[k], 8 * (t - k) + 64, pe_tick)
                    await_count(pe, dscaled, t + 1, pe_tick)
                    await_count(pe, scan, 3 * (t - 2) + 2, pe_tick)
                    pe.transpose(pX[0:J * H, k % 2, 0:P], heads(k)[:, :, :, C], ident[:, :])
                    pe.transpose(pX[0:J * H, k % 2, P:2 * P], dsc[:, k, :, :].rearrange("p j h -> p (j h)"),
                                 ident[:, :]).then_inc(turned, 1)
                    await_count(pe, local, 2 * t + 2, pe_tick)
                    await_count(pe, rowcopy, 2 * (t - 1) + 2, pe_tick)
                    for j in range(J):
                        last = pe.transpose(pH[:, P * j:P * j + P], hot[:, k, j, :], ident[:, :])
                    last.then_inc(turned, 1)

                def turn_last(t, k):
                    await_count(pe, scan, 3 * t + 3, pe_tick)
                    await_count(pe, lastcopy, t, pe_tick)
                    pe.transpose(pL[:, 0:J * H], lmax[:, k, :], ident[0:J * H, 0:J * H]).then_inc(lastT, 1)

                def chunk_max(t, k):
                    await_count(pe, lastcopy, t + 1, pe_tick)
                    await_count(pe, upd, UPD * (t - 1) + 1, pe_tick)
                    for j in range(J):
                        o = j * (H + 1)
                        last = pe.matmul(pM[:, o:o + H + 1], hot[:, k, j, :], zb[:, k, j, :], start=True,
                                         stop=True)
                    last.then_inc(tomax, 1)

                def expand_nodes(t, k):
                    await_count(pe, scored, t + 1, pe_tick)
                    await_count(pe, upd, UPD * t + 5, pe_tick)
                    await_count(pe, rowcopy, 2 * t + 2, pe_tick)
                    await_count(pe, shift, 3 * (t - 1) + 3, pe_tick)
                    for j in range(J):
                        o = j * 2 * H
                        last = pe.matmul(pD[:, o:o + 2 * H], hotT[:, k, j, :], dd[:, k, :], start=True,
                                         stop=True)
                    last.then_inc(expand, 1)

                def aggregate(t, k):
                    await_count(pe, msg, t + 1, pe_tick)
                    await_count(pe, accum, 2 * (t - 2) + 2, pe_tick)
                    for j in range(J):
                        last = pe.matmul(pA[:, k % 2, 0:ROW], hot[:, k, j, :], gat[k][:, j, :], start=(j == 0),
                                         stop=(j == J - 1))
                    last.then_inc(agg, 1)

                def body(t, k, on):
                    if on(6):
                        aggregate(t - 6, (k - 6) % RING)
                    if on(2):
                        chunk_max(t - 2, (k - 2) % RING)
                    if on(0):
                        turn(t, k)
                    if on(3):
                        expand_nodes(t - 3, (k - 3) % RING)
                    if on(1):
                        turn_last(t - 1, (k - 1) % RING)
                walk(pe, STEPS, 6, RING, body)

        with ExitStack() as ctx:
            s = lambda name, shape, dt=F32: sb("m_" + name, shape, dt, ctx)
            R = 4
            wq = s("wq", [P, 2, D])
            w1 = s("w1", [P, 2, D])
            w2 = s("w2", [P, 2, D])
            wgate = s("wgate", [P, 2, X])
            b1c = s("b1c", [P, 2])
            VEC = {n: s(n, [P, D]) for n in ("ln1g", "ln1b", "ln2g", "ln2b", "b2", "gbias")}
            gateb = s("gateb", [P, X])
            eps = s("eps", [P, 1])
            xt, xn, tt, x1p, x1c, x1, gnn, nb, x1b, yb, yc, yn, x2, x3 = (
                s(n, [P, R, D]) for n in ("xt", "xn", "tt", "x1p", "x1c", "x1", "gnn", "nb", "x1b", "yb", "yc",
                                          "yn", "x2", "x3"))
            xnT, eq, rq, qf, x1T, hT, x3T = (
                s(n, [P, R, 2, P]) for n in ("xnT", "eq", "rq", "qf", "x1T", "hT", "x3T"))
            den, zi, gden, gzi = (s(n, [P, R, H]) for n in ("den", "zi", "gden", "gzi"))
            st, mv, ve, rstd = ([s(f"{n}{i}", [P, R, w]) for i in range(3)]
                                for n, w in (("st", 6), ("mv", 2), ("ve", 1), ("rstd", 1)))
            lg = s("lg", [P, R, X])
            v8 = s("v8", [P, R, 8])
            i8 = s("i8", [P, R, 8], U32)
            zeros = s("zeros", [P, D])
            ps = ctx.enter_context(nc.psum_tensor("m_ps", [P, 8, 512], F32))
            p_xT, p_q, p_att, p_x1T, p_h, p_y, p_x3T, p_lg = (ps[:, b, :] for b in range(8))
            sem = lambda n: ctx.enter_context(nc.semaphore("m_" + n))
            w_in = sem("weights_in")
            x_in = [sem(f"x_in{k}") for k in range(R)]
            x2_out = [sem(f"x2_out{k}") for k in range(R)]
            zeroed, slots_zero, eps_set = sem("zeroed"), sem("slots_zeroed"), sem("eps_set")
            turned, qprod, attprod, x1turned, hprod, yprod, x3turned, gateprod = (
                sem(n) for n in ("xn_turned", "q_product", "attention_product", "x1_turned", "hidden_product",
                                 "mlp_product", "x3_turned", "gate_product"))
            xT_ready, q_act, x1T_ready, gelu, x3T_ready, kept = (
                sem(n) for n in ("xnT_ready", "q_activated", "x1T_ready", "gelu", "x3T_ready", "x3_kept"))
            qfs, att, aff, gat, mlp, res, nrm, top = (
                sem(n) for n in ("q_features", "attention", "x1_affine", "gat_part", "mlp_sum", "residual",
                                 "x3_normalised", "top2"))
            ATT, AFF, GAT, MLP, RES, TOP = 6, 3, 5, 3, 5, 5
            eps_added, rooted = [sem(f"eps_added{i}") for i in range(3)], [sem(f"rooted{i}") for i in range(3)]
            block = ctx.enter_context(nc.Block())

            @block.gpsimd
            def _(pool):
                pool.memset(eps[:, :], LN_EPS).then_inc(eps_set, 1)
                pool.wait_ge(eps_set, 1)

                def body(t, k, on):
                    for i, lag, stats, per in ((1, 3, mlp, MLP), (2, 4, res, RES), (0, 1, att, ATT)):
                        if on(lag):
                            q = (k - lag) % R
                            await_count(pool, stats, per * (t - lag) + per)
                            pool.tensor_tensor(ve[i][:, q, :], mv[i][:, q, 1:2], eps[:, :], ALU.add
                                               ).then_inc(eps_added[i], 1)
                            await_count(pool, eps_added[i], t - lag + 1)
                            pool.tensor_tensor(rstd[i][:, q, :], ve[i][:, q, :], mhalf[:, :], ALU.pow
                                               ).then_inc(rooted[i], 1)
                walk(pool, NT, 4, R, body, head=3)

            @block.sync
            def _(sp):
                for dst, src in ((wq, wqkvT[:, 0:D]), (w1, w1T), (w2, w2T), (wgate, gate_w)):
                    sp.dma_start(dst[:, :, :], src.rearrange("(k p) n -> p k n", p=P)).then_inc(w_in, 16)
                with nc.allow_non_contiguous_dma(reason="a bias of 256 floats, once"):
                    sp.dma_start(b1c[:, :], b1.rearrange("(k p) -> p k", p=P)).then_inc(w_in, 16)
                for n, v in (("ln1g", ln1g), ("ln1b", ln1b), ("ln2g", ln2g), ("ln2b", ln2b), ("b2", b2),
                             ("gbias", gbias)):
                    sp.dma_start(VEC[n][:, :], v.partition_broadcast(P)).then_inc(w_in, 16)
                sp.dma_start(gateb[:, :], gate_b.partition_broadcast(P)).then_inc(w_in, 16)
                sp.wait_ge(zeroed, 1)
                sp.dma_start(slots_d.rearrange("(t p) n -> p t n", p=P),
                             zeros[:, :].unsqueeze(1).to_broadcast([P, XT, D])).then_inc(slots_zero, 16)

                def body(t, k, on):
                    if on(0):
                        await_count(sp, gat, GAT * (t - R) + GAT, sp_tick)
                        sp.dma_start(xt[:, k, :], x[bass.ds(t * P, P), :]).then_inc(x_in[k], 16)
                        sp.dma_start(xn[:, k, :], xn_d[bass.ds(t * P, P), :]).then_inc(x_in[k], 16)
                    if on(5):
                        t5, k5 = t - 5, (k - 5) % R
                        await_count(sp, res, RES * t5 + 3, sp_tick)
                        sp.dma_start(x2_d[bass.ds(t5 * P, P), :], x2[:, k5, :]).then_inc(x2_out[k5], 16)
                walk(sp, NT, 5, R, body, head=3)
                for k in range(R):
                    sp.wait_ge(x2_out[k], 16 * ((NT + R - 1 - k) // R))
                sp.wait_ge(slots_zero, 16)

            @block.vector
            def _(dve):
                dve.memset(zeros[:, :], 0.0).then_inc(zeroed, 1)
                dve.wait_ge(w_in, 16 * 12)
                hd = lambda ap: ap.rearrange("p (h c) -> p h c", h=H)
                halves = lambda ap: ap.rearrange("p (c h) -> p c h", c=2)
                p_at = p_att[:, 0:2 * (P + 4)].rearrange("p (c n) -> p c n", c=2)

                def body(t, k, on):
                    t1, k1 = t - 1, (k - 1) % R
                    t2, k2 = t - 2, (k - 2) % R
                    t3, k3 = t - 3, (k - 3) % R
                    t4, k4 = t - 4, (k - 4) % R
                    t5, k5 = t - 5, (k - 5) % R
                    t6, k6 = t - 6, (k - 6) % R
                    if on(2):
                        a = acc[:, bass.ds(t2, 1), :].rearrange("p a n -> p (a n)")
                    two = lambda tab: tab[:, bass.ds(t6, 1), :].rearrange("p a n -> p (a n)")
                    if on(5):
                        await_count(dve, rooted[2], t5 + 1)
                        dve.tensor_scalar(x3[:, k5, :], x2[:, k5, :], mv[2][:, k5, 0:1], rstd[2][:, k5, :],
                                          ALU.subtract, ALU.mult).then_inc(nrm, 1)
                    if on(3):
                        await_count(dve, aff, AFF * t3 + 3)
                        await_count(dve, yprod, t3 + 1)
                        dve.tensor_tensor(yb[:, k3, :], p_y[:, 0:D], x1b[:, k3, :], ALU.add).then_inc(mlp, 1)
                    if on(6):
                        await_count(dve, gateprod, t6 + 1)
                        dve.tensor_tensor(lg[:, k6, :], p_lg[:, 0:X], gateb[:, :], ALU.add).then_inc(top, 1)
                    if on(4):
                        await_count(dve, rooted[1], t4 + 1)
                        dve.scalar_tensor_tensor(yc[:, k4, :], yb[:, k4, :], mv[1][:, k4, 0:1], VEC["ln2g"][:, :],
                                                 ALU.subtract, ALU.mult).then_inc(res, 1)
                    if on(3):
                        await_count(dve, mlp, MLP * t3 + 1, dve_tick)
                        dve.bn_stats(st[1][:, k3, :], yb[:, k3, :]).then_inc(mlp, 1)
                    if on(2):
                        await_count(dve, rooted[0], t2 + 1)
                        dve.scalar_tensor_tensor(x1c[:, k2, :], x1p[:, k2, :], mv[0][:, k2, 0:1], VEC["ln1g"][:, :],
                                                 ALU.subtract, ALU.mult).then_inc(aff, 1)
                    if on(6):
                        await_count(dve, top, TOP * t6 + 1, dve_tick)
                        dve.max(v8[:, k6, :], lg[:, k6, :]).then_inc(top, 1)
                    if on(4):
                        await_count(dve, res, RES * t4 + 1)
                        dve.scalar_tensor_tensor(yn[:, k4, :], yc[:, k4, :], rstd[1][:, k4, :], VEC["ln2b"][:, :],
                                                 ALU.mult, ALU.add).then_inc(res, 1)
                    if on(3):
                        await_count(dve, mlp, MLP * t3 + 2, dve_tick)
                        dve.bn_aggr(mv[1][:, k3, :], st[1][:, k3, :]).then_inc(mlp, 1)
                    if on(2):
                        await_count(dve, aff, AFF * t2 + 1)
                        dve.scalar_tensor_tensor(x1[:, k2, :], x1c[:, k2, :], rstd[0][:, k2, :], VEC["ln1b"][:, :],
                                                 ALU.mult, ALU.add).then_inc(aff, 1)
                    if on(6):
                        await_count(dve, top, TOP * t6 + 2, dve_tick)
                        dve.max_index(i8[:, k6, :], v8[:, k6, :], lg[:, k6, :]).then_inc(top, 1)
                    if on(1):
                        await_count(dve, attprod, t1 + 1)
                        dve.tensor_scalar(halves(den[:, k1, :]), p_at[:, :, P:P + 4], 1e-6, None,
                                          ALU.add).then_inc(att, 1)
                    if on(4):
                        await_count(dve, res, RES * t4 + 2)
                        await_count(dve, gat, GAT * t4 + 5)
                        await_count(dve, x2_out[k4], 4 * (t4 - k4))
                        dve.tensor_tensor(x2[:, k4, :], nb[:, k4, :], yn[:, k4, :], ALU.add).then_inc(res, 1)
                    if on(2):
                        dve.tensor_scalar(gden[:, k2, :], hd(a)[:, :, C], 1e-16, None, ALU.add).then_inc(gat, 1)
                    if on(1):
                        await_count(dve, att, ATT * t1 + 1)
                        dve.reciprocal(zi[:, k1, :], den[:, k1, :]).then_inc(att, 1)
                    if on(4):
                        await_count(dve, res, RES * t4 + 3, dve_tick)
                        dve.bn_stats(st[2][:, k4, :], x2[:, k4, :]).then_inc(res, 1)
                    if on(2):
                        await_count(dve, gat, GAT * t2 + 1)
                        dve.reciprocal(gzi[:, k2, :], gden[:, k2, :]).then_inc(gat, 1)
                    if on(1):
                        await_count(dve, att, ATT * t1 + 2)
                        dve.tensor_tensor(tt[:, k1, :].rearrange("p (c h n) -> p c h n", c=2, h=4),
                                          p_at[:, :, 0:P].rearrange("p c (h n) -> p c h n", h=4),
                                          halves(zi[:, k1, :]).unsqueeze(3).to_broadcast([P, 2, 4, C]),
                                          ALU.mult).then_inc(att, 1)
                    if on(4):
                        await_count(dve, res, RES * t4 + 4, dve_tick)
                        dve.bn_aggr(mv[2][:, k4, :], st[2][:, k4, :]).then_inc(res, 1)
                    if on(2):
                        await_count(dve, gat, GAT * t2 + 2, dve_tick)
                        dve.tensor_tensor(hd(gnn[:, k2, :]), hd(a)[:, :, 0:C],
                                          gzi[:, k2, :].unsqueeze(2).to_broadcast([P, H, C]),
                                          ALU.mult).then_inc(gat, 1)
                    if on(1):
                        await_count(dve, att, ATT * t1 + 3)
                        dve.tensor_tensor(x1p[:, k1, :], tt[:, k1, :], xn[:, k1, :], ALU.add).then_inc(att, 1)
                    if on(6):
                        await_count(dve, top, TOP * t6 + 3, dve_tick)
                        dve.tensor_scalar(two(top_v), v8[:, k6, 0:2], 1.0, None, ALU.mult).then_inc(top, 1)
                    if on(2):
                        await_count(dve, gat, GAT * t2 + 3)
                        dve.tensor_tensor(gnn[:, k2, :], gnn[:, k2, :], VEC["gbias"][:, :], ALU.add).then_inc(gat, 1)
                    if on(1):
                        await_count(dve, att, ATT * t1 + 4, dve_tick)
                        dve.bn_stats(st[0][:, k1, :], x1p[:, k1, :]).then_inc(att, 1)
                    if on(0):
                        await_count(dve, q_act, 2 * t + 2)
                        dve.scalar_tensor_tensor(qf[:, k, :, :], eq[:, k, :, :], 1.0, rq[:, k, :, :], ALU.min,
                                                 ALU.add).then_inc(qfs, 1)
                    if on(1):
                        await_count(dve, att, ATT * t1 + 5, dve_tick)
                        dve.bn_aggr(mv[0][:, k1, :], st[0][:, k1, :]).then_inc(att, 1)
                    if on(2):
                        await_count(dve, gat, GAT * t2 + 4)
                        dve.scalar_tensor_tensor(nb[:, k2, :], gnn[:, k2, :], 0.0, xt[:, k2, :], ALU.max,
                                                 ALU.add).then_inc(gat, 1)
                    if on(2):
                        await_count(dve, aff, AFF * t2 + 2)
                        dve.tensor_tensor(x1b[:, k2, :], x1[:, k2, :], VEC["b2"][:, :], ALU.add).then_inc(aff, 1)
                    if on(6):
                        dve.tensor_scalar(two(top_i), i8[:, k6, 0:2], 1.0, None, ALU.mult).then_inc(top, 1)
                walk(dve, NT, 6, R, body, head=3)

            @block.tensor
            def _(pe):
                pe.wait_ge(w_in, 16 * 12)

                def turn(dst, src):
                    for c in range(2):
                        last = pe.transpose(dst[:, P * c:P * c + P], src[:, P * c:P * c + P], ident[:, :])
                    return last

                def columns(dst, w, srcT):
                    for o in range(2):
                        for c in range(2):
                            last = pe.matmul(dst[:, P * o:P * o + P], w[:, c, P * o:P * o + P], srcT[:, c, :],
                                             start=(c == 0), stop=(c == 1))
                    return last

                def rows(dst, srcT, w):
                    for c in range(2):
                        last = pe.matmul(dst, srcT[:, c, :], w[:, c, :], start=(c == 0), stop=(c == 1))
                    return last

                def body(t, k, on):
                    w = lambda sem, v: await_count(pe, sem, v, pe_tick)
                    t1, k1 = t - 1, (k - 1) % R
                    t2, k2 = t - 2, (k - 2) % R
                    t5, k5 = t - 5, (k - 5) % R
                    if on(0):
                        w(x_in[k], 8 * (t - k) + 32)
                        w(xT_ready, t)
                        turn(p_xT, xn[:, k, :]).then_inc(turned, 1)
                    if on(1):
                        w(qfs, t1 + 1)
                        w(att, ATT * (t1 - 1) + 3)
                        for c in range(2):
                            last = pe.matmul(p_att[:, (P + 4) * c:(P + 4) * (c + 1)], qf[:, k1, c, :],
                                             kvb[:, c, :], start=True, stop=True)
                        last.then_inc(attprod, 1)
                    if on(5):
                        w(nrm, t5 + 1)
                        w(x3T_ready, t5)
                        turn(p_x3T, x3[:, k5, :]).then_inc(x3turned, 1)
                    if on(0):
                        w(xT_ready, t + 1)
                        w(q_act, 2 * t)
                        columns(p_q, wq, xnT[:, k, :, :]).then_inc(qprod, 1)
                    if on(5):
                        w(x3T_ready, t5 + 1)
                        w(top, TOP * (t5 - 1) + 1)
                        rows(p_lg[:, 0:X], x3T[:, k5, :, :], wgate).then_inc(gateprod, 1)
                    if on(2):
                        w(aff, AFF * t2 + 2)
                        w(x1T_ready, t2)
                        turn(p_x1T, x1[:, k2, :]).then_inc(x1turned, 1)
                        w(x1T_ready, t2 + 1)
                        w(gelu, 2 * t2)
                        columns(p_h, w1, x1T[:, k2, :, :]).then_inc(hprod, 1)
                        w(gelu, 2 * t2 + 2)
                        w(mlp, MLP * (t2 - 1) + 1)
                        rows(p_y[:, 0:D], hT[:, k2, :, :], w2).then_inc(yprod, 1)
                walk(pe, NT, 5, R, body, head=3)

            @block.scalar
            def _(act):
                act.wait_ge(w_in, 16 * 12)
                both = lambda ap, k: ap[:, k, :, :].rearrange("p c n -> p (c n)")

                def body(t, k, on):
                    t2, k2 = t - 2, (k - 2) % R
                    t5, k5 = t - 5, (k - 5) % R
                    if on(0):
                        await_count(act, turned, t + 1)
                        act.activation(both(xnT, k), p_xT[:, 0:D], ACT.Copy).then_inc(xT_ready, 1)
                    if on(5):
                        await_count(act, x3turned, t5 + 1)
                        act.activation(both(x3T, k5), p_x3T[:, 0:D], ACT.Copy).then_inc(x3T_ready, 1)
                    if on(0):
                        await_count(act, qprod, t + 1)
                        act.activation(both(eq, k), p_q[:, 0:D], ACT.Exp).then_inc(q_act, 1)
                        act.activation(both(rq, k), p_q[:, 0:D], ACT.Relu).then_inc(q_act, 1)
                    if on(5):
                        await_count(act, nrm, t5 + 1, act_tick)
                        act.activation(acc[:, bass.ds(t5, 1), 0:D].rearrange("p a n -> p (a n)"), x3[:, k5, :],
                                       ACT.Copy).then_inc(kept, 1)
                    if on(2):
                        await_count(act, x1turned, t2 + 1)
                        act.activation(both(x1T, k2), p_x1T[:, 0:D], ACT.Copy).then_inc(x1T_ready, 1)
                        await_count(act, hprod, t2 + 1)
                        for c in range(2):
                            act.activation(hT[:, k2, c, :], p_h[:, P * c:P * c + P], ACT.Gelu,
                                           bias=b1c[:, c:c + 1]).then_inc(gelu, 1)
                walk(act, NT, 5, R, body, head=3)
                act.wait_ge(gelu, 2 * NT)
                act.wait_ge(kept, NT)

        with ExitStack() as ctx:
            s = lambda name, shape, dt=F32: sb("r_" + name, shape, dt, ctx)
            oh = s("oh", [P, 2, NT, X])
            both = s("both", [P, NT, X])
            tot = s("tot", [P, NT, X])
            cum = s("cum", [P, NT, X])
            sl = s("sl", [P, NT, X])
            pick = s("pick", [P, NT, X])
            cnt = s("cnt", [P, X])
            cnt_i = s("cnt_i", [P, X], I32)
            cumx = s("cumx", [P, X])
            base = s("base", [P, X])
            slot_f = s("slot_f", [P, 2, NT])
            dv = s("dv", [P, NT])
            ev = s("ev", [P, NT])
            ev1 = s("ev1", [P, NT])
            past = s("past", [1, XT, X])
            te = s("te", [1, XT])
            R = 4
            stage = [s(f"stage{k}", [P, D]) for k in range(R)]
            sidx = [s(f"sidx{k}", [P, 2], I32) for k in range(R)]
            pr = ctx.enter_context(nc.psum_tensor("r_pr", [P, 4, 512], F32))
            sem = lambda n: ctx.enter_context(nc.semaphore("r_" + n))
            chain, hots, sums, diffs, exps = sem("ops"), sem("one_hots"), sem("prefix_sums"), sem("diffs"), sem("exps")
            rows_staged, idx_staged = sem("rows_staged"), sem("idx_staged")
            scattered = [sem(f"scattered{k}") for k in range(R)]
            block = ctx.enter_context(nc.Block())
            HALF = 25 * X

            @block.vector
            def _(dve):
                done = [0]

                def link(ins):
                    done[0] += 1
                    ins.then_inc(chain, 1)
                    dve.wait_ge(chain, done[0])

                for k in range(2):
                    link(dve.tensor_tensor(oh[:, k, :, :], iota_n[:, 0:X].unsqueeze(1).to_broadcast([P, NT, X]),
                                           top_i[:, :, k:k + 1].to_broadcast([P, NT, X]), ALU.is_equal))
                dve.tensor_tensor(both[:, :, :], oh[:, 0, :, :], oh[:, 1, :, :], ALU.add).then_inc(hots, 1)
                dve.tensor_tensor(dv[:, :], top_v[:, :, 1], top_v[:, :, 0], ALU.subtract).then_inc(diffs, 1)
                dve.wait_ge(exps, 1)
                link(dve.tensor_scalar(ev1[:, :], ev[:, :], 1.0, None, ALU.add))
                link(dve.reciprocal(dv[:, :], ev1[:, :]))
                link(dve.tensor_copy(wtop[:, :, 0], dv[:, :]))
                link(dve.tensor_tensor(wtop[:, :, 1], dv[:, :], ev[:, :], ALU.mult))
                dve.wait_ge(sums, 1)
                fl = lambda ap: ap[:, :, :].rearrange("p t x -> p (t x)")
                link(dve.tensor_copy(fl(tot)[:, 0:HALF], pr[:, 2, 0:HALF]))
                link(dve.tensor_copy(fl(tot)[:, HALF:NT * X], pr[:, 3, 0:NT * X - HALF]))
                for e in range(X):
                    link(dve.tensor_tensor_scan(cum[:, :, e], tot[:, :, e], ones[:, 0:NT], 0.0, ALU.add, ALU.mult))
                link(dve.tensor_scalar(cnt_i[:, :], cum[:, NT - 1, :], float(P - 1), None, ALU.add))
                link(dve.tensor_scalar(cnt_i[:, :], cnt_i[:, :], P.bit_length() - 1, None, ALU.logical_shift_right))
                link(dve.tensor_copy(cnt[:, :], cnt_i[:, :]))
                link(dve.tensor_tensor_scan(cumx[:, :], cnt[:, :], ones[:, 0:X], 0.0, ALU.add, ALU.mult))
                link(dve.tensor_tensor(base[:, :], cumx[:, :], cnt[:, :], ALU.subtract))
                link(dve.tensor_tensor(sl[:, :, :], cum[:, :, :], tot[:, :, :], ALU.subtract))
                link(dve.tensor_tensor(fl(sl)[:, 0:HALF], fl(sl)[:, 0:HALF], pr[:, 0, 0:HALF], ALU.add))
                link(dve.tensor_tensor(fl(sl)[:, HALF:NT * X], fl(sl)[:, HALF:NT * X], pr[:, 1, 0:NT * X - HALF],
                                       ALU.add))
                link(dve.scalar_tensor_tensor(sl[:, :, :], base[:, :].unsqueeze(1).to_broadcast([P, NT, X]), float(P),
                                              sl[:, :, :], ALU.mult, ALU.add))
                for k in range(2):
                    link(dve.tensor_tensor(pick[:, :, :], sl[:, :, :], oh[:, k, :, :], ALU.mult))
                    link(dve.tensor_reduce(slot_f[:, k, :], pick[:, :, :], AX.X, ALU.add))
                    link(dve.tensor_copy(slot[:, :, k], slot_f[:, k, :]))
                link(dve.tensor_tensor(past[:, :, :], iota_n[0:1, 0:XT].unsqueeze(2).to_broadcast([1, XT, X]),
                                       cumx[0:1, :].unsqueeze(1).to_broadcast([1, XT, X]), ALU.is_ge))
                link(dve.tensor_reduce(te[:, :], past[:, :, :], AX.X, ALU.add))
                link(dve.tensor_scalar(texp[:, :], te[:, :], float(X - 1), None, ALU.min))

                def body(t, k, on):
                    await_count(dve, scattered[k], (t - k - R) * (32 // R) + 32, dve_tick)
                    dve.tensor_copy(sidx[k][:, :], slot[:, bass.ds(t, 1), :].rearrange("p a n -> p (a n)")
                                    ).then_inc(idx_staged, 1)
                walk(dve, NT, 0, R, body)

            @block.tensor
            def _(pe):
                pe.wait_ge(hots, 1)
                flat = both[:, :, :].rearrange("p t x -> p (t x)")
                for a, w in ((0, lower), (2, ones)):
                    pe.matmul(pr[:, a, 0:HALF], w[:, :], flat[:, 0:HALF], start=True, stop=True)
                    last = pe.matmul(pr[:, a + 1, 0:NT * X - HALF], w[:, :], flat[:, HALF:NT * X], start=True, stop=True)
                last.then_inc(sums, 1)

            @block.scalar
            def _(act):
                act.wait_ge(diffs, 1)
                act.activation(ev[:, :], dv[:, :], ACT.Exp).then_inc(exps, 1)

                def body(t, k, on):
                    await_count(act, scattered[k], (t - k - R) * (32 // R) + 32, act_tick)
                    act.activation(stage[k][:, :], acc[:, bass.ds(t, 1), 0:D].rearrange("p a n -> p (a n)"),
                                   ACT.Copy).then_inc(rows_staged, 1)
                walk(act, NT, 0, R, body)

            @block.gpsimd
            def _(pool):
                def body(t, k, on):
                    await_count(pool, rows_staged, t + 1, pool_tick)
                    await_count(pool, idx_staged, t + 1, pool_tick)
                    for c in range(2):
                        pool.indirect_dma_start(slots_d, bass.IndirectOffsetOnAxis(sidx[k][:, c:c + 1], 0),
                                                stage[k][:, :], None).then_inc(scattered[k], 16)
                walk(pool, NT, 0, R, body)
                for k in range(R):
                    pool.wait_ge(scattered[k], 32 * ((NT + R - 1 - k) // R))

        with ExitStack() as ctx:
            s = lambda name, shape, dt=F32: sb("x_" + name, shape, dt, ctx)
            R = 4
            w1e = s("w1e", [P, R, 2, F])
            w2e = s("w2e", [P, R, 4, D])
            b1a = s("b1a", [P, X * 4])
            b2a = s("b2a", [P, X, D])
            xs = s("xs", [P, R, D])
            xsT = s("xsT", [P, R, 2, P])
            hT = s("hT", [P, R, 4, P])
            ye = s("ye", [P, R, D])
            pT = ctx.enter_context(nc.psum_tensor("x_pT", [P, 2, 512], F32))
            pH = ctx.enter_context(nc.psum_tensor("x_pH", [P, 2, 512], F32))
            pY = ctx.enter_context(nc.psum_tensor("x_pY", [P, 2, 512], F32))
            sem = lambda n: ctx.enter_context(nc.semaphore("x_" + n))
            b_in = sem("biases_in")
            in_ = [sem(f"in{k}") for k in range(R)]
            out_ = [sem(f"out{k}") for k in range(R)]
            turned, tcopied, hid, relu, prod, summed = (sem("turned"), sem("turned_copied"), sem("hidden"),
                                                        sem("relu"), sem("product"), sem("bias_added"))
            block = ctx.enter_context(nc.Block())
            UN = R

            @block.sync
            def _(sp):
                sp.dma_start(b1a[:, :], eb1).then_inc(b_in, 16)
                sp.dma_start(b2a[:, :, :].rearrange("p x n -> p (x n)"),
                             eb2.rearrange("x n -> (x n)").partition_broadcast(P)).then_inc(b_in, 16)

                def body(t, k, on):
                    e = sp.value_load(texp[0:1, bass.ds(t, 1)], min_val=0, max_val=X - 1)
                    await_count(sp, prod, t - R + 1, sp_tick)
                    sp.dma_start(xs[:, k, :], slots_d[bass.ds(t * P, P), :]).then_inc(in_[k], 16)
                    sp.dma_start(w1e[:, k, :, :], ew1[bass.ds(e, 1), :, :].rearrange("a (k p) f -> p (a k) f", p=P)
                                 ).then_inc(in_[k], 16)
                    sp.dma_start(w2e[:, k, :, :], ew2[bass.ds(e, 1), :, :].rearrange("a (k p) f -> p (a k) f", p=P)
                                 ).then_inc(in_[k], 16)
                walk(sp, XT, 0, UN, body)

            @block.tensor
            def _(pe):
                def body(t, k, on):
                    w = lambda sem, v: await_count(pe, sem, v, pe_tick)
                    if on(0):
                        q, b = k % R, k % 2
                        w(in_[q], 12 * (t - q) + 48)
                        w(tcopied, t - 1)
                        for c in range(2):
                            last = pe.transpose(pT[:, b, P * c:P * c + P], xs[:, q, P * c:P * c + P], ident[:, :])
                        last.then_inc(turned, 1)
                    if on(1):
                        t1, q, b = t - 1, (k - 1) % R, (k - 1) % 2
                        w(tcopied, t1 + 1)
                        w(relu, 4 * (t1 - 2) + 4)
                        for o in range(4):
                            for c in range(2):
                                last = pe.matmul(pH[:, b, P * o:P * o + P], w1e[:, q, c, P * o:P * o + P],
                                                 xsT[:, q, c, :], start=(c == 0), stop=(c == 1))
                        last.then_inc(hid, 1)
                    if on(2):
                        t2, q, b = t - 2, (k - 2) % R, (k - 2) % 2
                        w(relu, 4 * t2 + 4)
                        w(summed, t2 - 1)
                        for c in range(4):
                            last = pe.matmul(pY[:, b, 0:D], hT[:, q, c, :], w2e[:, q, c, :], start=(c == 0),
                                             stop=(c == 3))
                        last.then_inc(prod, 1)
                walk(pe, XT, 2, UN, body)

            @block.scalar
            def _(act):
                act.wait_ge(b_in, 32)

                def body(t, k, on):
                    if on(0):
                        await_count(act, turned, t + 1)
                        await_count(act, hid, t - R + 1)
                        act.activation(xsT[:, k % R, :, :].rearrange("p c n -> p (c n)"), pT[:, k % 2, 0:D],
                                       ACT.Copy).then_inc(tcopied, 1)
                    if on(1):
                        t1, q, b = t - 1, (k - 1) % R, (k - 1) % 2
                        e = act.value_load(texp[0:1, bass.ds(t1, 1)], min_val=0, max_val=X - 1)
                        await_count(act, prod, t1 - R + 2, act_tick)
                        await_count(act, hid, t1 + 1, act_tick)
                        for o in range(4):
                            act.activation(hT[:, q, o, :], pH[:, b, P * o:P * o + P], ACT.Relu,
                                           bias=b1a[:, bass.ds(e * 4 + o, 1)]).then_inc(relu, 1)
                walk(act, XT, 1, UN, body)

            @block.vector
            def _(dve):
                dve.wait_ge(b_in, 32)

                def body(t, k, on):
                    if on(0):
                        e = dve.value_load(texp[0:1, bass.ds(t, 1)], min_val=0, max_val=X - 1)
                        await_count(dve, out_[k], 4 * (t - k))
                        await_count(dve, prod, t + 1)
                        dve.tensor_tensor(ye[:, k % R, :], pY[:, k % 2, 0:D],
                                          b2a[:, bass.ds(e, 1), :].rearrange("p a n -> p (a n)"), ALU.add
                                          ).then_inc(summed, 1)
                walk(dve, XT, 0, UN, body)

            @block.gpsimd
            def _(pool):
                def body(t, k, on):
                    await_count(pool, summed, t + 1, pool_tick)
                    pool.dma_start(eout_d[bass.ds(t * P, P), :], ye[:, k % R, :]).then_inc(out_[k % R], 16)
                walk(pool, XT, 0, UN, body)
                for k in range(R):
                    pool.wait_ge(out_[k], 16 * ((XT + R - 1 - k) // R))

        with ExitStack() as ctx:
            s = lambda name, shape, dt=F32: sb("c_" + name, shape, dt, ctx)
            R = 4
            gb = s("gb", [P, D])
            bb = s("bb", [P, D])
            sidx = [s(f"sidx{k}", [P, 2], I32) for k in range(R)]
            eo = [s(f"eo{k}", [P, 2, D]) for k in range(R)]
            x2 = s("x2", [P, R, D])
            y1 = s("y1", [P, R, D])
            y2 = s("y2", [P, R, D])
            st = s("st", [P, R, 6])
            mv = s("mv", [P, R, 2])
            ve = s("ve", [P, R, 1])
            rstd = s("rstd", [P, R, 1])
            o = s("o", [P, R, D])
            sem = lambda n: ctx.enter_context(nc.semaphore("c_" + n))
            w_in = sem("affine_in")
            eo_in = [sem(f"expert_rows_in{k}") for k in range(R)]
            x2_in = [sem(f"x2_in{k}") for k in range(R)]
            out_ = [sem(f"out{k}") for k in range(R)]
            staged, vec = sem("index_staged"), sem("vector_ops")
            block = ctx.enter_context(nc.Block())
            rooted = sem("rooted")
            NV = 8

            @block.sync
            def _(sp):
                sp.dma_start(gb[:, :], gamma.partition_broadcast(P)).then_inc(w_in, 16)
                sp.dma_start(bb[:, :], beta.partition_broadcast(P)).then_inc(w_in, 16)

                def body(t, k, on):
                    if on(0):
                        await_count(sp, vec, NV * (t - R) + NV, sp_tick)
                        sp.dma_start(x2[:, k, :], x2_d[bass.ds(t * P, P), :]).then_inc(x2_in[k], 16)
                    if on(2):
                        q = (k - 2) % R
                        await_count(sp, vec, NV * (t - 2) + NV, sp_tick)
                        sp.dma_start(out[bass.ds((t - 2) * P, P), :], o[:, q, :]).then_inc(out_[q], 16)
                walk(sp, NT, 2, R, body)
                for k in range(R):
                    sp.wait_ge(out_[k], 16 * ((NT + R - 1 - k) // R))

            @block.scalar
            def _(act):
                def body(t, k, on):
                    await_count(act, eo_in[k], 8 * (t - k), act_tick)
                    act.activation(sidx[k][:, :], slot[:, bass.ds(t, 1), :].rearrange("p a n -> p (a n)"),
                                   ACT.Copy).then_inc(staged, 1)
                walk(act, NT, 0, R, body)

            @block.gpsimd
            def _(pool):
                def body(t, k, on):
                    if on(0):
                        await_count(pool, staged, t + 1, pool_tick)
                        await_count(pool, vec, NV * (t - R) + NV, pool_tick)
                        for c in range(2):
                            pool.indirect_dma_start(eo[k][:, c, :], None, eout_d,
                                                    bass.IndirectOffsetOnAxis(sidx[k][:, c:c + 1], 0)
                                                    ).then_inc(eo_in[k], 16)
                    if on(2):
                        await_count(pool, vec, NV * (t - 2) + 5)
                        pool.tensor_tensor(rstd[:, (k - 2) % R, :], ve[:, (k - 2) % R, :], mhalf[:, :],
                                           ALU.pow).then_inc(rooted, 1)
                walk(pool, NT, 2, R, body)
                for k in range(R):
                    pool.wait_ge(eo_in[k], 32 * ((NT + R - 1 - k) // R))

            @block.vector
            def _(dve):
                dve.wait_ge(w_in, 32)

                def body(t, k, on):
                    done = [0]

                    def link(ins):
                        done[0] += 1
                        ins.then_inc(vec, 1)
                        await_count(dve, vec, NV * t + done[0], dve_tick)

                    wt = lambda c: wtop[:, bass.ds(t, 1), c:c + 1].rearrange("p a n -> p (a n)")
                    await_count(dve, eo_in[k], 8 * (t - k) + 32)
                    link(dve.scalar_tensor_tensor(y1[:, k, :], eo[k][:, 0, :], wt(0),
                                                  acc[:, bass.ds(t, 1), 0:D].rearrange("p a n -> p (a n)"),
                                                  ALU.mult, ALU.add))
                    link(dve.scalar_tensor_tensor(y2[:, k, :], eo[k][:, 1, :], wt(1), y1[:, k, :], ALU.mult, ALU.add))
                    link(dve.bn_stats(st[:, k, :], y2[:, k, :]))
                    link(dve.bn_aggr(mv[:, k, :], st[:, k, :]))
                    link(dve.tensor_scalar(ve[:, k, :], mv[:, k, 1:2], LN_EPS, None, ALU.add))
                    await_count(dve, rooted, t + 1)
                    link(dve.scalar_tensor_tensor(y1[:, k, :], y2[:, k, :], mv[:, k, 0:1], gb[:, :], ALU.subtract,
                                                  ALU.mult))
                    link(dve.scalar_tensor_tensor(y2[:, k, :], y1[:, k, :], rstd[:, k, :], bb[:, :], ALU.mult, ALU.add))
                    await_count(dve, x2_in[k], 4 * (t - k) + 16)
                    await_count(dve, out_[k], 4 * (t - k))
                    link(dve.tensor_tensor(o[:, k, :], y2[:, k, :], x2[:, k, :], ALU.add))
                walk(dve, NT, 0, R, body)


_OUTS = [((NPAD, D), 'float32')]


def kernel(**inputs):
    import numpy as _np
    import concourse.bacc as _bacc
    from concourse import mybir as _mybir
    from concourse.bass_utils import run_bass_kernel_spmd as _run

    g = {k: _np.asarray(v) for k, v in inputs.items()}
    c = _np.ascontiguousarray
    edges = _np.full((2, EPAD), 0, _np.int32)
    edges[1, E:] = PAD_DST
    edges[0, :E] = g['src']
    edges[1, :E] = g['dst']
    xp = _np.zeros((NPAD, D), _np.float32)
    xp[:N] = g['x']
    ins = {
        'x': xp, 'edges': edges, 'gW': g['L0_gnn_W'], 'att_src': g['L0_gnn_att_src'],
        'att_dst': g['L0_gnn_att_dst'], 'gbias': g['L0_gnn_bias'], 'wqkvT': c(g['L0_mix_Wqkv'].T),
        'ln1g': g['L0_mix_ln1_g'], 'ln1b': g['L0_mix_ln1_b'], 'w1T': c(g['L0_mix_W1'].T), 'b1': g['L0_mix_b1'],
        'w2T': c(g['L0_mix_W2'].T), 'b2': g['L0_mix_b2'], 'ln2g': g['L0_mix_ln2_g'], 'ln2b': g['L0_mix_ln2_b'],
        'gate_w': g['L0_ffn_gate_w'], 'gate_b': g['L0_ffn_gate_b'], 'ew1': g['L0_ffn_w1'],
        'eb1': c(g['L0_ffn_b1'].reshape(X, 4, P).transpose(2, 0, 1).reshape(P, X * 4)), 'ew2': g['L0_ffn_w2'],
        'eb2': g['L0_ffn_b2'], 'gamma': g['L0_ffn_gamma'], 'beta': g['L0_ffn_beta'],
    }
    nc = _bacc.Bacc("TRN2", target_bir_lowering=False, num_devices=1)
    arrays, args = {}, []
    for name, a in ins.items():
        a = c(a)
        arrays[f"in_{name}_dram"] = a
        args.append(nc.dram_tensor(f"in_{name}_dram", a.shape, _mybir.dt.from_np(a.dtype), kind="ExternalInput").ap())
    for i, (shape, dtype) in enumerate(_OUTS):
        dt = _mybir.dt.from_np(_np.dtype(dtype))
        args.append(nc.dram_tensor(f"out_{i}_dram", shape, dt, kind="ExternalOutput").ap())
    gps_kernel(nc, *args)
    r = _run(nc, [arrays], core_ids=[0])
    return r.results[0]["out_0_dram"][:N]
```

```python
from contextlib import ExitStack

import concourse.bass as bass
from concourse import mybir

F32 = mybir.dt.float32
I32 = mybir.dt.int32
U32 = mybir.dt.uint32
ALU = mybir.AluOpType
ACT = mybir.ActivationFunctionType
AX = mybir.AxisListType

P = 128
N = 6250
D = 256
H = 8
C = D // H
CW = C + 1
ROW = H * CW
NT = -(-N // P)
NPAD = NT * P
E = 206250
J = 4
SE = J * P
STEPS = (E + NT * (SE - 1)) // SE
EPAD = E + SE
EC = -(-E // P)
PAD_DST = 1000000
X = 16
F = 512
XT = (2 * NPAD + X * (P - 1)) // P
NEG = -1.0e30
LN_EPS = 1e-5
RING = 8
QS = -(-STEPS // P)
STEPS_PAD = QS * P
DIAGS = 17


def walk(eng, count, lag, unroll, body, head=1):
    full = count // unroll - head
    for t in range(head * unroll):
        body(t, t % unroll, lambda l, t=t: 0 <= t - l < count)
    if full > 0:
        with eng.Fori(head, head + full) as u:
            for s in range(unroll):
                body(u * unroll + s, s, lambda l: True)
    for t in range((head + full) * unroll, count + lag):
        body(t, t % unroll, lambda l, t=t: 0 <= t - l < count)


def await_count(eng, sem, value, tick=None):
    if isinstance(value, int):
        if value > 0:
            eng.wait_ge(sem, value)
        return
    eng.wait_ge(sem, value)
    if tick is not None:
        eng.sem_inc(tick, 1)


def gps_kernel(nc, x, edges, gW, att_src, att_dst, gbias, wqkvT, ln1g, ln1b, w1T, b1, w2T, b2, ln2g, ln2b,
               gate_w, gate_b, ew1, eb1, ew2, eb2, gamma, beta, out):
    dram = lambda name, shape, dt=F32: nc.dram_tensor(name, shape, dt, kind="Internal").ap()
    table = dram("gather_table", (NPAD, ROW))
    xn_d = dram("xn_rows", (NPAD, D))
    x2_d = dram("x2_rows", (NPAD, D))
    slots_d = dram("slot_rows", (XT * P, D))
    eout_d = dram("expert_rows", (XT * P, D))

    with ExitStack() as whole:
        sb = lambda name, shape, dt=F32, ctx=whole: ctx.enter_context(nc.sbuf_tensor(name, shape, dt))
        sp_tick = whole.enter_context(nc.semaphore("sp_ticks"))
        dve_tick = whole.enter_context(nc.semaphore("dve_ticks"))
        act_tick = whole.enter_context(nc.semaphore("act_ticks"))
        pe_tick = whole.enter_context(nc.semaphore("pe_ticks"))
        pool_tick = whole.enter_context(nc.semaphore("pool_ticks"))
        ident = sb("ident", [P, P])
        mhalf = sb("mhalf", [P, 1])
        iota_n = sb("iota_n", [P, P])
        ones = sb("ones", [P, P])
        stepcol = sb("stepcol", [P, QS])
        bound = sb("bound", [P, NT])
        lower = sb("lower", [P, P])
        valid = sb("valid", [P, NT])
        adst = sb("adst", [P, NT, H])
        acc = sb("acc", [P, NT, ROW])
        kvb = sb("kvb", [P, 2, P + 4])
        top_v = sb("top_v", [P, NT, 2])
        top_i = sb("top_i", [P, NT, 2])
        slot = sb("slot", [P, NT, 2], I32)
        wtop = sb("wtop", [P, NT, 2])
        texp = sb("texp", [1, XT], I32)
        tile_f = sb("tile_f", [P, STEPS_PAD])
        reset = sb("reset", [P, STEPS_PAD])
        tile_i = sb("tile_i", [1, STEPS_PAD], I32)
        start_i = sb("start_i", [1, STEPS_PAD], I32)

        with ExitStack() as ctx:
            iota_i = sb("t_iota_i", [P, P], I32, ctx)
            stepcol_i = sb("t_stepcol_i", [P, QS], I32, ctx)
            bound_i = sb("t_bound_i", [P, NT], I32, ctx)
            made = ctx.enter_context(nc.semaphore("constants_made"))
            cast = ctx.enter_context(nc.semaphore("constants_cast"))
            block = ctx.enter_context(nc.Block())

            @block.gpsimd
            def _(pool):
                pool.memset(ident[:, :], 0.0).then_inc(made, 1)
                pool.memset(lower[:, :], 1.0).then_inc(made, 1)
                pool.memset(valid[:, :], 1.0).then_inc(made, 1)
                pool.memset(ones[:, :], 1.0).then_inc(made, 1)
                pool.memset(mhalf[:, :], -0.5).then_inc(made, 1)
                pool.iota(iota_i[:, :], [[1, P]], base=0, channel_multiplier=0).then_inc(made, 1)
                pool.iota(stepcol_i[:, :], [[P, QS]], base=0, channel_multiplier=1).then_inc(made, 1)
                pool.iota(bound_i[:, :], [[P, NT]], base=P, channel_multiplier=0).then_inc(made, 1)
                pool.wait_ge(made, 8)
                pool.affine_select(out=ident[:, :], in_=ident[:, :], compare_op=ALU.not_equal, fill=1.0,
                                   base=0, pattern=[[-1, P]], channel_multiplier=1).then_inc(made, 1)
                pool.affine_select(out=lower[:, :], in_=lower[:, :], compare_op=ALU.is_gt, fill=0.0,
                                   base=0, pattern=[[1, P]], channel_multiplier=-1).then_inc(made, 1)
                pool.affine_select(out=valid[:, :], in_=valid[:, :], compare_op=ALU.is_gt, fill=0.0,
                                   base=N, pattern=[[-P, NT]], channel_multiplier=-1).then_inc(made, 1)

            @block.vector
            def _(dve):
                dve.wait_ge(made, 8)
                dve.tensor_copy(iota_n[:, :], iota_i[:, :]).then_inc(cast, 1)
                dve.tensor_copy(stepcol[:, :], stepcol_i[:, :]).then_inc(cast, 1)
                dve.tensor_copy(bound[:, :], bound_i[:, :]).then_inc(cast, 1)

        with ExitStack() as ctx:
            s = lambda name, shape, dt=F32: sb("n_" + name, shape, dt, ctx)
            R = 4
            gw_sb = s("gw", [P, 2, D])
            wg = s("wg", [P, 2, ROW + H])
            prod = s("prod", [P, 2, D])
            attb = s("attb", [P, 2, D])
            wkv = s("wkv", [P, 2, 2 * D])
            xt = s("xt", [P, R, D])
            xn = s("xn", [P, R, D])
            xnT = s("xnT", [P, R, 2, P])
            st = s("st", [P, R, 6])
            mv = s("mv", [P, R, 2])
            ve = s("ve", [P, R, 1])
            rstd = s("rstd", [P, R, 1])
            rows = s("rows", [P, R, ROW])
            ek = s("ek", [P, R, D])
            rk = s("rk", [P, R, D])
            kf = s("kf", [P, R, D])
            vv = s("vv", [P, R, 2, P + 1])
            zero = s("zero", [P, P + 1])
            dst_i = s("dst_i", [P, EC], I32)
            dst_f = s("dst_f", [P, EC])
            less = s("less", [P, EC])
            part = s("part", [P, NT + 1])
            below = s("below", [P, NT + 1])
            cnt = s("cnt", [P, NT])
            cnt_i = s("cnt_i", [P, NT], I32)
            cumt = s("cumt", [P, NT])
            fst = s("fst", [P, NT])
            dfst = s("dfst", [P, NT])
            mask = s("mask", [P, QS, NT])
            tile_c = s("tile_c", [P, QS])
            offs_c = s("offs_c", [P, QS])
            diag = s("diag", [P, 2, QS, P])
            changed = s("changed", [P, STEPS_PAD])
            pT = ctx.enter_context(nc.psum_tensor("n_pT", [P, 2, 512], F32))
            pG = ctx.enter_context(nc.psum_tensor("n_pG", [P, 2, 512], F32))
            pK = ctx.enter_context(nc.psum_tensor("n_pK", [P, 2, 512], F32))
            pKV = ctx.enter_context(nc.psum_tensor("n_pKV", [P, 2, 512], F32))
            sem = lambda n: ctx.enter_context(nc.semaphore("n_" + n))
            w_in, dst_in = sem("weights_in"), sem("dst_in")
            x_in = [sem(f"x_in{k}") for k in range(R)]
            stored = [sem(f"stored{k}") for k in range(R)]
            prep, norm, tr, trc = sem("weights_ready"), sem("norm"), sem("transposed"), sem("transposed_copied")
            proj, kproj = sem("projected"), sem("kv_projected")
            evac, kact, kdone, kvsum = sem("rows_ready"), sem("k_activated"), sem("k_ready"), sem("kv_summed")
            fin, rooted = sem("kv_copied"), sem("rooted")
            counted, chain, summed = sem("counted"), sem("schedule_ops"), sem("schedule_sums")
            block = ctx.enter_context(nc.Block())

            @block.gpsimd
            def _(pool):
                pool.memset(acc[:, :, :], 0.0).then_inc(fin, 1)

                def body(t, k, on):
                    await_count(pool, norm, 4 * t + 3)
                    pool.tensor_tensor(rstd[:, k, :], ve[:, k, :], mhalf[:, :], ALU.pow).then_inc(rooted, 1)
                walk(pool, NT, 0, R, body, head=2)

            @block.sync
            def _(sp):
                sp.dma_start(gw_sb[:, :, :], gW.rearrange("(k p) n -> p k n", p=P)).then_inc(w_in, 16)
                sp.dma_start(attb[:, 0, :], att_src.rearrange("h c -> (h c)").partition_broadcast(P)).then_inc(w_in, 16)
                sp.dma_start(attb[:, 1, :], att_dst.rearrange("h c -> (h c)").partition_broadcast(P)).then_inc(w_in, 16)
                sp.dma_start(wkv[:, :, :], wqkvT[:, D:3 * D].rearrange("(k p) n -> p k n", p=P)).then_inc(w_in, 16)
                sp.dma_start(dst_i[:, :], edges[1, 0:P * EC].rearrange("(p n) -> p n", p=P)).then_inc(dst_in, 16)

                def body(t, k, on):
                    if on(0):
                        await_count(sp, norm, 4 * (t - R) + 4, sp_tick)
                        sp.dma_start(xt[:, k, :], x[bass.ds(t * P, P), :]).then_inc(x_in[k], 16)
                    if on(1):
                        t1, k1 = t - 1, (k - 1) % R
                        await_count(sp, norm, 4 * t1 + 4, sp_tick)
                        sp.dma_start(xn_d[bass.ds(t1 * P, P), :], xn[:, k1, :]).then_inc(stored[k1], 16)
                    if on(2):
                        t2, k2 = t - 2, (k - 2) % R
                        await_count(sp, evac, 3 * t2 + 1, sp_tick)
                        sp.dma_start(table[bass.ds(t2 * P, P), :], rows[:, k2, :]).then_inc(stored[k2], 16)
                walk(sp, NT, 2, R, body, head=2)
                for k in range(R):
                    sp.wait_ge(stored[k], 32 * ((NT + R - 1 - k) // R))

            @block.vector
            def _(dve):
                dve.memset(zero[:, :], 0.0).then_inc(prep, 1)
                dve.memset(part[:, :], 0.0).then_inc(counted, 1)
                dve.wait_ge(w_in, 64)
                for k in range(2):
                    dve.tensor_copy(wg[:, k, 0:ROW].rearrange("p (h c) -> p h c", h=H)[:, :, 0:C],
                                    gw_sb[:, k, :].rearrange("p (h c) -> p h c", h=H)).then_inc(prep, 1)
                n = 3
                for a in range(2):
                    for k in range(2):
                        dve.tensor_tensor(prod[:, k, :], gw_sb[:, k, :], attb[:, a, :], ALU.mult).then_inc(prep, 1)
                        n += 1
                        dve.wait_ge(prep, n)
                        o = (wg[:, k, 0:ROW].rearrange("p (h c) -> p h c", h=H)[:, :, C] if a == 0
                             else wg[:, k, ROW:ROW + H])
                        dve.tensor_reduce(o, prod[:, k, :].rearrange("p (h c) -> p h c", h=H), AX.X,
                                          ALU.add).then_inc(prep, 1)
                        n += 1
                        dve.wait_ge(prep, n)
                dve.wait_ge(dst_in, 16)
                dve.tensor_copy(dst_f[:, :], dst_i[:, :]).then_inc(counted, 1)
                dve.wait_ge(counted, 2)

                def body(t, k, on):
                    t3, k3 = t - 3, (k - 3) % R
                    if on(0):
                        await_count(dve, x_in[k], 4 * (t - k) + 16, dve_tick)
                        dve.bn_stats(st[:, k, :], xt[:, k, :]).then_inc(norm, 1)
                        await_count(dve, norm, 4 * t + 1, dve_tick)
                        dve.bn_aggr(mv[:, k, :], st[:, k, :]).then_inc(norm, 1)
                        await_count(dve, norm, 4 * t + 2)
                        dve.tensor_scalar(ve[:, k, :], mv[:, k, 1:2], LN_EPS, None, ALU.add).then_inc(norm, 1)
                    if on(0):
                        await_count(dve, counted, t + 2, dve_tick)
                        dve.tensor_scalar(less[:, :], dst_f[:, :], bound[:, bass.ds(t, 1)], None, ALU.is_lt,
                                          ALU.add, accum_out=part[:, bass.ds(t + 1, 1)]).then_inc(counted, 1)
                        await_count(dve, rooted, t + 1)
                        await_count(dve, stored[k], 8 * (t - k))
                        await_count(dve, tr, t - R + 1)
                        dve.tensor_scalar(xn[:, k, :], xt[:, k, :], mv[:, k, 0:1], rstd[:, k, :],
                                          ALU.subtract, ALU.mult).then_inc(norm, 1)
                    if on(3):
                        await_count(dve, kact, 3 * t3 + 2)
                        dve.scalar_tensor_tensor(kf[:, k3, :], ek[:, k3, :], 1.0, rk[:, k3, :], ALU.min,
                                                 ALU.add).then_inc(kdone, 1)
                walk(dve, NT, 3, R, body, head=2)
                done = [0]

                def link(ins):
                    done[0] += 1
                    ins.then_inc(chain, 1)
                    dve.wait_ge(chain, done[0])

                dve.wait_ge(summed, 1)
                link(dve.tensor_copy(below[:, :], pT[:, 0, 0:NT + 1]))
                link(dve.tensor_tensor(cnt[:, :], below[:, 1:NT + 1], below[:, 0:NT], ALU.subtract))
                link(dve.tensor_scalar(cnt_i[:, :], cnt[:, :], float(SE - 1), None, ALU.add))
                link(dve.tensor_scalar(cnt_i[:, :], cnt_i[:, :], SE.bit_length() - 1, None,
                                       ALU.logical_shift_right))
                link(dve.tensor_copy(cnt[:, :], cnt_i[:, :]))
                link(dve.tensor_tensor_scan(cumt[:, :], cnt[:, :], ones[:, 0:NT], 0.0, ALU.add, ALU.mult))
                link(dve.tensor_tensor(fst[:, :], cumt[:, :], cnt[:, :], ALU.subtract))
                link(dve.scalar_tensor_tensor(fst[:, :], fst[:, :], -float(SE), below[:, 0:NT], ALU.mult, ALU.add))
                link(dve.tensor_tensor(dfst[:, 0:NT - 1], fst[:, 1:NT], fst[:, 0:NT - 1], ALU.subtract))
                m = mask[:, :, 0:NT - 1]
                link(dve.tensor_tensor(m, stepcol[:, :].unsqueeze(2).to_broadcast([P, QS, NT - 1]),
                                       cumt[:, 0:NT - 1].unsqueeze(1).to_broadcast([P, QS, NT - 1]), ALU.is_ge))
                link(dve.tensor_reduce(tile_c[:, :], m, AX.X, ALU.add))
                link(dve.tensor_tensor(m, m, dfst[:, 0:NT - 1].unsqueeze(1).to_broadcast([P, QS, NT - 1]), ALU.mult))
                link(dve.tensor_reduce(offs_c[:, :], m, AX.X, ALU.add))
                link(dve.tensor_scalar(offs_c[:, :], offs_c[:, :], fst[:, 0:1], None, ALU.add))
                link(dve.scalar_tensor_tensor(offs_c[:, :], stepcol[:, :], float(SE), offs_c[:, :], ALU.mult, ALU.add))
                for i, col in enumerate((tile_c, offs_c)):
                    link(dve.tensor_tensor(diag[:, i, :, :], ident[:, :].unsqueeze(1).to_broadcast([P, QS, P]),
                                           col[:, :].unsqueeze(2).to_broadcast([P, QS, P]), ALU.mult))
                assert done[0] == DIAGS
                dve.wait_ge(summed, 3)
                link(dve.tensor_scalar(tile_f[:, :], pG[:, 0, 0:STEPS_PAD], float(P), None, ALU.mult))
                link(dve.tensor_copy(tile_i[:, :], pG[0:1, 0, 0:STEPS_PAD]))
                link(dve.tensor_scalar(start_i[:, :], pG[0:1, 1, 0:STEPS_PAD], float(E), None, ALU.min))
                link(dve.memset(reset[:, :], NEG))
                link(dve.tensor_tensor(changed[:, 1:STEPS_PAD], tile_f[:, 1:STEPS_PAD], tile_f[:, 0:STEPS_PAD - 1],
                                       ALU.not_equal))
                link(dve.tensor_scalar(reset[:, 1:STEPS_PAD], changed[:, 1:STEPS_PAD], NEG, None, ALU.mult))
                dve.memset(kvb[:, :, :], 0.0).then_inc(fin, 1)
                dve.wait_ge(fin, 2)
                dve.wait_ge(kvsum, NT + 2)
                for c in range(2):
                    for h in range(4):
                        q = slice(C * h, C * h + C)
                        dve.tensor_copy(kvb[q, c, q], pKV[q, c, q]).then_inc(fin, 1)
                        dve.tensor_copy(kvb[q, c, P + h:P + h + 1], pKV[q, c, P:P + 1]).then_inc(fin, 1)

            @block.tensor
            def _(pe):
                pe.wait_ge(prep, 11)
                for c in range(2):
                    pe.matmul(pKV[:, c, 0:P + 1], zero[:, 0:P], zero[:, :], start=True, stop=False,
                              skip_group_check=True)

                def body(t, k, on):
                    w = lambda sem, v: await_count(pe, sem, v, pe_tick)
                    t1, k1 = t - 1, (k - 1) % R
                    t3, k3 = t - 3, (k - 3) % R
                    if on(0):
                        w(norm, 4 * t + 4)
                        w(trc, t - 1)
                        for c in range(2):
                            last = pe.transpose(pT[:, k % 2, P * c:P * c + P], xn[:, k, P * c:P * c + P],
                                                ident[:, :])
                        last.then_inc(tr, 1)
                    if on(1):
                        w(trc, t1 + 1)
                        w(evac, 3 * (t1 - 2) + 2)
                        for c in range(2):
                            last = pe.matmul(pG[:, k1 % 2, 0:ROW + H], xnT[:, k1, c, :], wg[:, c, :],
                                             start=(c == 0), stop=(c == 1))
                        last.then_inc(proj, 1)
                        w(kact, 3 * (t1 - 2) + 3)
                        for c in range(2):
                            last = pe.matmul(pK[:, k1 % 2, :], xnT[:, k1, c, :], wkv[:, c, :], start=(c == 0),
                                             stop=(c == 1))
                        last.then_inc(kproj, 1)
                    if on(3):
                        w(kdone, t3 + 1)
                        w(kact, 3 * t3 + 3)
                        w(evac, 3 * t3 + 3)
                        for c in range(2):
                            last = pe.matmul(pKV[:, c, 0:P + 1], kf[:, k3, P * c:P * c + P], vv[:, k3, c, :],
                                             start=False, stop=False, skip_group_check=True)
                        last.then_inc(kvsum, 1)
                walk(pe, NT, 3, R, body, head=2)
                for c in range(2):
                    pe.matmul(pKV[:, c, 0:P + 1], zero[:, 0:P], zero[:, :], start=False, stop=True,
                              skip_group_check=True).then_inc(kvsum, 1)
                pe.wait_ge(counted, NT + 2)
                pe.wait_ge(trc, NT)
                pe.matmul(pT[:, 0, 0:NT + 1], ones[:, :], part[:, :], start=True, stop=True).then_inc(summed, 1)
                pe.wait_ge(chain, DIAGS)
                pe.wait_ge(evac, 3 * NT)
                for i in range(2):
                    pe.matmul(pG[:, i, 0:STEPS_PAD], ones[:, :], diag[:, i, :, :].rearrange("p q n -> p (q n)"),
                              start=True, stop=True).then_inc(summed, 1)

            @block.scalar
            def _(act):
                def body(t, k, on):
                    t1, k1 = t - 1, (k - 1) % R
                    if on(0):
                        await_count(act, tr, t + 1)
                        await_count(act, kproj, t - R + 1)
                        act.activation(xnT[:, k, :, :].rearrange("p c n -> p (c n)"), pT[:, k % 2, 0:2 * P],
                                       ACT.Copy).then_inc(trc, 1)
                    if on(1):
                        await_count(act, proj, t1 + 1)
                        await_count(act, stored[k1], 8 * (t1 - k1))
                        act.activation(rows[:, k1, :], pG[:, k1 % 2, 0:ROW], ACT.Copy).then_inc(evac, 1)
                        act.activation(adst[:, bass.ds(t1, 1), :], pG[:, k1 % 2, ROW:ROW + H].unsqueeze(1),
                                       ACT.Copy).then_inc(evac, 1)
                        await_count(act, kproj, t1 + 1)
                        await_count(act, kdone, t1 - R + 1)
                        act.activation(ek[:, k1, :], pK[:, k1 % 2, 0:D], ACT.Exp).then_inc(kact, 1)
                        act.activation(rk[:, k1, :], pK[:, k1 % 2, 0:D], ACT.Relu).then_inc(kact, 1)
                        await_count(act, kvsum, t1 - R + 1)
                        act.activation(vv[:, k1, :, 0:P], pK[:, k1 % 2, D:2 * D].rearrange("p (c n) -> p c n", c=2),
                                       ACT.Copy).then_inc(kact, 1)
                        act.activation(vv[:, k1, :, P], valid[:, bass.ds(t1, 1)].to_broadcast([P, 2]),
                                       ACT.Copy).then_inc(evac, 1)
                walk(act, NT, 1, R, body, head=2)
                act.wait_ge(evac, 3 * NT)

        with ExitStack() as ctx:
            s = lambda name, shape, dt=F32: sb("e_" + name, shape, dt, ctx)
            pair = s("pair", [P, RING, 2, J], I32)
            gat = [s(f"gat{k}", [P, J, ROW]) for k in range(RING)]
            dloc = s("dloc", [P, RING, J])
            hot = s("hot", [P, RING, J, P])
            hotT = s("hotT", [P, RING, J, P])
            dsc = s("dsc", [P, RING, J, H])
            drow = s("drow", [J * H, RING, P])
            diff = s("diff", [J * H, RING, P + 1])
            smax = s("smax", [J * H, RING, P])
            lmax = s("lmax", [J * H, RING, P])
            zb = s("zb", [P, RING, J, H + 1])
            big = s("big", [P, 1])
            pen = s("pen", [P, RING, J])
            mc4 = s("mc4", [P, RING, J, H])
            mc = s("mc", [P, RING, H])
            uc = s("uc", [P, RING, H])
            lc = s("lc", [P, RING, H])
            dd = s("dd", [P, RING, 2 * H])
            dr = s("dr", [P, RING, H])
            rr = s("rr", [P, RING, H])
            ze = s("ze", [P, RING, J, H])
            le = s("le", [P, RING, J, H])
            se = s("se", [P, RING, J, H])
            sc = s("sc", [P, RING, J, H])
            AR = 4
            accb = s("accb", [P, AR, ROW])
            pX = ctx.enter_context(nc.psum_tensor("e_pX", [P, 2, 512], F32))
            pH = ctx.enter_context(nc.psum_tensor("e_pH", [P, 512], F32))
            pL = ctx.enter_context(nc.psum_tensor("e_pL", [P, 512], F32))
            pM = ctx.enter_context(nc.psum_tensor("e_pM", [P, 512], F32))
            pD = ctx.enter_context(nc.psum_tensor("e_pD", [P, 512], F32))
            pA = ctx.enter_context(nc.psum_tensor("e_pA", [P, 2, 512], F32))
            sem = lambda n: ctx.enter_context(nc.semaphore("e_" + n))
            pair_in = [sem(f"pair_in{k}") for k in range(RING)]
            rows_in = [sem(f"rows_in{k}") for k in range(RING)]
            init, absent, scored, stored = sem("init"), sem("absent"), sem("node_scores"), sem("sums_stored")
            local, scan, upd, shift, msg, accum = (sem("local_dst"), sem("segment_max"), sem("max_updated"),
                                                   sem("shifted"), sem("messages"), sem("accumulated"))
            dscaled, rowcopy, lastcopy, factor, expd = (sem("dst_scaled"), sem("rows_copied"), sem("last_copied"),
                                                        sem("rescale_factor"), sem("exponentials"))
            turned, lastT, tomax, expand, agg = (sem("turned"), sem("last_turned"), sem("chunk_max"),
                                                 sem("expanded"), sem("aggregated"))
            block = ctx.enter_context(nc.Block())
            UPD = 6

            @block.sync
            def _(sp):
                def body(t, k, on):
                    start = sp.value_load(start_i[0:1, bass.ds(t, 1)], min_val=0, max_val=E)
                    await_count(sp, local, 2 * (t - RING) + 1, sp_tick)
                    await_count(sp, rows_in[k], 8 * (t - k - RING) + 64, sp_tick)
                    sp.dma_start(pair[:, k, :, :],
                                 edges[:, bass.ds(start, SE)].rearrange("a (p j) -> p a j", p=P)).then_inc(pair_in[k], 16)
                walk(sp, STEPS, 0, RING, body)

            @block.gpsimd
            def _(pool):
                def body(t, k, on):
                    await_count(pool, pair_in[k], 2 * (t - k) + 16, pool_tick)
                    await_count(pool, agg, t - RING + 1, pool_tick)
                    for j in range(J):
                        pool.indirect_dma_start(gat[k][:, j, :], None, table,
                                                bass.IndirectOffsetOnAxis(pair[:, k, 0, j:j + 1], 0)
                                                ).then_inc(rows_in[k], 16)
                walk(pool, STEPS, 0, RING, body)
                for k in range(RING):
                    pool.wait_ge(rows_in[k], 64 * ((STEPS + RING - 1 - k) // RING))

            def heads(k):
                return gat[k][:, :, :].rearrange("p j (h c) -> p j h c", h=H)

            @block.vector
            def _(dve):
                dve.memset(diff[:, :, :], -1.0e25).then_inc(init, 1)
                dve.memset(zb[:, :, :, :], 1.0).then_inc(init, 1)
                dve.memset(dd[:, :, :], NEG).then_inc(init, 1)
                dve.memset(accb[:, :, :], 0.0).then_inc(init, 1)
                dve.memset(big[:, :], -NEG).then_inc(init, 1)
                dve.wait_ge(init, 5)

                pm = pM[:, 0:J * (H + 1)].rearrange("p (j h) -> p j h", j=J)
                pd = pD[:, 0:J * 2 * H].rearrange("p (j h) -> p j h", j=J)
                per_head = lambda ap: ap.rearrange("p (h c) -> p h c", h=H)

                def body(t, k, on):
                    t1, k1 = t - 1, (k - 1) % RING
                    t3, k3 = t - 3, (k - 3) % RING
                    t4, k4 = t - 4, (k - 4) % RING
                    t7, k7 = t - 7, (k - 7) % RING
                    if on(4):
                        await_count(dve, expand, t4 + 1)
                        dve.tensor_tensor(ze[:, k4, :, :], heads(k4)[:, :, :, C], pd[:, :, 0:H],
                                          ALU.add).then_inc(shift, 1)
                    if on(0):
                        await_count(dve, pair_in[k], 2 * (t - k) + 16)
                        await_count(dve, agg, t - RING + 1)
                        dve.tensor_scalar(dloc[:, k, :], pair[:, k, 1, :], tile_f[:, bass.ds(t, 1)], None,
                                          ALU.subtract).then_inc(local, 1)
                    if on(4):
                        await_count(dve, shift, 3 * t4 + 1)
                        dve.scalar_tensor_tensor(le[:, k4, :, :], ze[:, k4, :, :], 0.2, ze[:, k4, :, :], ALU.mult,
                                                 ALU.max).then_inc(shift, 1)
                    if on(3):
                        await_count(dve, absent, t3 + 1)
                        dve.tensor_tensor(mc4[:, k3, :, :], pm[:, :, 0:H],
                                          pen[:, k3, :].unsqueeze(2).to_broadcast([P, J, H]),
                                          ALU.subtract).then_inc(upd, 1)
                    if on(4):
                        await_count(dve, shift, 3 * t4 + 2)
                        dve.tensor_tensor(se[:, k4, :, :], le[:, k4, :, :], pd[:, :, H:2 * H],
                                          ALU.subtract).then_inc(shift, 1)
                    if on(3):
                        await_count(dve, upd, UPD * t3 + 1)
                        dve.tensor_reduce(mc[:, k3, :], mc4[:, k3, :, :].rearrange("p j h -> p h j"), AX.X,
                                          ALU.max).then_inc(upd, 1)
                    if on(0):
                        await_count(dve, local, 2 * t + 1)
                        dve.tensor_tensor(hot[:, k, :, :], iota_n[:, :].unsqueeze(1).to_broadcast([P, J, P]),
                                          dloc[:, k, :].unsqueeze(2).to_broadcast([P, J, P]),
                                          ALU.is_equal).then_inc(local, 1)
                    if on(3):
                        await_count(dve, upd, UPD * t3 + 2)
                        await_count(dve, scored, t3 + 1)
                        dve.tensor_tensor(uc[:, k3, :], mc[:, k3, :], dd[:, k3, 0:H], ALU.add).then_inc(upd, 1)
                    if on(1):
                        await_count(dve, rowcopy, 2 * t1 + 1)
                        dve.tensor_tensor(diff[:, k1, 1:P], drow[:, k1, 0:P - 1], drow[:, k1, 1:P],
                                          ALU.subtract).then_inc(scan, 1)
                    if on(3):
                        await_count(dve, upd, UPD * t3 + 3)
                        dve.scalar_tensor_tensor(lc[:, k3, :], uc[:, k3, :], 0.2, uc[:, k3, :], ALU.mult,
                                                 ALU.max).then_inc(upd, 1)
                    if on(1):
                        await_count(dve, scan, 3 * t1 + 1)
                        dve.tensor_tensor_scan(smax[:, k1, :], diff[:, k1, 0:P], pX[0:J * H, k1 % 2, 0:P], 0.0,
                                               ALU.add, ALU.max).then_inc(scan, 1)
                    if on(3):
                        await_count(dve, upd, UPD * t3 + 4)
                        dve.scalar_tensor_tensor(dd[:, k3, H:2 * H], dd[:, (k3 - 1) % RING, H:2 * H],
                                                 reset[:, bass.ds(t3, 1)], lc[:, k3, :], ALU.add,
                                                 ALU.max).then_inc(upd, 1)
                    if on(7):
                        await_count(dve, accum, 2 * t7)
                        await_count(dve, factor, t7 + 1)
                        await_count(dve, stored, t7 - AR + 1)
                        a = accb[:, k7 % AR, :]
                        dve.tensor_tensor(per_head(a), per_head(accb[:, (k7 - 1) % AR, :]),
                                          rr[:, k7, :].unsqueeze(2).to_broadcast([P, H, CW]),
                                          ALU.mult).then_inc(accum, 1)
                    if on(3):
                        await_count(dve, upd, UPD * t3 + 5)
                        dve.scalar_tensor_tensor(dr[:, k3, :], dd[:, (k3 - 1) % RING, H:2 * H],
                                                 reset[:, bass.ds(t3, 1)], dd[:, k3, H:2 * H], ALU.add,
                                                 ALU.subtract).then_inc(upd, 1)
                    if on(1):
                        await_count(dve, scan, 3 * t1 + 2)
                        dve.scalar_tensor_tensor(lmax[:, k1, :], diff[:, k1, 1:P + 1], 0.0, smax[:, k1, :],
                                                 ALU.is_lt, ALU.mult).then_inc(scan, 1)
                    if on(4):
                        await_count(dve, expd, 2 * t4 + 2)
                        g = heads(k4)
                        dve.tensor_tensor(g[:, :, :, 0:C], g[:, :, :, 0:C],
                                          g[:, :, :, C:CW].to_broadcast([P, J, H, C]), ALU.mult).then_inc(msg, 1)
                    if on(7):
                        await_count(dve, accum, 2 * t7 + 1)
                        await_count(dve, agg, t7 + 1)
                        dve.tensor_tensor(a, a, pA[:, k7 % 2, 0:ROW], ALU.add).then_inc(accum, 1)
                walk(dve, STEPS, 7, RING, body, head=2)

            @block.scalar
            def _(act):
                def body(t, k, on):
                    t1, k1 = t - 1, (k - 1) % RING
                    t2, k2 = t - 2, (k - 2) % RING
                    t3, k3 = t - 3, (k - 3) % RING
                    t4, k4 = t - 4, (k - 4) % RING
                    if on(0):
                        await_count(act, local, 2 * t + 1)
                        act.activation(dsc[:, k, :, :], dloc[:, k, :].unsqueeze(2).to_broadcast([P, J, H]),
                                       ACT.Copy, scale=1.0e25).then_inc(dscaled, 1)
                    if on(4):
                        await_count(act, shift, 3 * t4 + 3)
                        act.activation(sc[:, k4, :, :], se[:, k4, :, :], ACT.Relu, scale=-1.0).then_inc(expd, 1)
                        await_count(act, expd, 2 * t4 + 1)
                        act.activation(heads(k4)[:, :, :, C], sc[:, k4, :, :], ACT.Exp, scale=-1.0).then_inc(expd, 1)
                    if on(3):
                        await_count(act, upd, UPD * t3 + 6)
                        act.activation(rr[:, k3, :], dr[:, k3, :], ACT.Exp).then_inc(factor, 1)
                    if on(2):
                        await_count(act, tomax, t2 + 1)
                        act.activation(pen[:, k2, :], pM[:, 0:J * (H + 1)].rearrange("p (j h) -> p j h", j=J)[:, :, H],
                                       ACT.Relu, scale=NEG, bias=big[:, :]).then_inc(absent, 1)
                    if on(0):
                        await_count(act, turned, 2 * t + 1)
                        act.activation(drow[:, k, :], pX[0:J * H, k % 2, P:2 * P], ACT.Copy).then_inc(rowcopy, 1)
                        await_count(act, turned, 2 * t + 2)
                        act.activation(hotT[:, k, :, :].rearrange("p j n -> p (j n)"), pH[:, :],
                                       ACT.Copy).then_inc(rowcopy, 1)
                    if on(1):
                        await_count(act, lastT, t1 + 1)
                        act.activation(zb[:, k1, :, 0:H], pL[:, 0:J * H].rearrange("p (j h) -> p j h", j=J),
                                       ACT.Copy).then_inc(lastcopy, 1)
                    if on(2):
                        i2 = act.value_load(tile_i[0:1, bass.ds(t2, 1)], min_val=0, max_val=NT - 1)
                        act.activation(dd[:, k2, 0:H], adst[:, bass.ds(i2, 1), :].rearrange("p a h -> p (a h)"),
                                       ACT.Copy).then_inc(scored, 1)
                    if on(8):
                        t8 = t - 8
                        i8 = act.value_load(tile_i[0:1, bass.ds(t8, 1)], min_val=0, max_val=NT - 1)
                        await_count(act, stored, t8, act_tick)
                        await_count(act, accum, 2 * t8 + 2, act_tick)
                        act.activation(acc[:, bass.ds(i8, 1), :].rearrange("p a n -> p (a n)"),
                                       accb[:, k % AR, :], ACT.Copy).then_inc(stored, 1)
                act.wait_ge(init, 5)
                walk(act, STEPS, 8, RING, body, head=2)
                act.wait_ge(stored, STEPS)

            @block.tensor
            def _(pe):
                def turn(t, k):
                    await_count(pe, pair_in[k], 2 * (t - k) + 16, pe_tick)
                    await_count(pe, rows_in[k], 8 * (t - k) + 64, pe_tick)
                    await_count(pe, dscaled, t + 1, pe_tick)
                    await_count(pe, scan, 3 * (t - 2) + 2, pe_tick)
                    pe.transpose(pX[0:J * H, k % 2, 0:P], heads(k)[:, :, :, C], ident[:, :])
                    pe.transpose(pX[0:J * H, k % 2, P:2 * P], dsc[:, k, :, :].rearrange("p j h -> p (j h)"),
                                 ident[:, :]).then_inc(turned, 1)
                    await_count(pe, local, 2 * t + 2, pe_tick)
                    await_count(pe, rowcopy, 2 * (t - 1) + 2, pe_tick)
                    for j in range(J):
                        last = pe.transpose(pH[:, P * j:P * j + P], hot[:, k, j, :], ident[:, :])
                    last.then_inc(turned, 1)

                def turn_last(t, k):
                    await_count(pe, scan, 3 * t + 3, pe_tick)
                    await_count(pe, lastcopy, t, pe_tick)
                    pe.transpose(pL[:, 0:J * H], lmax[:, k, :], ident[0:J * H, 0:J * H]).then_inc(lastT, 1)

                def chunk_max(t, k):
                    await_count(pe, lastcopy, t + 1, pe_tick)
                    await_count(pe, upd, UPD * (t - 1) + 1, pe_tick)
                    for j in range(J):
                        o = j * (H + 1)
                        last = pe.matmul(pM[:, o:o + H + 1], hot[:, k, j, :], zb[:, k, j, :], start=True,
                                         stop=True)
                    last.then_inc(tomax, 1)

                def expand_nodes(t, k):
                    await_count(pe, scored, t + 1, pe_tick)
                    await_count(pe, upd, UPD * t + 5, pe_tick)
                    await_count(pe, rowcopy, 2 * t + 2, pe_tick)
                    await_count(pe, shift, 3 * (t - 1) + 3, pe_tick)
                    for j in range(J):
                        o = j * 2 * H
                        last = pe.matmul(pD[:, o:o + 2 * H], hotT[:, k, j, :], dd[:, k, :], start=True,
                                         stop=True)
                    last.then_inc(expand, 1)

                def aggregate(t, k):
                    await_count(pe, msg, t + 1, pe_tick)
                    await_count(pe, accum, 2 * (t - 2) + 2, pe_tick)
                    for j in range(J):
                        last = pe.matmul(pA[:, k % 2, 0:ROW], hot[:, k, j, :], gat[k][:, j, :], start=(j == 0),
                                         stop=(j == J - 1))
                    last.then_inc(agg, 1)

                def body(t, k, on):
                    if on(6):
                        aggregate(t - 6, (k - 6) % RING)
                    if on(2):
                        chunk_max(t - 2, (k - 2) % RING)
                    if on(3):
                        expand_nodes(t - 3, (k - 3) % RING)
                    if on(0):
                        turn(t, k)
                    if on(1):
                        turn_last(t - 1, (k - 1) % RING)
                walk(pe, STEPS, 6, RING, body)

        with ExitStack() as ctx:
            s = lambda name, shape, dt=F32: sb("m_" + name, shape, dt, ctx)
            R = 4
            wq = s("wq", [P, 2, D])
            w1 = s("w1", [P, 2, D])
            w2 = s("w2", [P, 2, D])
            wgate = s("wgate", [P, 2, X])
            b1c = s("b1c", [P, 2])
            VEC = {n: s(n, [P, D]) for n in ("ln1g", "ln1b", "ln2g", "ln2b", "b2", "gbias")}
            gateb = s("gateb", [P, X])
            eps = s("eps", [P, 1])
            xt, xn, tt, x1p, x1c, x1, gnn, nb, x1b, yb, yc, yn, x2, x3 = (
                s(n, [P, R, D]) for n in ("xt", "xn", "tt", "x1p", "x1c", "x1", "gnn", "nb", "x1b", "yb", "yc",
                                          "yn", "x2", "x3"))
            xnT, eq, rq, qf, x1T, hT, x3T = (
                s(n, [P, R, 2, P]) for n in ("xnT", "eq", "rq", "qf", "x1T", "hT", "x3T"))
            den, zi, gden, gzi = (s(n, [P, R, H]) for n in ("den", "zi", "gden", "gzi"))
            st, mv, ve, rstd = ([s(f"{n}{i}", [P, R, w]) for i in range(3)]
                                for n, w in (("st", 6), ("mv", 2), ("ve", 1), ("rstd", 1)))
            lg = s("lg", [P, R, X])
            v8 = s("v8", [P, R, 8])
            i8 = s("i8", [P, R, 8], U32)
            zeros = s("zeros", [P, D])
            ps = ctx.enter_context(nc.psum_tensor("m_ps", [P, 8, 512], F32))
            p_xT, p_q, p_att, p_x1T, p_h, p_y, p_x3T, p_lg = (ps[:, b, :] for b in range(8))
            sem = lambda n: ctx.enter_context(nc.semaphore("m_" + n))
            w_in = sem("weights_in")
            x_in = [sem(f"x_in{k}") for k in range(R)]
            x2_out = [sem(f"x2_out{k}") for k in range(R)]
            zeroed, slots_zero, eps_set = sem("zeroed"), sem("slots_zeroed"), sem("eps_set")
            turned, qprod, attprod, x1turned, hprod, yprod, x3turned, gateprod = (
                sem(n) for n in ("xn_turned", "q_product", "attention_product", "x1_turned", "hidden_product",
                                 "mlp_product", "x3_turned", "gate_product"))
            xT_ready, q_act, x1T_ready, gelu, x3T_ready, kept = (
                sem(n) for n in ("xnT_ready", "q_activated", "x1T_ready", "gelu", "x3T_ready", "x3_kept"))
            qfs, att, aff, gat, mlp, res, nrm, top = (
                sem(n) for n in ("q_features", "attention", "x1_affine", "gat_part", "mlp_sum", "residual",
                                 "x3_normalised", "top2"))
            ATT, AFF, GAT, MLP, RES, TOP = 6, 3, 5, 3, 5, 5
            rooted = [sem(f"rooted{i}") for i in range(3)]
            block = ctx.enter_context(nc.Block())

            @block.gpsimd
            def _(pool):
                pool.memset(eps[:, :], LN_EPS).then_inc(eps_set, 1)
                pool.wait_ge(eps_set, 1)

                def body(t, k, on):
                    for i, lag, stats, per in ((1, 4, mlp, MLP), (2, 5, res, RES), (0, 1, att, ATT)):
                        if on(lag):
                            q = (k - lag) % R
                            await_count(pool, stats, per * (t - lag) + per)
                            pool.tensor_tensor(ve[i][:, q, :], mv[i][:, q, 1:2], eps[:, :], ALU.add
                                               ).then_inc(rooted[i], 1)
                            await_count(pool, rooted[i], 2 * (t - lag) + 1)
                            pool.tensor_tensor(rstd[i][:, q, :], ve[i][:, q, :], mhalf[:, :], ALU.pow
                                               ).then_inc(rooted[i], 1)
                walk(pool, NT, 5, R, body, head=3)

            @block.sync
            def _(sp):
                for dst, src in ((wq, wqkvT[:, 0:D]), (w1, w1T), (w2, w2T), (wgate, gate_w)):
                    sp.dma_start(dst[:, :, :], src.rearrange("(k p) n -> p k n", p=P)).then_inc(w_in, 16)
                with nc.allow_non_contiguous_dma(reason="a bias of 256 floats, once"):
                    sp.dma_start(b1c[:, :], b1.rearrange("(k p) -> p k", p=P)).then_inc(w_in, 16)
                for n, v in (("ln1g", ln1g), ("ln1b", ln1b), ("ln2g", ln2g), ("ln2b", ln2b), ("b2", b2),
                             ("gbias", gbias)):
                    sp.dma_start(VEC[n][:, :], v.partition_broadcast(P)).then_inc(w_in, 16)
                sp.dma_start(gateb[:, :], gate_b.partition_broadcast(P)).then_inc(w_in, 16)
                sp.wait_ge(zeroed, 1)
                sp.dma_start(slots_d.rearrange("(t p) n -> p t n", p=P),
                             zeros[:, :].unsqueeze(1).to_broadcast([P, XT, D])).then_inc(slots_zero, 16)

                def body(t, k, on):
                    if on(0):
                        await_count(sp, gat, GAT * (t - R) + GAT, sp_tick)
                        sp.dma_start(xt[:, k, :], x[bass.ds(t * P, P), :]).then_inc(x_in[k], 16)
                        sp.dma_start(xn[:, k, :], xn_d[bass.ds(t * P, P), :]).then_inc(x_in[k], 16)
                    if on(6):
                        t6, k6 = t - 6, (k - 6) % R
                        await_count(sp, res, RES * t6 + 3, sp_tick)
                        sp.dma_start(x2_d[bass.ds(t6 * P, P), :], x2[:, k6, :]).then_inc(x2_out[k6], 16)
                walk(sp, NT, 6, R, body, head=3)
                for k in range(R):
                    sp.wait_ge(x2_out[k], 16 * ((NT + R - 1 - k) // R))
                sp.wait_ge(slots_zero, 16)

            @block.vector
            def _(dve):
                dve.memset(zeros[:, :], 0.0).then_inc(zeroed, 1)
                dve.wait_ge(w_in, 16 * 12)
                hd = lambda ap: ap.rearrange("p (h c) -> p h c", h=H)
                halves = lambda ap: ap.rearrange("p (c h) -> p c h", c=2)
                p_at = p_att[:, 0:2 * (P + 4)].rearrange("p (c n) -> p c n", c=2)

                def body(t, k, on):
                    t1, k1 = t - 1, (k - 1) % R
                    t2, k2 = t - 2, (k - 2) % R
                    t4, k4 = t - 4, (k - 4) % R
                    t5, k5 = t - 5, (k - 5) % R
                    t6, k6 = t - 6, (k - 6) % R
                    t7, k7 = t - 7, (k - 7) % R
                    if on(2):
                        a = acc[:, bass.ds(t2, 1), :].rearrange("p a n -> p (a n)")
                    two = lambda tab: tab[:, bass.ds(t7, 1), :].rearrange("p a n -> p (a n)")
                    if on(6):
                        await_count(dve, rooted[2], 2 * t6 + 2)
                        dve.tensor_scalar(x3[:, k6, :], x2[:, k6, :], mv[2][:, k6, 0:1], rstd[2][:, k6, :],
                                          ALU.subtract, ALU.mult).then_inc(nrm, 1)
                    if on(4):
                        await_count(dve, aff, AFF * t4 + 3)
                        await_count(dve, yprod, t4 + 1)
                        dve.tensor_tensor(yb[:, k4, :], p_y[:, 0:D], x1b[:, k4, :], ALU.add).then_inc(mlp, 1)
                    if on(7):
                        await_count(dve, gateprod, t7 + 1)
                        dve.tensor_tensor(lg[:, k7, :], p_lg[:, 0:X], gateb[:, :], ALU.add).then_inc(top, 1)
                    if on(5):
                        await_count(dve, rooted[1], 2 * t5 + 2)
                        dve.scalar_tensor_tensor(yc[:, k5, :], yb[:, k5, :], mv[1][:, k5, 0:1], VEC["ln2g"][:, :],
                                                 ALU.subtract, ALU.mult).then_inc(res, 1)
                    if on(4):
                        await_count(dve, mlp, MLP * t4 + 1, dve_tick)
                        dve.bn_stats(st[1][:, k4, :], yb[:, k4, :]).then_inc(mlp, 1)
                    if on(2):
                        await_count(dve, rooted[0], 2 * t2 + 2)
                        dve.scalar_tensor_tensor(x1c[:, k2, :], x1p[:, k2, :], mv[0][:, k2, 0:1], VEC["ln1g"][:, :],
                                                 ALU.subtract, ALU.mult).then_inc(aff, 1)
                    if on(7):
                        await_count(dve, top, TOP * t7 + 1, dve_tick)
                        dve.max(v8[:, k7, :], lg[:, k7, :]).then_inc(top, 1)
                    if on(5):
                        await_count(dve, res, RES * t5 + 1)
                        dve.scalar_tensor_tensor(yn[:, k5, :], yc[:, k5, :], rstd[1][:, k5, :], VEC["ln2b"][:, :],
                                                 ALU.mult, ALU.add).then_inc(res, 1)
                    if on(4):
                        await_count(dve, mlp, MLP * t4 + 2, dve_tick)
                        dve.bn_aggr(mv[1][:, k4, :], st[1][:, k4, :]).then_inc(mlp, 1)
                    if on(2):
                        await_count(dve, aff, AFF * t2 + 1)
                        dve.scalar_tensor_tensor(x1[:, k2, :], x1c[:, k2, :], rstd[0][:, k2, :], VEC["ln1b"][:, :],
                                                 ALU.mult, ALU.add).then_inc(aff, 1)
                    if on(7):
                        await_count(dve, top, TOP * t7 + 2, dve_tick)
                        dve.max_index(i8[:, k7, :], v8[:, k7, :], lg[:, k7, :]).then_inc(top, 1)
                    if on(1):
                        await_count(dve, attprod, t1 + 1)
                        dve.tensor_scalar(halves(den[:, k1, :]), p_at[:, :, P:P + 4], 1e-6, None,
                                          ALU.add).then_inc(att, 1)
                    if on(5):
                        await_count(dve, res, RES * t5 + 2)
                        await_count(dve, gat, GAT * t5 + 5)
                        await_count(dve, x2_out[k5], 4 * (t5 - k5))
                        dve.tensor_tensor(x2[:, k5, :], nb[:, k5, :], yn[:, k5, :], ALU.add).then_inc(res, 1)
                    if on(2):
                        dve.tensor_scalar(gden[:, k2, :], hd(a)[:, :, C], 1e-16, None, ALU.add).then_inc(gat, 1)
                    if on(1):
                        await_count(dve, att, ATT * t1 + 1)
                        dve.reciprocal(zi[:, k1, :], den[:, k1, :]).then_inc(att, 1)
                    if on(5):
                        await_count(dve, res, RES * t5 + 3, dve_tick)
                        dve.bn_stats(st[2][:, k5, :], x2[:, k5, :]).then_inc(res, 1)
                    if on(2):
                        await_count(dve, gat, GAT * t2 + 1)
                        dve.reciprocal(gzi[:, k2, :], gden[:, k2, :]).then_inc(gat, 1)
                    if on(1):
                        await_count(dve, att, ATT * t1 + 2)
                        dve.tensor_tensor(tt[:, k1, :].rearrange("p (c h n) -> p c h n", c=2, h=4),
                                          p_at[:, :, 0:P].rearrange("p c (h n) -> p c h n", h=4),
                                          halves(zi[:, k1, :]).unsqueeze(3).to_broadcast([P, 2, 4, C]),
                                          ALU.mult).then_inc(att, 1)
                    if on(5):
                        await_count(dve, res, RES * t5 + 4, dve_tick)
                        dve.bn_aggr(mv[2][:, k5, :], st[2][:, k5, :]).then_inc(res, 1)
                    if on(2):
                        await_count(dve, gat, GAT * t2 + 2, dve_tick)
                        dve.tensor_tensor(hd(gnn[:, k2, :]), hd(a)[:, :, 0:C],
                                          gzi[:, k2, :].unsqueeze(2).to_broadcast([P, H, C]),
                                          ALU.mult).then_inc(gat, 1)
                    if on(1):
                        await_count(dve, att, ATT * t1 + 3)
                        dve.tensor_tensor(x1p[:, k1, :], tt[:, k1, :], xn[:, k1, :], ALU.add).then_inc(att, 1)
                    if on(7):
                        await_count(dve, top, TOP * t7 + 3, dve_tick)
                        dve.tensor_scalar(two(top_v), v8[:, k7, 0:2], 1.0, None, ALU.mult).then_inc(top, 1)
                    if on(2):
                        await_count(dve, gat, GAT * t2 + 3)
                        dve.tensor_tensor(gnn[:, k2, :], gnn[:, k2, :], VEC["gbias"][:, :], ALU.add).then_inc(gat, 1)
                    if on(1):
                        await_count(dve, att, ATT * t1 + 4, dve_tick)
                        dve.bn_stats(st[0][:, k1, :], x1p[:, k1, :]).then_inc(att, 1)
                    if on(0):
                        await_count(dve, q_act, 2 * t + 2)
                        dve.scalar_tensor_tensor(qf[:, k, :, :], eq[:, k, :, :], 1.0, rq[:, k, :, :], ALU.min,
                                                 ALU.add).then_inc(qfs, 1)
                    if on(1):
                        await_count(dve, att, ATT * t1 + 5, dve_tick)
                        dve.bn_aggr(mv[0][:, k1, :], st[0][:, k1, :]).then_inc(att, 1)
                    if on(2):
                        await_count(dve, gat, GAT * t2 + 4)
                        dve.scalar_tensor_tensor(nb[:, k2, :], gnn[:, k2, :], 0.0, xt[:, k2, :], ALU.max,
                                                 ALU.add).then_inc(gat, 1)
                    if on(2):
                        await_count(dve, aff, AFF * t2 + 2)
                        dve.tensor_tensor(x1b[:, k2, :], x1[:, k2, :], VEC["b2"][:, :], ALU.add).then_inc(aff, 1)
                    if on(7):
                        dve.tensor_scalar(two(top_i), i8[:, k7, 0:2], 1.0, None, ALU.mult).then_inc(top, 1)
                walk(dve, NT, 7, R, body, head=3)

            @block.tensor
            def _(pe):
                pe.wait_ge(w_in, 16 * 12)

                def turn(dst, src):
                    for c in range(2):
                        last = pe.transpose(dst[:, P * c:P * c + P], src[:, P * c:P * c + P], ident[:, :])
                    return last

                def columns(dst, w, srcT):
                    for o in range(2):
                        for c in range(2):
                            last = pe.matmul(dst[:, P * o:P * o + P], w[:, c, P * o:P * o + P], srcT[:, c, :],
                                             start=(c == 0), stop=(c == 1))
                    return last

                def rows(dst, srcT, w):
                    for c in range(2):
                        last = pe.matmul(dst, srcT[:, c, :], w[:, c, :], start=(c == 0), stop=(c == 1))
                    return last

                def body(t, k, on):
                    w = lambda sem, v: await_count(pe, sem, v, pe_tick)
                    t1, k1 = t - 1, (k - 1) % R
                    t2, k2 = t - 2, (k - 2) % R
                    t3, k3 = t - 3, (k - 3) % R
                    t6, k6 = t - 6, (k - 6) % R
                    if on(0):
                        w(x_in[k], 8 * (t - k) + 32)
                        w(xT_ready, t)
                        turn(p_xT, xn[:, k, :]).then_inc(turned, 1)
                    if on(1):
                        w(qfs, t1 + 1)
                        w(att, ATT * (t1 - 1) + 3)
                        for c in range(2):
                            last = pe.matmul(p_att[:, (P + 4) * c:(P + 4) * (c + 1)], qf[:, k1, c, :],
                                             kvb[:, c, :], start=True, stop=True)
                        last.then_inc(attprod, 1)
                    if on(6):
                        w(nrm, t6 + 1)
                        w(x3T_ready, t6)
                        turn(p_x3T, x3[:, k6, :]).then_inc(x3turned, 1)
                    if on(0):
                        w(xT_ready, t + 1)
                        w(q_act, 2 * t)
                        columns(p_q, wq, xnT[:, k, :, :]).then_inc(qprod, 1)
                    if on(3):
                        w(gelu, 2 * t3 + 2)
                        w(mlp, MLP * (t3 - 1) + 1)
                        rows(p_y[:, 0:D], hT[:, k3, :, :], w2).then_inc(yprod, 1)
                    if on(6):
                        w(x3T_ready, t6 + 1)
                        w(top, TOP * (t6 - 1) + 1)
                        rows(p_lg[:, 0:X], x3T[:, k6, :, :], wgate).then_inc(gateprod, 1)
                    if on(2):
                        w(aff, AFF * t2 + 2)
                        w(x1T_ready, t2)
                        turn(p_x1T, x1[:, k2, :]).then_inc(x1turned, 1)
                        w(x1T_ready, t2 + 1)
                        w(gelu, 2 * t2)
                        columns(p_h, w1, x1T[:, k2, :, :]).then_inc(hprod, 1)
                walk(pe, NT, 6, R, body, head=3)

            @block.scalar
            def _(act):
                act.wait_ge(w_in, 16 * 12)
                both = lambda ap, k: ap[:, k, :, :].rearrange("p c n -> p (c n)")

                def body(t, k, on):
                    t2, k2 = t - 2, (k - 2) % R
                    t6, k6 = t - 6, (k - 6) % R
                    if on(0):
                        await_count(act, turned, t + 1)
                        act.activation(both(xnT, k), p_xT[:, 0:D], ACT.Copy).then_inc(xT_ready, 1)
                    if on(6):
                        await_count(act, x3turned, t6 + 1)
                        act.activation(both(x3T, k6), p_x3T[:, 0:D], ACT.Copy).then_inc(x3T_ready, 1)
                    if on(0):
                        await_count(act, qprod, t + 1)
                        act.activation(both(eq, k), p_q[:, 0:D], ACT.Exp).then_inc(q_act, 1)
                        act.activation(both(rq, k), p_q[:, 0:D], ACT.Relu).then_inc(q_act, 1)
                    if on(6):
                        await_count(act, nrm, t6 + 1, act_tick)
                        act.activation(acc[:, bass.ds(t6, 1), 0:D].rearrange("p a n -> p (a n)"), x3[:, k6, :],
                                       ACT.Copy).then_inc(kept, 1)
                    if on(2):
                        await_count(act, x1turned, t2 + 1)
                        act.activation(both(x1T, k2), p_x1T[:, 0:D], ACT.Copy).then_inc(x1T_ready, 1)
                        await_count(act, hprod, t2 + 1)
                        for c in range(2):
                            act.activation(hT[:, k2, c, :], p_h[:, P * c:P * c + P], ACT.Gelu,
                                           bias=b1c[:, c:c + 1]).then_inc(gelu, 1)
                walk(act, NT, 6, R, body, head=3)
                act.wait_ge(gelu, 2 * NT)
                act.wait_ge(kept, NT)

        with ExitStack() as ctx:
            s = lambda name, shape, dt=F32: sb("r_" + name, shape, dt, ctx)
            oh = s("oh", [P, 2, NT, X])
            both = s("both", [P, NT, X])
            tot = s("tot", [P, NT, X])
            cum = s("cum", [P, NT, X])
            sl = s("sl", [P, NT, X])
            pick = s("pick", [P, NT, X])
            cnt = s("cnt", [P, X])
            cnt_i = s("cnt_i", [P, X], I32)
            cumx = s("cumx", [P, X])
            base = s("base", [P, X])
            slot_f = s("slot_f", [P, 2, NT])
            dv = s("dv", [P, NT])
            ev = s("ev", [P, NT])
            ev1 = s("ev1", [P, NT])
            past = s("past", [1, XT, X])
            te = s("te", [1, XT])
            R = 4
            stage = [s(f"stage{k}", [P, D]) for k in range(R)]
            sidx = [s(f"sidx{k}", [P, 2], I32) for k in range(R)]
            pr = ctx.enter_context(nc.psum_tensor("r_pr", [P, 4, 512], F32))
            sem = lambda n: ctx.enter_context(nc.semaphore("r_" + n))
            chain, hots, sums, diffs, exps = sem("ops"), sem("one_hots"), sem("prefix_sums"), sem("diffs"), sem("exps")
            rows_staged, idx_staged = sem("rows_staged"), sem("idx_staged")
            scattered = [sem(f"scattered{k}") for k in range(R)]
            block = ctx.enter_context(nc.Block())
            HALF = 25 * X

            @block.vector
            def _(dve):
                done = [0]

                def link(ins):
                    done[0] += 1
                    ins.then_inc(chain, 1)
                    dve.wait_ge(chain, done[0])

                for k in range(2):
                    link(dve.tensor_tensor(oh[:, k, :, :], iota_n[:, 0:X].unsqueeze(1).to_broadcast([P, NT, X]),
                                           top_i[:, :, k:k + 1].to_broadcast([P, NT, X]), ALU.is_equal))
                dve.tensor_tensor(both[:, :, :], oh[:, 0, :, :], oh[:, 1, :, :], ALU.add).then_inc(hots, 1)
                dve.tensor_tensor(dv[:, :], top_v[:, :, 1], top_v[:, :, 0], ALU.subtract).then_inc(diffs, 1)
                dve.wait_ge(exps, 1)
                link(dve.tensor_scalar(ev1[:, :], ev[:, :], 1.0, None, ALU.add))
                link(dve.reciprocal(dv[:, :], ev1[:, :]))
                link(dve.tensor_copy(wtop[:, :, 0], dv[:, :]))
                link(dve.tensor_tensor(wtop[:, :, 1], dv[:, :], ev[:, :], ALU.mult))
                dve.wait_ge(sums, 1)
                fl = lambda ap: ap[:, :, :].rearrange("p t x -> p (t x)")
                link(dve.tensor_copy(fl(tot)[:, 0:HALF], pr[:, 2, 0:HALF]))
                link(dve.tensor_copy(fl(tot)[:, HALF:NT * X], pr[:, 3, 0:NT * X - HALF]))
                for e in range(X):
                    link(dve.tensor_tensor_scan(cum[:, :, e], tot[:, :, e], ones[:, 0:NT], 0.0, ALU.add, ALU.mult))
                link(dve.tensor_scalar(cnt_i[:, :], cum[:, NT - 1, :], float(P - 1), None, ALU.add))
                link(dve.tensor_scalar(cnt_i[:, :], cnt_i[:, :], P.bit_length() - 1, None, ALU.logical_shift_right))
                link(dve.tensor_copy(cnt[:, :], cnt_i[:, :]))
                link(dve.tensor_tensor_scan(cumx[:, :], cnt[:, :], ones[:, 0:X], 0.0, ALU.add, ALU.mult))
                link(dve.tensor_tensor(base[:, :], cumx[:, :], cnt[:, :], ALU.subtract))
                link(dve.tensor_tensor(sl[:, :, :], cum[:, :, :], tot[:, :, :], ALU.subtract))
                link(dve.tensor_tensor(fl(sl)[:, 0:HALF], fl(sl)[:, 0:HALF], pr[:, 0, 0:HALF], ALU.add))
                link(dve.tensor_tensor(fl(sl)[:, HALF:NT * X], fl(sl)[:, HALF:NT * X], pr[:, 1, 0:NT * X - HALF],
                                       ALU.add))
                link(dve.scalar_tensor_tensor(sl[:, :, :], base[:, :].unsqueeze(1).to_broadcast([P, NT, X]), float(P),
                                              sl[:, :, :], ALU.mult, ALU.add))
                for k in range(2):
                    link(dve.tensor_tensor(pick[:, :, :], sl[:, :, :], oh[:, k, :, :], ALU.mult))
                    link(dve.tensor_reduce(slot_f[:, k, :], pick[:, :, :], AX.X, ALU.add))
                    link(dve.tensor_copy(slot[:, :, k], slot_f[:, k, :]))
                link(dve.tensor_tensor(past[:, :, :], iota_n[0:1, 0:XT].unsqueeze(2).to_broadcast([1, XT, X]),
                                       cumx[0:1, :].unsqueeze(1).to_broadcast([1, XT, X]), ALU.is_ge))
                link(dve.tensor_reduce(te[:, :], past[:, :, :], AX.X, ALU.add))
                link(dve.tensor_scalar(texp[:, :], te[:, :], float(X - 1), None, ALU.min))

                def body(t, k, on):
                    await_count(dve, scattered[k], (t - k - R) * (32 // R) + 32, dve_tick)
                    dve.tensor_copy(sidx[k][:, :], slot[:, bass.ds(t, 1), :].rearrange("p a n -> p (a n)")
                                    ).then_inc(idx_staged, 1)
                walk(dve, NT, 0, R, body)

            @block.tensor
            def _(pe):
                pe.wait_ge(hots, 1)
                flat = both[:, :, :].rearrange("p t x -> p (t x)")
                for a, w in ((0, lower), (2, ones)):
                    pe.matmul(pr[:, a, 0:HALF], w[:, :], flat[:, 0:HALF], start=True, stop=True)
                    last = pe.matmul(pr[:, a + 1, 0:NT * X - HALF], w[:, :], flat[:, HALF:NT * X], start=True, stop=True)
                last.then_inc(sums, 1)

            @block.scalar
            def _(act):
                act.wait_ge(diffs, 1)
                act.activation(ev[:, :], dv[:, :], ACT.Exp).then_inc(exps, 1)

                def body(t, k, on):
                    await_count(act, scattered[k], (t - k - R) * (32 // R) + 32, act_tick)
                    act.activation(stage[k][:, :], acc[:, bass.ds(t, 1), 0:D].rearrange("p a n -> p (a n)"),
                                   ACT.Copy).then_inc(rows_staged, 1)
                walk(act, NT, 0, R, body)

            @block.gpsimd
            def _(pool):
                def body(t, k, on):
                    await_count(pool, rows_staged, t + 1, pool_tick)
                    await_count(pool, idx_staged, t + 1, pool_tick)
                    for c in range(2):
                        pool.indirect_dma_start(slots_d, bass.IndirectOffsetOnAxis(sidx[k][:, c:c + 1], 0),
                                                stage[k][:, :], None).then_inc(scattered[k], 16)
                walk(pool, NT, 0, R, body)
                for k in range(R):
                    pool.wait_ge(scattered[k], 32 * ((NT + R - 1 - k) // R))

        with ExitStack() as ctx:
            s = lambda name, shape, dt=F32: sb("x_" + name, shape, dt, ctx)
            R = 4
            w1e = s("w1e", [P, R, 2, F])
            w2e = s("w2e", [P, R, 4, D])
            b1a = s("b1a", [P, X * 4])
            b2a = s("b2a", [P, X, D])
            xs = s("xs", [P, R, D])
            xsT = s("xsT", [P, R, 2, P])
            hT = s("hT", [P, R, 4, P])
            ye = s("ye", [P, R, D])
            pT = ctx.enter_context(nc.psum_tensor("x_pT", [P, 2, 512], F32))
            pH = ctx.enter_context(nc.psum_tensor("x_pH", [P, 2, 512], F32))
            pY = ctx.enter_context(nc.psum_tensor("x_pY", [P, 2, 512], F32))
            sem = lambda n: ctx.enter_context(nc.semaphore("x_" + n))
            b_in = sem("biases_in")
            rows_in = [sem(f"rows_in{k}") for k in range(R)]
            w1_in = [sem(f"w1_in{k}") for k in range(R)]
            w2_in = [sem(f"w2_in{k}") for k in range(R)]
            out_ = [sem(f"out{k}") for k in range(R)]
            turned, tcopied, hid, relu, prod, summed = (sem("turned"), sem("turned_copied"), sem("hidden"),
                                                        sem("relu"), sem("product"), sem("bias_added"))
            block = ctx.enter_context(nc.Block())
            UN = R

            @block.sync
            def _(sp):
                sp.dma_start(b1a[:, :], eb1).then_inc(b_in, 16)
                sp.dma_start(b2a[:, :, :].rearrange("p x n -> p (x n)"),
                             eb2.rearrange("x n -> (x n)").partition_broadcast(P)).then_inc(b_in, 16)

                def body(t, k, on):
                    t1, k1 = t - 1, (k - 1) % R
                    t2, k2 = t - 2, (k - 2) % R
                    if on(0):
                        await_count(sp, turned, t - R + 1, sp_tick)
                        sp.dma_start(xs[:, k, :], slots_d[bass.ds(t * P, P), :]).then_inc(rows_in[k], 16)
                    if on(1):
                        e = sp.value_load(texp[0:1, bass.ds(t1, 1)], min_val=0, max_val=X - 1)
                        await_count(sp, hid, t1 - R + 1, sp_tick)
                        sp.dma_start(w1e[:, k1, :, :], ew1[bass.ds(e, 1), :, :].rearrange(
                            "a (k p) f -> p (a k) f", p=P)).then_inc(w1_in[k1], 16)
                    if on(2):
                        e = sp.value_load(texp[0:1, bass.ds(t2, 1)], min_val=0, max_val=X - 1)
                        await_count(sp, prod, t2 - R + 1, sp_tick)
                        sp.dma_start(w2e[:, k2, :, :], ew2[bass.ds(e, 1), :, :].rearrange(
                            "a (k p) f -> p (a k) f", p=P)).then_inc(w2_in[k2], 16)
                walk(sp, XT, 2, UN, body, head=2)

            @block.tensor
            def _(pe):
                def body(t, k, on):
                    w = lambda sem, v: await_count(pe, sem, v, pe_tick)
                    if on(0):
                        q, b = k % R, k % 2
                        w(rows_in[q], 4 * (t - q) + 16)
                        w(tcopied, t - 1)
                        for c in range(2):
                            last = pe.transpose(pT[:, b, P * c:P * c + P], xs[:, q, P * c:P * c + P], ident[:, :])
                        last.then_inc(turned, 1)
                    if on(1):
                        t1, q, b = t - 1, (k - 1) % R, (k - 1) % 2
                        w(w1_in[q], 4 * (t1 - q) + 16)
                        w(tcopied, t1 + 1)
                        w(relu, 4 * (t1 - 2) + 4)
                        for o in range(4):
                            for c in range(2):
                                last = pe.matmul(pH[:, b, P * o:P * o + P], w1e[:, q, c, P * o:P * o + P],
                                                 xsT[:, q, c, :], start=(c == 0), stop=(c == 1))
                        last.then_inc(hid, 1)
                    if on(2):
                        t2, q, b = t - 2, (k - 2) % R, (k - 2) % 2
                        w(w2_in[q], 4 * (t2 - q) + 16)
                        w(relu, 4 * t2 + 4)
                        w(summed, t2 - 1)
                        for c in range(4):
                            last = pe.matmul(pY[:, b, 0:D], hT[:, q, c, :], w2e[:, q, c, :], start=(c == 0),
                                             stop=(c == 3))
                        last.then_inc(prod, 1)
                walk(pe, XT, 2, UN, body)

            @block.scalar
            def _(act):
                act.wait_ge(b_in, 32)

                def body(t, k, on):
                    if on(0):
                        await_count(act, turned, t + 1)
                        await_count(act, hid, t - R + 1)
                        act.activation(xsT[:, k % R, :, :].rearrange("p c n -> p (c n)"), pT[:, k % 2, 0:D],
                                       ACT.Copy).then_inc(tcopied, 1)
                    if on(1):
                        t1, q, b = t - 1, (k - 1) % R, (k - 1) % 2
                        e = act.value_load(texp[0:1, bass.ds(t1, 1)], min_val=0, max_val=X - 1)
                        await_count(act, prod, t1 - R + 2, act_tick)
                        await_count(act, hid, t1 + 1, act_tick)
                        for o in range(4):
                            act.activation(hT[:, q, o, :], pH[:, b, P * o:P * o + P], ACT.Relu,
                                           bias=b1a[:, bass.ds(e * 4 + o, 1)]).then_inc(relu, 1)
                walk(act, XT, 1, UN, body)

            @block.vector
            def _(dve):
                dve.wait_ge(b_in, 32)

                def body(t, k, on):
                    if on(0):
                        e = dve.value_load(texp[0:1, bass.ds(t, 1)], min_val=0, max_val=X - 1)
                        await_count(dve, out_[k], 4 * (t - k))
                        await_count(dve, prod, t + 1)
                        dve.tensor_tensor(ye[:, k % R, :], pY[:, k % 2, 0:D],
                                          b2a[:, bass.ds(e, 1), :].rearrange("p a n -> p (a n)"), ALU.add
                                          ).then_inc(summed, 1)
                walk(dve, XT, 0, UN, body)

            @block.gpsimd
            def _(pool):
                def body(t, k, on):
                    await_count(pool, summed, t + 1, pool_tick)
                    pool.dma_start(eout_d[bass.ds(t * P, P), :], ye[:, k % R, :]).then_inc(out_[k % R], 16)
                walk(pool, XT, 0, UN, body)
                for k in range(R):
                    pool.wait_ge(out_[k], 16 * ((XT + R - 1 - k) // R))

        with ExitStack() as ctx:
            s = lambda name, shape, dt=F32: sb("c_" + name, shape, dt, ctx)
            R = 4
            gb = s("gb", [P, D])
            bb = s("bb", [P, D])
            sidx = [s(f"sidx{k}", [P, 2], I32) for k in range(R)]
            eo = [s(f"eo{k}", [P, 2, D]) for k in range(R)]
            x2 = s("x2", [P, R, D])
            y1 = s("y1", [P, R, D])
            y2 = s("y2", [P, R, D])
            z1 = s("z1", [P, R, D])
            z2 = s("z2", [P, R, D])
            st = s("st", [P, R, 6])
            mv = s("mv", [P, R, 2])
            ve = s("ve", [P, R, 1])
            rstd = s("rstd", [P, R, 1])
            o = s("o", [P, R, D])
            sem = lambda n: ctx.enter_context(nc.semaphore("c_" + n))
            w_in = sem("affine_in")
            eo_in = [sem(f"expert_rows_in{k}") for k in range(R)]
            x2_in = [sem(f"x2_in{k}") for k in range(R)]
            out_ = [sem(f"out{k}") for k in range(R)]
            staged, rooted = sem("index_staged"), sem("rooted")
            summed, done = sem("rows_summed"), sem("results_done")
            block = ctx.enter_context(nc.Block())
            SUM, FIN = 5, 3

            @block.sync
            def _(sp):
                sp.dma_start(gb[:, :], gamma.partition_broadcast(P)).then_inc(w_in, 16)
                sp.dma_start(bb[:, :], beta.partition_broadcast(P)).then_inc(w_in, 16)

                def body(t, k, on):
                    if on(0):
                        await_count(sp, done, FIN * (t - R) + FIN, sp_tick)
                        sp.dma_start(x2[:, k, :], x2_d[bass.ds(t * P, P), :]).then_inc(x2_in[k], 16)
                    if on(3):
                        t3, k3 = t - 3, (k - 3) % R
                        await_count(sp, done, FIN * t3 + FIN, sp_tick)
                        sp.dma_start(out[bass.ds(t3 * P, P), :], o[:, k3, :]).then_inc(out_[k3], 16)
                walk(sp, NT, 3, R, body, head=2)
                for k in range(R):
                    sp.wait_ge(out_[k], 16 * ((NT + R - 1 - k) // R))

            @block.scalar
            def _(act):
                def body(t, k, on):
                    await_count(act, eo_in[k], 8 * (t - k), act_tick)
                    act.activation(sidx[k][:, :], slot[:, bass.ds(t, 1), :].rearrange("p a n -> p (a n)"),
                                   ACT.Copy).then_inc(staged, 1)
                walk(act, NT, 0, R, body)

            @block.gpsimd
            def _(pool):
                def body(t, k, on):
                    if on(0):
                        await_count(pool, staged, t + 1, pool_tick)
                        await_count(pool, summed, SUM * (t - R) + 2, pool_tick)
                        for c in range(2):
                            pool.indirect_dma_start(eo[k][:, c, :], None, eout_d,
                                                    bass.IndirectOffsetOnAxis(sidx[k][:, c:c + 1], 0)
                                                    ).then_inc(eo_in[k], 16)
                    if on(3):
                        t3, k3 = t - 3, (k - 3) % R
                        await_count(pool, summed, SUM * t3 + SUM)
                        pool.tensor_tensor(rstd[:, k3, :], ve[:, k3, :], mhalf[:, :], ALU.pow).then_inc(rooted, 1)
                walk(pool, NT, 3, R, body, head=2)
                for k in range(R):
                    pool.wait_ge(eo_in[k], 32 * ((NT + R - 1 - k) // R))

            @block.vector
            def _(dve):
                dve.wait_ge(w_in, 32)

                def body(t, k, on):
                    t2, k2 = t - 2, (k - 2) % R
                    wt = lambda c: wtop[:, bass.ds(t, 1), c:c + 1].rearrange("p a n -> p (a n)")
                    if on(0):
                        await_count(dve, eo_in[k], 8 * (t - k) + 32, dve_tick)
                        dve.scalar_tensor_tensor(y1[:, k, :], eo[k][:, 0, :], wt(0),
                                                 acc[:, bass.ds(t, 1), 0:D].rearrange("p a n -> p (a n)"),
                                                 ALU.mult, ALU.add).then_inc(summed, 1)
                    if on(2):
                        await_count(dve, rooted, t2 + 1)
                        dve.scalar_tensor_tensor(z1[:, k2, :], y2[:, k2, :], mv[:, k2, 0:1], gb[:, :], ALU.subtract,
                                                 ALU.mult).then_inc(done, 1)
                    if on(0):
                        await_count(dve, summed, SUM * t + 1, dve_tick)
                        dve.scalar_tensor_tensor(y2[:, k, :], eo[k][:, 1, :], wt(1), y1[:, k, :], ALU.mult,
                                                 ALU.add).then_inc(summed, 1)
                    if on(2):
                        await_count(dve, done, FIN * t2 + 1)
                        dve.scalar_tensor_tensor(z2[:, k2, :], z1[:, k2, :], rstd[:, k2, :], bb[:, :], ALU.mult,
                                                 ALU.add).then_inc(done, 1)
                    if on(0):
                        await_count(dve, summed, SUM * t + 2, dve_tick)
                        dve.bn_stats(st[:, k, :], y2[:, k, :]).then_inc(summed, 1)
                    if on(2):
                        await_count(dve, done, FIN * t2 + 2)
                        await_count(dve, x2_in[k2], 4 * (t2 - k2) + 16)
                        await_count(dve, out_[k2], 4 * (t2 - k2))
                        dve.tensor_tensor(o[:, k2, :], z2[:, k2, :], x2[:, k2, :], ALU.add).then_inc(done, 1)
                    if on(0):
                        await_count(dve, summed, SUM * t + 3, dve_tick)
                        dve.bn_aggr(mv[:, k, :], st[:, k, :]).then_inc(summed, 1)
                        await_count(dve, summed, SUM * t + 4)
                        dve.tensor_scalar(ve[:, k, :], mv[:, k, 1:2], LN_EPS, None, ALU.add).then_inc(summed, 1)
                walk(dve, NT, 2, R, body, head=2)


_OUTS = [((NPAD, D), 'float32')]


def kernel(**inputs):
    import numpy as _np
    import concourse.bacc as _bacc
    from concourse import mybir as _mybir
    from concourse.bass_utils import run_bass_kernel_spmd as _run

    g = {k: _np.asarray(v) for k, v in inputs.items()}
    c = _np.ascontiguousarray
    edges = _np.full((2, EPAD), 0, _np.int32)
    edges[1, E:] = PAD_DST
    edges[0, :E] = g['src']
    edges[1, :E] = g['dst']
    xp = _np.zeros((NPAD, D), _np.float32)
    xp[:N] = g['x']
    ins = {
        'x': xp, 'edges': edges, 'gW': g['L0_gnn_W'], 'att_src': g['L0_gnn_att_src'],
        'att_dst': g['L0_gnn_att_dst'], 'gbias': g['L0_gnn_bias'], 'wqkvT': c(g['L0_mix_Wqkv'].T),
        'ln1g': g['L0_mix_ln1_g'], 'ln1b': g['L0_mix_ln1_b'], 'w1T': c(g['L0_mix_W1'].T), 'b1': g['L0_mix_b1'],
        'w2T': c(g['L0_mix_W2'].T), 'b2': g['L0_mix_b2'], 'ln2g': g['L0_mix_ln2_g'], 'ln2b': g['L0_mix_ln2_b'],
        'gate_w': g['L0_ffn_gate_w'], 'gate_b': g['L0_ffn_gate_b'], 'ew1': g['L0_ffn_w1'],
        'eb1': c(g['L0_ffn_b1'].reshape(X, 4, P).transpose(2, 0, 1).reshape(P, X * 4)), 'ew2': g['L0_ffn_w2'],
        'eb2': g['L0_ffn_b2'], 'gamma': g['L0_ffn_gamma'], 'beta': g['L0_ffn_beta'],
    }
    nc = _bacc.Bacc("TRN2", target_bir_lowering=False, num_devices=1)
    arrays, args = {}, []
    for name, a in ins.items():
        a = c(a)
        arrays[f"in_{name}_dram"] = a
        args.append(nc.dram_tensor(f"in_{name}_dram", a.shape, _mybir.dt.from_np(a.dtype), kind="ExternalInput").ap())
    for i, (shape, dtype) in enumerate(_OUTS):
        dt = _mybir.dt.from_np(_np.dtype(dtype))
        args.append(nc.dram_tensor(f"out_{i}_dram", shape, dt, kind="ExternalOutput").ap())
    gps_kernel(nc, *args)
    r = _run(nc, [arrays], core_ids=[0])
    return r.results[0]["out_0_dram"][:N]
```
